# Optimizing a Trainium2 kernel written in Bass

```python
import numpy as np
import jax
import jax.numpy as jnp

def _softmax(x, axis=-1):
    return jax.nn.softmax(x, axis=axis)

def _gelu(x):
    return jax.nn.gelu(x, approximate=True)

def _silu(x):
    return jax.nn.silu(x)

def _sigmoid(x):
    return jax.nn.sigmoid(x)

def _layernorm(x, axis=-1, eps=1e-05):
    m = jnp.mean(x, axis=axis, keepdims=True)
    v = jnp.var(x, axis=axis, keepdims=True)
    return (x - m) / jnp.sqrt(v + eps)

def _scatter_add(tgt, idx, src, axis=0):
    return tgt.at[idx].add(src)

def _segment_sum(src, seg, n):
    return jax.ops.segment_sum(src, seg, n)
kernel_name = 'mk_vit_tower_d2_tok_img1024_r4_bfb637'

def setup_inputs(seed: int=0):
    np.random.seed(seed)
    _w = jnp.asarray

    def _rec_inputs():
        import jax
        import jax.numpy as jnp
        _rk = jax.random.key(seed)
        x = -0.00016672 + 0.999947 * jax.random.normal(jax.random.fold_in(_rk, 1), (16, 96, 96, 3), jnp.float32)
        return x
    x = _rec_inputs()

    def _L0_tok_setup():
        import jax, jax.numpy as jnp
        import numpy as np
        P = 16
        E = 256

        def patchify(images, patch_size):
            B, H, W, C = images.shape
            hp, wp = (H // patch_size, W // patch_size)
            x = images.reshape(B, hp, patch_size, wp, patch_size, C)
            x = x.transpose(0, 1, 3, 2, 4, 5)
            return x.reshape(B, hp * wp, patch_size * patch_size * C)
        key = jax.random.key(seed)
        k_img, k_w, k_b, k_pos = jax.random.split(key, 4)
        B, H, W, C = (64, 96, 96, 3)
        patch_dim = P * P * C
        patch_count = H // P * (W // P)
        images = jax.random.normal(k_img, (B, H, W, C), dtype=jnp.float32)
        W_proj = jax.random.normal(k_w, (E, patch_dim), dtype=jnp.float32) * patch_dim ** (-0.5)
        b_proj = jax.random.normal(k_b, (E,), dtype=jnp.float32) * 0.02
        pos_emb = jax.random.normal(k_pos, (patch_count, E), dtype=jnp.float32) * 0.02
        return {'images': images, 'W_proj': W_proj, 'b_proj': b_proj, 'pos_emb': pos_emb}
    _L0_tok_all = _L0_tok_setup()
    _L0_tok_in = {k: v for k, v in _L0_tok_all.items() if k in ('W_proj', 'b_proj', 'pos_emb')}
    del _L0_tok_all

    def _L0_attn_setup():
        import jax, jax.numpy as jnp
        import numpy as np
        import math
        N_EMBD = 256
        NUM_HEADS = 16
        HEAD_DIM = N_EMBD // NUM_HEADS

        def alibi_slopes(num_heads):
            x = (2 ** 8) ** (1.0 / num_heads)
            return jnp.array([1.0 / x ** (i + 1) for i in range(num_heads)], dtype=jnp.float32)
        key = jax.random.key(seed)
        k1, k2 = jax.random.split(key)
        x = jax.random.normal(k1, (2, 512, N_EMBD), dtype=jnp.float32)
        W_kqv = jax.random.normal(k2, (3 * N_EMBD, N_EMBD), dtype=jnp.float32) * (1.0 / math.sqrt(N_EMBD))
        return {'x': x, 'W_kqv': W_kqv}
    _L0_attn_all = _L0_attn_setup()
    _L0_attn_in = {k: v for k, v in _L0_attn_all.items() if k in ('W_kqv',)}
    del _L0_attn_all

    def _L0_ffn_setup():
        import jax, jax.numpy as jnp
        import numpy as np
        B, S, H = (8, 1024, 256)
        NAV = 128
        E = 8
        F = 2 * H
        key = jax.random.key(seed)
        ks = jax.random.split(key, 12)

        def w(k, shape, fan_in):
            return jax.random.normal(k, shape, dtype=jnp.float32) / np.sqrt(fan_in)
        return {'hidden_states': jax.random.normal(ks[0], (B, S, H), dtype=jnp.float32), 'Wp1': w(ks[1], (H, NAV), H), 'bp1': jnp.zeros((NAV,), jnp.float32), 'Wp2': w(ks[2], (NAV, E), NAV), 'bp2': jnp.zeros((E,), jnp.float32), 'W1': w(ks[3], (E, H, F), H), 'b1': jnp.zeros((E, F), jnp.float32), 'W2': w(ks[4], (E, F, H), F), 'b2': jnp.zeros((E, H), jnp.float32), 'Wo': w(ks[5], (H, H), H), 'bo': jnp.zeros((H,), jnp.float32)}
    _L0_ffn_all = _L0_ffn_setup()
    _L0_ffn_in = {k: v for k, v in _L0_ffn_all.items() if k in ('Wp1', 'bp1', 'Wp2', 'bp2', 'W1', 'b1', 'W2', 'b2', 'Wo', 'bo')}
    del _L0_ffn_all

    def _L1_attn_setup():
        import jax, jax.numpy as jnp
        import numpy as np
        D_MODEL = 256
        N_HEAD = 16
        HEAD_D = D_MODEL // N_HEAD
        D_FF = 1024
        LN_EPS = 1e-05
        ATTN_EPS = 1e-06

        def _layer_norm(x, g, b, eps=LN_EPS):
            mu = jnp.mean(x, axis=-1, keepdims=True)
            var = jnp.var(x, axis=-1, keepdims=True)
            return (x - mu) * jax.lax.rsqrt(var + eps) * g + b

        def _linear_attention(x, qkv_w, qkv_b, out_w, out_b):
            B, N, C = x.shape
            qkv = (x @ qkv_w + qkv_b).reshape(B, N, 3, N_HEAD, HEAD_D)
            qkv = jnp.transpose(qkv, (2, 0, 3, 1, 4))
            q, k, v = (qkv[0], qkv[1], qkv[2])
            qf = jax.nn.elu(q) + 1.0
            kf = jax.nn.elu(k) + 1.0
            kv = jnp.einsum('bhnd,bhne->bhde', kf.astype(jnp.float32), v.astype(jnp.float32)).astype(v.dtype)
            y_num = jnp.einsum('bhnd,bhde->bhne', qf, kv)
            z = jnp.sum(kf.astype(jnp.float32), axis=2)
            y_den = jnp.einsum('bhnd,bhd->bhn', qf, z.astype(qf.dtype))
            y_den = jnp.maximum(y_den, ATTN_EPS)[..., None]
            y = (y_num / y_den).transpose(0, 2, 1, 3).reshape(B, N, C)
            return y @ out_w + out_b
        key = jax.random.key(seed)
        ks = jax.random.split(key, 16)
        s = 0.02
        return {'src': jax.random.normal(ks[0], (4, 1024, D_MODEL), dtype=jnp.float32), 'qkv_w': jax.random.normal(ks[1], (D_MODEL, 3 * D_MODEL), dtype=jnp.float32) * s, 'qkv_b': jax.random.normal(ks[2], (3 * D_MODEL,), dtype=jnp.float32) * s, 'out_w': jax.random.normal(ks[3], (D_MODEL, D_MODEL), dtype=jnp.float32) * s, 'out_b': jax.random.normal(ks[4], (D_MODEL,), dtype=jnp.float32) * s, 'w1': jax.random.normal(ks[5], (D_MODEL, D_FF), dtype=jnp.float32) * s, 'b1': jax.random.normal(ks[6], (D_FF,), dtype=jnp.float32) * s, 'w2': jax.random.normal(ks[7], (D_FF, D_MODEL), dtype=jnp.float32) * s, 'b2': jax.random.normal(ks[8], (D_MODEL,), dtype=jnp.float32) * s, 'g1': jnp.ones((D_MODEL,), dtype=jnp.float32), 'be1': jnp.zeros((D_MODEL,), dtype=jnp.float32), 'g2': jnp.ones((D_MODEL,), dtype=jnp.float32), 'be2': jnp.zeros((D_MODEL,), dtype=jnp.float32)}
    _L1_attn_all = _L1_attn_setup()
    _L1_attn_in = {k: v for k, v in _L1_attn_all.items() if k in ('qkv_w', 'qkv_b', 'out_w', 'out_b', 'w1', 'b1', 'w2', 'b2', 'g1', 'be1', 'g2', 'be2')}
    del _L1_attn_all

    def _L1_ffn_setup():
        import jax, jax.numpy as jnp
        import numpy as np
        HIDDEN_SIZE = 256
        NUM_EXPERTS = 8
        MOE_INTERMEDIATE_SIZE = 352
        NUM_EXPERTS_PER_TOK = 2
        SHARED_EXPERT_INTERMEDIATE_SIZE = 704
        B, T = (2, 256)
        W_SCALE = 0.02
        key = jax.random.key(seed)
        ks = jax.random.split(key, 8)
        H, E, I, SI = (HIDDEN_SIZE, NUM_EXPERTS, MOE_INTERMEDIATE_SIZE, SHARED_EXPERT_INTERMEDIATE_SIZE)
        return {'x': jax.random.normal(ks[0], (B, T, H), jnp.float32), 'gate_w': jax.random.normal(ks[1], (E, H), jnp.float32) * W_SCALE, 'experts_gate_up': jax.random.normal(ks[2], (E, 2 * I, H), jnp.float32) * W_SCALE, 'experts_down': jax.random.normal(ks[3], (E, H, I), jnp.float32) * W_SCALE, 'shared_gate_w': jax.random.normal(ks[4], (SI, H), jnp.float32) * W_SCALE, 'shared_up_w': jax.random.normal(ks[5], (SI, H), jnp.float32) * W_SCALE, 'shared_down_w': jax.random.normal(ks[6], (H, SI), jnp.float32) * W_SCALE, 'shared_expert_gate_w': jax.random.normal(ks[7], (1, H), jnp.float32) * W_SCALE}
    _L1_ffn_all = _L1_ffn_setup()
    _L1_ffn_in = {k: v for k, v in _L1_ffn_all.items() if k in ('gate_w', 'experts_gate_up', 'experts_down', 'shared_gate_w', 'shared_up_w', 'shared_down_w', 'shared_expert_gate_w')}
    del _L1_ffn_all
    return {'x': x, 'L0_tok_W_proj': _L0_tok_in['W_proj'], 'L0_tok_b_proj': _L0_tok_in['b_proj'], 'L0_tok_pos_emb': _L0_tok_in['pos_emb'], 'L0_attn_W_kqv': _L0_attn_in['W_kqv'], 'L0_ffn_Wp1': _L0_ffn_in['Wp1'], 'L0_ffn_bp1': _L0_ffn_in['bp1'], 'L0_ffn_Wp2': _L0_ffn_in['Wp2'], 'L0_ffn_bp2': _L0_ffn_in['bp2'], 'L0_ffn_W1': _L0_ffn_in['W1'], 'L0_ffn_b1': _L0_ffn_in['b1'], 'L0_ffn_W2': _L0_ffn_in['W2'], 'L0_ffn_b2': _L0_ffn_in['b2'], 'L0_ffn_Wo': _L0_ffn_in['Wo'], 'L0_ffn_bo': _L0_ffn_in['bo'], 'L1_attn_qkv_w': _L1_attn_in['qkv_w'], 'L1_attn_qkv_b': _L1_attn_in['qkv_b'], 'L1_attn_out_w': _L1_attn_in['out_w'], 'L1_attn_out_b': _L1_attn_in['out_b'], 'L1_attn_w1': _L1_attn_in['w1'], 'L1_attn_b1': _L1_attn_in['b1'], 'L1_attn_w2': _L1_attn_in['w2'], 'L1_attn_b2': _L1_attn_in['b2'], 'L1_attn_g1': _L1_attn_in['g1'], 'L1_attn_be1': _L1_attn_in['be1'], 'L1_attn_g2': _L1_attn_in['g2'], 'L1_attn_be2': _L1_attn_in['be2'], 'L1_ffn_gate_w': _L1_ffn_in['gate_w'], 'L1_ffn_experts_gate_up': _L1_ffn_in['experts_gate_up'], 'L1_ffn_experts_down': _L1_ffn_in['experts_down'], 'L1_ffn_shared_gate_w': _L1_ffn_in['shared_gate_w'], 'L1_ffn_shared_up_w': _L1_ffn_in['shared_up_w'], 'L1_ffn_shared_down_w': _L1_ffn_in['shared_down_w'], 'L1_ffn_shared_expert_gate_w': _L1_ffn_in['shared_expert_gate_w']}

def reference(x, L0_tok_W_proj, L0_tok_b_proj, L0_tok_pos_emb, L0_attn_W_kqv, L0_ffn_Wp1, L0_ffn_bp1, L0_ffn_Wp2, L0_ffn_bp2, L0_ffn_W1, L0_ffn_b1, L0_ffn_W2, L0_ffn_b2, L0_ffn_Wo, L0_ffn_bo, L1_attn_qkv_w, L1_attn_qkv_b, L1_attn_out_w, L1_attn_out_b, L1_attn_w1, L1_attn_b1, L1_attn_w2, L1_attn_b2, L1_attn_g1, L1_attn_be1, L1_attn_g2, L1_attn_be2, L1_ffn_gate_w, L1_ffn_experts_gate_up, L1_ffn_experts_down, L1_ffn_shared_gate_w, L1_ffn_shared_up_w, L1_ffn_shared_down_w, L1_ffn_shared_expert_gate_w):
    import jax
    import jax.numpy as jnp

    def _L0_tok_ref(images, W_proj, b_proj, pos_emb):
        import jax, jax.numpy as jnp
        import numpy as np
        P = 16
        E = 256

        def patchify(images, patch_size):
            B, H, W, C = images.shape
            hp, wp = (H // patch_size, W // patch_size)
            x = images.reshape(B, hp, patch_size, wp, patch_size, C)
            x = x.transpose(0, 1, 3, 2, 4, 5)
            return x.reshape(B, hp * wp, patch_size * patch_size * C)
        patches = patchify(images, P)
        out = jnp.einsum('bnd,ed->bne', patches, W_proj) + b_proj + pos_emb[None, :, :]
        return out

    def _L0_attn_ref(x, W_kqv):
        import jax, jax.numpy as jnp
        import numpy as np
        import math
        N_EMBD = 256
        NUM_HEADS = 16
        HEAD_DIM = N_EMBD // NUM_HEADS

        def alibi_slopes(num_heads):
            x = (2 ** 8) ** (1.0 / num_heads)
            return jnp.array([1.0 / x ** (i + 1) for i in range(num_heads)], dtype=jnp.float32)
        B, S, E = x.shape
        H, D = (NUM_HEADS, HEAD_DIM)
        kqv = jnp.einsum('bse,fe->bsf', x, W_kqv)
        k, q, v = jnp.split(kqv, 3, axis=-1)
        q = q.reshape(B, S, H, D).transpose(0, 2, 1, 3)
        k = k.reshape(B, S, H, D).transpose(0, 2, 1, 3)
        v = v.reshape(B, S, H, D).transpose(0, 2, 1, 3)
        rel = jnp.arange(S)[None, :] - jnp.arange(S)[:, None]
        bias = alibi_slopes(H)[:, None, None] * rel.astype(jnp.float32)
        scale = math.sqrt(E)
        score = jnp.einsum('bhqd,bhkd->bhqk', q, k) / scale + bias[None]
        causal = jnp.tril(jnp.ones((S, S), dtype=bool))
        score = jnp.where(causal[None, None], score, -jnp.inf)
        attn = jax.nn.softmax(score, axis=-1)
        out = jnp.einsum('bhqk,bhkd->bhqd', attn, v)
        return out.transpose(0, 2, 1, 3).reshape(B, S, E)

    def _L0_ffn_ref(hidden_states, Wp1, bp1, Wp2, bp2, W1, b1, W2, b2, Wo, bo):
        import jax, jax.numpy as jnp
        import numpy as np
        B, S, H = (8, 1024, 256)
        NAV = 128
        E = 8
        F = 2 * H
        last = hidden_states[:, -1, :]
        logits = jax.nn.gelu(last @ Wp1 + bp1, approximate=False) @ Wp2 + bp2
        action_probs = jax.nn.softmax(logits, axis=-1)
        sel = jnp.argmax(action_probs, axis=-1)
        w1 = W1[sel]
        w2 = W2[sel]
        h = jax.nn.gelu(jnp.einsum('bsh,bhf->bsf', hidden_states, w1) + b1[sel][:, None, :], approximate=False)
        reasoned = jnp.einsum('bsf,bfh->bsh', h, w2) + b2[sel][:, None, :]
        out = reasoned @ Wo + bo
        return hidden_states + 0.3 * out

    def _L1_attn_ref(src, qkv_w, qkv_b, out_w, out_b, w1, b1, w2, b2, g1, be1, g2, be2):
        import jax, jax.numpy as jnp
        import numpy as np
        D_MODEL = 256
        N_HEAD = 16
        HEAD_D = D_MODEL // N_HEAD
        D_FF = 1024
        LN_EPS = 1e-05
        ATTN_EPS = 1e-06

        def _layer_norm(x, g, b, eps=LN_EPS):
            mu = jnp.mean(x, axis=-1, keepdims=True)
            var = jnp.var(x, axis=-1, keepdims=True)
            return (x - mu) * jax.lax.rsqrt(var + eps) * g + b

        def _linear_attention(x, qkv_w, qkv_b, out_w, out_b):
            B, N, C = x.shape
            qkv = (x @ qkv_w + qkv_b).reshape(B, N, 3, N_HEAD, HEAD_D)
            qkv = jnp.transpose(qkv, (2, 0, 3, 1, 4))
            q, k, v = (qkv[0], qkv[1], qkv[2])
            qf = jax.nn.elu(q) + 1.0
            kf = jax.nn.elu(k) + 1.0
            kv = jnp.einsum('bhnd,bhne->bhde', kf.astype(jnp.float32), v.astype(jnp.float32)).astype(v.dtype)
            y_num = jnp.einsum('bhnd,bhde->bhne', qf, kv)
            z = jnp.sum(kf.astype(jnp.float32), axis=2)
            y_den = jnp.einsum('bhnd,bhd->bhn', qf, z.astype(qf.dtype))
            y_den = jnp.maximum(y_den, ATTN_EPS)[..., None]
            y = (y_num / y_den).transpose(0, 2, 1, 3).reshape(B, N, C)
            return y @ out_w + out_b
        attn_out = _linear_attention(_layer_norm(src, g1, be1), qkv_w, qkv_b, out_w, out_b)
        x = src + attn_out
        h = jax.nn.gelu(_layer_norm(x, g2, be2) @ w1 + b1, approximate=False)
        return x + h @ w2 + b2

    def _L1_ffn_ref(x, gate_w, experts_gate_up, experts_down, shared_gate_w, shared_up_w, shared_down_w, shared_expert_gate_w):
        import jax, jax.numpy as jnp
        import numpy as np
        HIDDEN_SIZE = 256
        NUM_EXPERTS = 8
        MOE_INTERMEDIATE_SIZE = 352
        NUM_EXPERTS_PER_TOK = 2
        SHARED_EXPERT_INTERMEDIATE_SIZE = 704
        B, T = (2, 256)
        W_SCALE = 0.02
        Bx, Tx, H = x.shape
        E = gate_w.shape[0]
        I = experts_down.shape[2]
        x_flat = x.reshape(Bx * Tx, H)
        logits = x_flat @ gate_w.T
        scores = jax.nn.softmax(logits, axis=-1)
        _, topk_ids = jax.lax.top_k(scores, NUM_EXPERTS_PER_TOK)
        in_topk = jax.nn.one_hot(topk_ids, E, dtype=x.dtype).sum(axis=1)
        w = scores * in_topk
        gu = jnp.einsum('nh,eih->nei', x_flat, experts_gate_up)
        g, u = (gu[..., :I], gu[..., I:])
        h = jax.nn.silu(g) * u
        expert_out = jnp.einsum('nei,ehi->neh', h, experts_down)
        out = jnp.einsum('neh,ne->nh', expert_out, w)
        shared = jax.nn.silu(x_flat @ shared_gate_w.T) * (x_flat @ shared_up_w.T) @ shared_down_w.T
        shared_weight = jax.nn.sigmoid(x_flat @ shared_expert_gate_w.T)
        out = out + shared_weight * shared
        return out.reshape(Bx, Tx, H)
    h = _L0_tok_ref(x, L0_tok_W_proj, L0_tok_b_proj, L0_tok_pos_emb)
    h = h + _L0_attn_ref(_layernorm(h, axis=-1), L0_attn_W_kqv)
    h = h + _L0_ffn_ref(_layernorm(h, axis=-1), L0_ffn_Wp1, L0_ffn_bp1, L0_ffn_Wp2, L0_ffn_bp2, L0_ffn_W1, L0_ffn_b1, L0_ffn_W2, L0_ffn_b2, L0_ffn_Wo, L0_ffn_bo)
    h = h + _L1_attn_ref(_layernorm(h, axis=-1), L1_attn_qkv_w, L1_attn_qkv_b, L1_attn_out_w, L1_attn_out_b, L1_attn_w1, L1_attn_b1, L1_attn_w2, L1_attn_b2, L1_attn_g1, L1_attn_be1, L1_attn_g2, L1_attn_be2)
    h = h + _L1_ffn_ref(_layernorm(h, axis=-1), L1_ffn_gate_w, L1_ffn_experts_gate_up, L1_ffn_experts_down, L1_ffn_shared_gate_w, L1_ffn_shared_up_w, L1_ffn_shared_down_w, L1_ffn_shared_expert_gate_w)
    return h

_drawn_inputs = setup_inputs


def setup_inputs(seed=0):
    import zlib

    import numpy as np

    out = dict(_drawn_inputs(seed))
    spreads = {'L0_ffn_bp1': (0.0, 0.1),
     'L0_ffn_bp2': (0.0, 0.1),
     'L0_ffn_b1': (0.0, 0.8),
     'L0_ffn_b2': (0.0, 0.542),
     'L0_ffn_bo': (0.0, 0.538),
     'L1_attn_g1': (1.0, 0.6),
     'L1_attn_be1': (0.0, 0.8),
     'L1_attn_g2': (1.0, 0.6),
     'L1_attn_be2': (0.0, 0.8)}
    factors = {'L1_attn_qkv_w': 5.64,
     'L1_attn_qkv_b': 8.0,
     'L1_attn_out_w': 5.612,
     'L1_attn_out_b': 8.0,
     'L1_attn_b1': 8.0,
     'L1_attn_b2': 8.0,
     'L1_ffn_gate_w': 8.0,
     'L1_ffn_experts_gate_up': 8.0,
     'L1_ffn_experts_down': 8.0,
     'L1_ffn_shared_gate_w': 8.0,
     'L1_ffn_shared_up_w': 8.0,
     'L1_ffn_shared_down_w': 8.0,
     'L1_ffn_shared_expert_gate_w': 8.0}
    for name, (base, spread) in spreads.items():
        noise = np.random.default_rng([zlib.crc32(name.encode()), seed]).standard_normal(out[name].shape)
        drawn = base * np.exp(spread * noise) if base else spread * noise
        out[name] = jnp.asarray(drawn.astype(out[name].dtype))
    for name, factor in factors.items():
        out[name] = (out[name] * factor).astype(out[name].dtype)
    return out
```

```python
from contextlib import ExitStack

import numpy as np

import concourse.bass as bass
from concourse import mybir

F32 = mybir.dt.float32
F32R = mybir.dt.float32r
U32 = mybir.dt.uint32
ALU = mybir.AluOpType
ACT = mybir.ActivationFunctionType
AX = mybir.AxisListType

IMGS, SEQ, EMB, PATCH = 16, 36, 256, 768
TOK = IMGS * SEQ
CH = EMB // 128
HALVES = 2
HT = TOK // HALVES
PAIRS = IMGS // 2
HPAIRS = PAIRS // HALVES
HEADS, HD = 16, 16
CHH = 128 // HD
SLOT = 64
PAD = SLOT - SEQ
KP = PATCH // 128
EXP, FFN = 8, 512
FC = FFN // 128
NAV = 128
DFF = 1024
DC = DFF // 128
MOE_I = 352
MCH = [(0, 128), (128, 128), (256, 96)]
MC = len(MCH)
BLOCKS = EXP + 2
GU = CH * 2 * MOE_I
DOWN = MC * EMB
RT = 96
RC = HT // RT
ROUTE = EXP + 1
EPS = 1e-5
DEN_EPS = 1e-6
NEG = -1e30

COLS = {}
_at = 0
for _name, _n in (("b_proj", CH), ("pos", CH * SEQ), ("bp1", 1), ("bp2", EXP), ("bo", CH), ("bq", CH),
                  ("out_b", CH), ("b1", DC), ("b2", CH), ("g1", CH), ("be1", CH), ("g2", CH), ("be2", CH)):
    COLS[_name] = (_at, _at + _n)
    _at += _n
NCOLS = _at
CONST = {}
_at = 0
for _name, _n in (("ident", 128), ("mean", 128), ("alibi", HEADS * SEQ), ("head", CHH), ("block", 128 + CHH),
                  ("iota", EXP)):
    CONST[_name] = (_at, _at + _n)
    _at += _n
NCONST = _at


def tower(nc, patches, w_proj, w_kqv, cols, consts, wp1, wp2, w1x, b1x, w2x, b2x, wo,
          qkv_w, kv_b, out_w, ffn_w1, ffn_w2, route_w, moe_gu, moe_down, out):
    with ExitStack() as ctx:
        def sb(name, shape, dt=F32, where=ctx):
            return where.enter_context(nc.sbuf_tensor(name, shape, dt))

        def sem(name):
            return ctx.enter_context(nc.semaphore(name))

        gate_dram = nc.dram_tensor("gate_dram", (ROUTE, TOK), F32, kind="Internal").ap()
        ps = ctx.enter_context(nc.psum_tensor("ps", [128, 8, 512], F32))

        h = sb("h", [128, CH, TOK])
        xc = sb("xc", [128, CH, TOK])
        sq = sb("sq", [128, CH, TOK])
        rstd = sb("rstd", [128, TOK])
        xn = sb("xn", [128, CH, TOK + PAD])
        xs = sb("xs", [128, CH, TOK])
        q = sb("q", [128, CH, TOK + PAD])
        vec = sb("vec", [128, NCOLS])
        cst = sb("cst", [128, NCONST])
        eps = sb("eps", [128, 1])
        bo3 = sb("bo3", [128, CH])
        kqv = sb("kqv", [128, CH, 3 * EMB])
        wo_sb = sb("wo_sb", [128, CH, EMB])
        wp1_sb = sb("wp1_sb", [128, CH, NAV])
        wp2_sb = sb("wp2_sb", [128, EXP])
        b1_sb = sb("b1_sb", [EXP, FFN])
        b2_sb = sb("b2_sb", [EXP, EMB])
        route_sb = sb("route_sb", [128, CH, ROUTE])
        sc = sb("sc", [128, 2, HEADS * SEQ])
        top = sb("top", [128, 2, HEADS])
        total = sb("total", [128, 2, HEADS])
        act8 = sb("act8", [128, HALVES, 8])
        lg = sb("lg", [8, HALVES, EXP])
        mx8 = sb("mx8", [8, HALVES, 8])
        nmx = sb("nmx", [8, HALVES])
        ex8 = sb("ex8", [8, HALVES, EXP])
        sm8 = sb("sm8", [8, HALVES])
        rs8 = sb("rs8", [8, HALVES])
        pr8 = sb("pr8", [8, HALVES, EXP])
        pick = sb("pick", [8, HALVES, 8], U32)
        pickf = sb("pickf", [8, HALVES])
        hot = sb("hot", [8, HALVES, EXP])
        hotT = sb("hotT", [EXP, IMGS, SLOT])

        def col(name, a=0, n=1):
            return vec[:, COLS[name][0] + a:COLS[name][0] + a + n]

        def const(name):
            return cst[:, CONST[name][0]:CONST[name][1]]

        ident = const("ident")
        ones_mean = const("mean")

        with ExitStack() as reg:
            kx = sb("kx", [128, HALVES, CH, CHH, HT], where=reg)
        with ExitStack() as reg:
            fw1 = sb("fw1", [128, CH, DFF], where=reg)
            fw2 = sb("fw2", [128, DC, EMB], where=reg)
            hid = sb("hid", [128, DC, HT], where=reg)
            qkv = sb("qkv", [128, CH, 3 * EMB], where=reg)
            wout = sb("wout", [128, CH, EMB], where=reg)
            kvb = sb("kvb", [128, 2 * EMB], where=reg)
        with ExitStack() as reg:
            hhi = sb("hhi", [128, 2, MC, TOK], F32R, where=reg)
            hlo = sb("hlo", [128, 2, MC, TOK], F32R, where=reg)
        holdC = sb("holdC", [128, 9216])
        with ExitStack() as reg:
            X = sb("X", [128, KP, TOK], where=reg)
            wp = sb("wp", [128, KP, EMB], where=reg)
        with ExitStack() as reg:
            vbd = sb("vbd", [128, IMGS, HEADS // 2, 2 * HD], where=reg)
            prob = sb("prob", [128, 2, HEADS, SLOT], where=reg)
            pT = sb("pT", [128, 2, HEADS // 2, 2, SEQ], where=reg)
        with ExitStack() as reg:
            w1s = sb("w1s", [128, 2, 2, CH, FFN], where=reg)
            w2s = sb("w2s", [128, 2, 2, FC, EMB], where=reg)
        with ExitStack() as reg:
            vx = sb("vx", [128, 2, CH, 128 + CHH], where=reg)
            kvm = sb("kvm", [128, 2, 2, CH, 128 + CHH], where=reg)
            xp = sb("xp", [128, CH, IMGS * SLOT], where=reg)
        with ExitStack() as reg:
            gate = sb("gate", [128, ROUTE, TOK], where=reg)
            xhi = sb("xhi", [128, CH, TOK], F32R, where=reg)
            xlo = sb("xlo", [128, CH, TOK], F32R, where=reg)
        holdB = sb("holdB", [128, 8192])
        with ExitStack() as reg:
            w1a = sb("w1a", [128, EXP, CH, FFN], where=reg)
            w2a = sb("w2a", [128, EXP, FC, EMB], where=reg)
        with ExitStack() as reg:
            guhi = sb("guhi", [128, 2, GU], F32R, where=reg)
            gulo = sb("gulo", [128, 2, GU], F32R, where=reg)
            dnhi = sb("dnhi", [128, 2, DOWN], F32R, where=reg)
            dnlo = sb("dnlo", [128, 2, DOWN], F32R, where=reg)
            guraw = sb("guraw", [128, 2, GU], where=reg)
            dnraw = sb("dnraw", [128, 2, DOWN], where=reg)
            sil = sb("sil", [128, 2, 2, HT], where=reg)
            prod = sb("prod", [128, 2, HT], where=reg)
            wrows = sb("wrows", [ROUTE, TOK], where=reg)
            rlog = sb("rlog", [ROUTE, TOK], where=reg)
        holdA = sb("holdA", [128, 16384])
        hg = sb("hg", [128, 2, FFN])
        hgT = sb("hgT", [128, 2, FC, 128])
        rr = sb("rr", [128, 2, EMB])
        rT = sb("rT", [128, CH, TOK])
        kf = hg
        ke = sc
        yt = rr
        dinv = sb("dinv", [128, 2, CH, CHH])
        yT = rT

        S = {}
        for name in (
            "patch_in", "cols_in", "const_in", "kqv_in", "wp_in", "qkv_in", "wout_in", "wo_in", "kvb_in",
            "wp1_in", "wp2_in", "b1_in", "b2_in", "route_in", "w1a_in", "w2a_in", "fw_in",
            "setup", "act_setup", "pool_setup", "dve_step", "act_step", "pool_step",
            "tok_mm", "h_ready", "mean_mm", "centred", "squared", "var_mm", "rstd_ready", "normed",
            "qk_mm", "q_ready", "kx_dve", "kx_act", "v_mm", "v_ready",
            "score_mm", "biased", "row_max", "shifted", "exped", "prob_ready", "prob_mm", "pT_ready", "pv_mm", "attn_added",
            "p1_mm", "p1_act", "p2_mm", "p2_logit", "p2_exp", "pick_ready", "hot_mm", "hot_ready",
            "w1_copied", "w2_copied", "f1_mm", "f1_gelu", "f1_t", "f1_T_ready", "f2_mm", "f2_ready", "f2_t", "r_ready",
            "wo_mm", "ffn_added",
            "lq_mm", "slotted", "lq_min", "lq_relu", "lq_exp", "lq_ready", "kv_mm", "k_ready", "k_min", "k_exp", "kf_ready", "v2_ready", "state_mm", "state_ready",
            "y_mm", "y_ready", "y_t", "yT_ready", "out_mm", "x_ready",
            "up_mm", "up_gelu", "ff_mm", "ff_added",
            "x_hi", "x_lo", "r_mm", "r_copied", "r_t", "r_max", "r_exp", "r_w", "r_back", "w_rows", "gate_in", "gate_out",
            "g_mm", "u_mm", "silu", "gated", "h_mul", "h_hi", "h_lo", "down_mm", "raw_used", "w_hi", "w_lo",
            "moe_added", "stored",
        ):
            S[name] = sem(name)
        raw_in = [sem(f"raw_in{i}") for i in range(2)]
        rtok = sb("rtok", [RT, HALVES, RC, ROUTE])
        rex = sb("rex", [RT, HALVES, RC, ROUTE])
        rw = sb("rw", [RT, HALVES, RC, ROUTE])
        rmx = sb("rmx", [RT, HALVES, RC, 8])
        rix = sb("rix", [RT, HALVES, RC, 8], U32)
        rixf = sb("rixf", [RT, HALVES, RC, 8])
        rsum = sb("rsum", [RT, HALVES, RC])
        rm2 = sb("rm2", [RT, HALVES, RC, EXP])

        def half(t):
            return slice(t * HT, (t + 1) * HT)

        def img(i):
            return slice(i * SEQ, (i + 1) * SEQ)

        def slot(i):
            return slice(i * SEQ, i * SEQ + SLOT)

        block = ctx.enter_context(nc.Block())

        @block.sync
        def _(sp):
            sp.dma_start(cst[:, :], consts).then_inc(S["const_in"], 16)
            sp.dma_start(vec[:, :], cols).then_inc(S["cols_in"], 16)
            sp.dma_start(wp[:, :, :], w_proj).then_inc(S["wp_in"], 16)
            sp.dma_start(X[:, :, :], patches).then_inc(S["patch_in"], 16)
            sp.dma_start(kqv[:, :, :], w_kqv).then_inc(S["kqv_in"], 16)
            sp.dma_start(w1a[:, :, :, :], w1x).then_inc(S["w1a_in"], 16)
            sp.dma_start(w2a[:, :, :, :], w2x).then_inc(S["w2a_in"], 16)
            sp.dma_start(wo_sb[:, :, :], wo).then_inc(S["wo_in"], 16)
            sp.wait_ge(S["score_mm"], PAIRS)
            sp.dma_start(qkv[:, :, :], qkv_w).then_inc(S["qkv_in"], 16)
            sp.dma_start(kvb[:, :], kv_b.partition_broadcast(128)).then_inc(S["kvb_in"], 16)
            sp.dma_start(wout[:, :, :], out_w).then_inc(S["wout_in"], 16)
            sp.dma_start(fw1[:, :, :], ffn_w1).then_inc(S["fw_in"], 16)
            sp.dma_start(fw2[:, :, :], ffn_w2).then_inc(S["fw_in"], 16)
            sp.wait_ge(S["w1_copied"], IMGS)
            sp.wait_ge(S["w2_copied"], IMGS)
            for e in range(BLOCKS):
                if e >= 2:
                    sp.wait_ge(S["w_hi"], 3 * (e - 1))
                    sp.wait_ge(S["w_lo"], 3 * (e - 1))
                sp.dma_start(guraw[:, e % 2, :], moe_gu[e]).then_inc(raw_in[e % 2], 16)
                sp.dma_start(dnraw[:, e % 2, 0:2 * EMB], moe_down[e, :, 0:2 * EMB]).then_inc(raw_in[e % 2], 16)
                sp.dma_start(dnraw[0:96, e % 2, 2 * EMB:], moe_down[e, 0:96, 2 * EMB:]).then_inc(raw_in[e % 2], 16)
            for c in range(CH):
                sp.wait_ge(S["moe_added"], HALVES * (c + 1))
                sp.dma_start(out[:, c, :], xs[:, c, :]).then_inc(S["stored"], 16)
            sp.wait_ge(S["stored"], 16 * CH)

        @block.gpsimd
        def _(pool):
            pool.dma_start(wp1_sb[:, :, :], wp1).then_inc(S["wp1_in"], 16)
            pool.dma_start(wp2_sb[:, :], wp2).then_inc(S["wp2_in"], 16)
            pool.dma_start(b1_sb[:, :], b1x).then_inc(S["b1_in"], 16)
            pool.dma_start(b2_sb[:, :], b2x).then_inc(S["b2_in"], 16)
            pool.dma_start(route_sb[:, :, :], route_w).then_inc(S["route_in"], 16)
            pool.memset(eps[:, :], EPS).then_inc(S["pool_setup"], 1)
            pool.memset(xn[:, :, TOK:], 0.0).then_inc(S["pool_setup"], 1)
            pool.memset(q[:, :, TOK:], 0.0).then_inc(S["pool_setup"], 1)
            pool.wait_ge(S["tok_mm"], HALVES)
            pool.memset(vbd[:, :, :, :], 0.0).then_inc(S["pool_setup"], 1)
            pool.memset(prob[:, :, :, :], 0.0).then_inc(S["pool_setup"], 1)
            for p in range(PAIRS):
                pool.wait_ge(S["row_max"], p + 1)
                s = sc[:, p % 2, :].rearrange("p (h k) -> p h k", k=SEQ)
                pool.tensor_tensor(s, s, top[:, p % 2, :].unsqueeze(2).to_broadcast([128, HEADS, SEQ]),
                                   ALU.subtract).then_inc(S["shifted"], 1)
            pool.wait_ge(S["f1_mm"], PAIRS)
            pool.wait_ge(S["f2_mm"], PAIRS)
            pool.memset(vx[:, :, :, 128:], 1.0).then_inc(S["pool_setup"], 1)
            pool.memset(xp[:, :, :], 0.0).then_inc(S["pool_setup"], 1)
            pool.wait_ge(S["w_rows"], HALVES)
            pool.wait_ge(S["f2_mm"], PAIRS)
            pool.dma_start(gate_dram, wrows[:, :]).then_inc(S["gate_out"], 16)
            pool.wait_ge(S["gate_out"], 16)
            for e in range(ROUTE):
                pool.dma_start(gate[:, e, :], gate_dram[e, :].partition_broadcast(128)).then_inc(S["gate_in"], 16)
            pool.wait_ge(S["gate_in"], 16 * ROUTE)
            n = 0
            for e in range(BLOCKS):
                for m, (_, rows) in enumerate(MCH):
                    for t in range(HALVES):
                        pool.wait_ge(S["silu"], n + 1)
                        if n >= 2:
                            pool.wait_ge(S["h_mul"], n - 1)
                        pool.tensor_tensor(sil[0:rows, 1, n % 2, :], sil[0:rows, 0, n % 2, :],
                                           gate[0:rows, min(e, EXP), half(t)], ALU.mult).then_inc(S["gated"], 1)
                        n += 1

        @block.scalar
        def _(act):
            steps = [0]

            def link(ins):
                steps[0] += 1
                ins.then_inc(S["act_step"], 1)
                act.wait_ge(S["act_step"], steps[0])

            def norm(k, t):
                n = HALVES * k + t
                act.wait_ge(S["centred"], n + 1)
                act.activation(sq[:, :, half(t)], xc[:, :, half(t)], ACT.Square).then_inc(S["squared"], 1)
                act.wait_ge(S["var_mm"], n + 1)
                link(act.activation(rstd[:, half(t)], ps[:, 4 * t + 1, 0:HT], ACT.Ln, bias=eps[:, :]))
                act.activation(rstd[:, half(t)], rstd[:, half(t)], ACT.Exp, scale=-0.5).then_inc(S["rstd_ready"], 1)

            act.wait_ge(S["pool_setup"], 3)
            for t in range(HALVES):
                norm(0, t)
            act.wait_ge(S["const_in"], 16)
            for t in range(HALVES):
                act.wait_ge(S["qk_mm"], 2 * t + 1)
                act.activation(q[:, :, half(t)], ps[:, 4 * t + 2:4 * t + 4, 0:HT], ACT.Copy,
                               scale=float(EMB) ** -0.5).then_inc(S["q_ready"], 1)
                act.wait_ge(S["qk_mm"], 2 * t + 2)
                for g in range(CHH):
                    last = act.activation(kx[:, t, 1, g, :], ps[:, 4 * t + 1, 0:HT], ACT.Copy,
                                          scale=const("head")[:, g:g + 1])
                last.then_inc(S["kx_act"], 1)
            act.wait_ge(S["pool_setup"], 5)
            for t in range(HALVES):
                act.wait_ge(S["v_mm"], t + 1)
                for b in range(2):
                    for o in range(2):
                        i0 = 8 * t + 4 * b
                        src = ps[64 * o:64 * o + 64, 4 * t + 2 + b, :].rearrange("p (i d) -> p i d", d=HD)
                        dst = vbd[64 * o:64 * o + 64, i0:i0 + 4, :, HD * o:HD * o + HD].rearrange(
                            "p i j d -> p (i j) d")
                        last = act.activation(dst, src, ACT.Copy)
                last.then_inc(S["v_ready"], 1)
            for p in range(PAIRS + 1):
                if p < PAIRS:
                    act.wait_ge(S["shifted"], p + 1)
                    act.activation(sc[:, p % 2, :], sc[:, p % 2, :], ACT.Exp).then_inc(S["exped"], 1)
                if p >= 1:
                    act.wait_ge(S["prob_mm"], p)
                    if p >= 3:
                        act.wait_ge(S["pv_mm"], p - 2)
                    src = ps[:, 4:6, :].rearrange("p b (j i s) -> p (b j) i s", j=4, i=2)
                    for i in range(2):
                        last = act.activation(pT[:, (p - 1) % 2, :, i, :], src[:, :, i, 0:SEQ], ACT.Copy)
                    last.then_inc(S["pT_ready"], 1)
            for t in range(HALVES):
                norm(1, t)
            for t in range(HALVES):
                act.wait_ge(S["p1_mm"], t + 1)
                act.activation(act8[:, t, :], ps[:, 4 * t, 0:8], ACT.Gelu, bias=col("bp1")).then_inc(S["p1_act"], 1)
            for t in range(HALVES):
                act.wait_ge(S["p2_logit"], t + 1)
                act.activation(ex8[:, t, :], lg[:, t, :], ACT.Exp, bias=nmx[:, t:t + 1],
                               accum_out=sm8[:, t:t + 1]).then_inc(S["p2_exp"], 1)
            act.wait_ge(S["w2a_in"], 16)
            for p in range(PAIRS + 1):
                if p < PAIRS:
                    act.wait_ge(S["pick_ready"], p // HPAIRS + 1)
                    for i in range(2):
                        if i == 0 and p >= 2:
                            act.wait_ge(S["f2_mm"], p - 1)
                        r = (2 * p + i) % 8
                        e = act.value_load(pick[r:r + 1, p // HPAIRS, 0:1], min_val=0, max_val=EXP - 1)
                        act.activation(w2s[:, p % 2, i, :, :], w2a[:, bass.ds(e, 1), :, :], ACT.Copy)\
                           .then_inc(S["w2_copied"], 1)
                    act.wait_ge(S["f1_mm"], p + 1)
                    if p >= 2:
                        act.wait_ge(S["f1_t"], p - 1)
                    act.activation(hg[:, p % 2, :], ps[:, p % 2, :], ACT.Gelu).then_inc(S["f1_gelu"], 1)
                if p >= 1:
                    act.wait_ge(S["f2_mm"], p)
                    if p >= 3:
                        act.wait_ge(S["f2_t"], p - 2)
                    act.activation(rr[:, (p - 1) % 2, :], ps[:, 4 + (p - 1) % 2, 0:EMB], ACT.Copy)\
                       .then_inc(S["f2_ready"], 1)
            for k in (2, 3):
                for t in range(HALVES):
                    norm(k, t)
            for t in range(HALVES):
                act.wait_ge(S["lq_min"], t + 1)
                for c in range(CH):
                    last = act.activation(q[:, c, half(t)], ps[:, 4 * t + 2 + c, 0:HT], ACT.Relu, bias=col("bq", c))
                last.then_inc(S["lq_relu"], 1)
                act.activation(xs[:, :, half(t)], xs[:, :, half(t)], ACT.Exp).then_inc(S["lq_exp"], 1)
            for p in range(PAIRS + 3):
                if p < PAIRS:
                    act.wait_ge(S["k_min"], p + 1)
                    act.activation(ke[:, p % 2, 0:EMB], ke[:, p % 2, 0:EMB], ACT.Exp).then_inc(S["k_exp"], 1)
                if p >= 3:
                    act.wait_ge(S["y_t"], p - 2)
                    src = ps[:, 6 + (p - 3) % 2, 0:2 * 128].rearrange("p (c i s) -> p c i s", c=CH, i=2)
                    dst = yT[:, :, 2 * (p - 3) * SEQ:2 * (p - 2) * SEQ].rearrange("p c (i s) -> p c i s", i=2)
                    for c in range(CH):
                        last = act.activation(dst[:, c], src[:, c, :, 0:SEQ], ACT.Copy)
                    last.then_inc(S["yT_ready"], 1)
            for t in range(HALVES):
                norm(4, t)
            for t in range(HALVES):
                for m in range(DC):
                    act.wait_ge(S["up_mm"], DC * t + m + 1)
                    if t == 1 and m == 0:
                        act.wait_ge(S["ff_mm"], 1)
                    act.activation(hid[:, m, :], ps[:, 4 * t + m % 2, 0:HT], ACT.Gelu,
                                   bias=col("b1", m)).then_inc(S["up_gelu"], 1)
            for t in range(HALVES):
                norm(5, t)
            for t in range(HALVES):
                act.wait_ge(S["r_mm"], t + 1)
                act.activation(rlog[:, half(t)], ps[0:ROUTE, 4 * t, 0:HT], ACT.Copy).then_inc(S["r_copied"], 1)
            for t in range(HALVES):
                act.wait_ge(S["r_max"], t + 1)
                act.activation(rex[:, t, :, :], rtok[:, t, :, :], ACT.Exp).then_inc(S["r_exp"], 1)
            for t in range(HALVES):
                act.wait_ge(S["r_back"], t + 1)
                act.activation(wrows[:, half(t)], ps[0:ROUTE, 4 * t + 2, 0:HT], ACT.Copy).then_inc(S["w_rows"], 1)

            def split_weights(e):
                act.wait_ge(raw_in[e % 2], 48 * (e // 2 + 1))
                if e >= 2:
                    act.wait_ge(S["down_mm"], e - 1)
                act.activation(guhi[:, e % 2, :], guraw[:, e % 2, :], ACT.Copy).then_inc(S["w_hi"], 1)
                act.activation(dnhi[:, e % 2, 0:2 * EMB], dnraw[:, e % 2, 0:2 * EMB], ACT.Copy).then_inc(S["w_hi"], 1)
                act.activation(dnhi[0:96, e % 2, 2 * EMB:], dnraw[0:96, e % 2, 2 * EMB:], ACT.Copy)\
                   .then_inc(S["w_hi"], 1)

            split_weights(0)
            n = 0
            for e in range(BLOCKS):
                for m, (_, rows) in enumerate(MCH):
                    for t in range(HALVES):
                        act.wait_ge(S["g_mm"], n + 1)
                        if n >= 2:
                            act.wait_ge(S["gated"], n - 1)
                        act.activation(sil[0:rows, 0, n % 2, :], ps[0:rows, 4 + 2 * (n % 2), 0:HT], ACT.Silu)\
                           .then_inc(S["silu"], 1)
                        act.wait_ge(S["h_mul"], n + 1)
                        if e >= 2 and m == 0 and t == 0:
                            act.wait_ge(S["down_mm"], e - 1)
                        act.activation(hhi[0:rows, e % 2, m, half(t)], prod[0:rows, n % 2, :], ACT.Copy)\
                           .then_inc(S["h_hi"], 1)
                        n += 1
                    if m == 1 and e + 1 < BLOCKS:
                        split_weights(e + 1)

        @block.vector
        def _(dve):
            steps = [0]

            def link(ins):
                steps[0] += 1
                ins.then_inc(S["dve_step"], 1)
                dve.wait_ge(S["dve_step"], steps[0])

            def norm(k, t, src, out_ap, gain=None):
                n = HALVES * k + t
                dve.wait_ge(S["mean_mm"], n + 1)
                mean = ps[:, 4 * t, 0:HT].unsqueeze(1).to_broadcast([128, CH, HT])
                dve.tensor_tensor(xc[:, :, half(t)], src[:, :, half(t)], mean, ALU.subtract).then_inc(S["centred"], 1)
                dve.wait_ge(S["rstd_ready"], n + 1)
                scale = rstd[:, half(t)].unsqueeze(1).to_broadcast([128, CH, HT])
                dve.wait_ge(S["centred"], n + 1)
                if gain is None:
                    dve.tensor_tensor(out_ap[:, :, half(t)], xc[:, :, half(t)], scale, ALU.mult)\
                       .then_inc(S["normed"], 1)
                else:
                    g, b = gain
                    link(dve.tensor_tensor(out_ap[:, :, half(t)], xc[:, :, half(t)], scale, ALU.mult))
                    for c in range(CH):
                        last = dve.tensor_scalar(out_ap[:, c, half(t)], out_ap[:, c, half(t)], col(g, c), col(b, c),
                                                 ALU.mult, ALU.add)
                        if c == 0:
                            link(last)
                    last.then_inc(S["normed"], 1)

            dve.wait_ge(S["cols_in"], 16)
            dve.wait_ge(S["const_in"], 16)
            dve.tensor_scalar(bo3[:, :], col("bo", 0, CH), 0.3, None, ALU.mult).then_inc(S["setup"], 1)
            for t in range(HALVES):
                dve.wait_ge(S["tok_mm"], t + 1)
                for c in range(CH):
                    pos = col("pos", c * SEQ, SEQ).unsqueeze(1).to_broadcast([128, HT // SEQ, SEQ])
                    dve.scalar_tensor_tensor(
                        out=h[:, c, half(t)].rearrange("p (i s) -> p i s", s=SEQ),
                        in0=ps[:, 4 * t + 2 + c, 0:HT].rearrange("p (i s) -> p i s", s=SEQ),
                        scalar=col("b_proj", c), in1=pos, op0=ALU.add, op1=ALU.add).then_inc(S["h_ready"], 1)
            for t in range(HALVES):
                dve.wait_ge(S["h_ready"], CH * (t + 1))
                norm(0, t, h, xn)
            for t in range(HALVES):
                dve.wait_ge(S["qk_mm"], 2 * t + 2)
                link(dve.tensor_copy(sq[:, 0, half(t)], ps[:, 4 * t, 0:HT]))
                for g in range(CHH):
                    last = dve.tensor_scalar(kx[:, t, 0, g, :], sq[:, 0, half(t)], const("head")[:, g:g + 1], None,
                                             ALU.mult)
                last.then_inc(S["kx_dve"], 1)
            def softmax_a(p):
                dve.wait_ge(S["score_mm"], p + 1)
                if p >= 2:
                    dve.wait_ge(S["prob_ready"], p - 1)
                b0 = 2 * (p % 2)
                link(dve.tensor_tensor(sc[:, p % 2, :].rearrange("p (b n) -> p b n", b=2), ps[:, b0:b0 + 2, 0:CHH * SEQ],
                                       const("alibi").rearrange("p (b n) -> p b n", b=2), ALU.add))
                dve.tensor_reduce(top[:, p % 2, :], sc[:, p % 2, :].rearrange("p (h k) -> p h k", k=SEQ), AX.X,
                                  ALU.max).then_inc(S["row_max"], 1)

            def softmax_b(p):
                dve.wait_ge(S["exped"], p + 1)
                s = sc[:, p % 2, :].rearrange("p (h k) -> p h k", k=SEQ)
                link(dve.tensor_reduce(total[:, p % 2, :], s, AX.X, ALU.add))
                link(dve.reciprocal(total[:, p % 2, :], total[:, p % 2, :]))
                if p >= 2:
                    dve.wait_ge(S["prob_mm"], p - 1)
                dve.tensor_tensor(prob[:, p % 2, :, 0:SEQ], s,
                                  total[:, p % 2, :].unsqueeze(2).to_broadcast([128, HEADS, SEQ]), ALU.mult)\
                   .then_inc(S["prob_ready"], 1)

            def add_attention(p):
                dve.wait_ge(S["pv_mm"], p + 1)
                toks = slice(2 * p * SEQ, 2 * (p + 1) * SEQ)
                dve.tensor_tensor(h[:, :, toks], h[:, :, toks],
                                  ps[:, 6 + p % 2, 0:CH * 2 * SEQ].rearrange("p (c n) -> p c n", c=CH), ALU.add)\
                   .then_inc(S["attn_added"], 1)

            dve.wait_ge(S["pool_setup"], 5)
            for p in range(PAIRS + 2):
                if p < PAIRS:
                    softmax_a(p)
                if 1 <= p <= PAIRS:
                    softmax_b(p - 1)
                if p >= 2:
                    add_attention(p - 2)
            for t in range(HALVES):
                dve.wait_ge(S["attn_added"], HPAIRS * (t + 1))
                norm(1, t, h, xn)
            for t in range(HALVES):
                dve.wait_ge(S["p2_mm"], t + 1)
                link(dve.tensor_tensor(lg[:, t, :], ps[0:8, 4 * t + 1, 0:EXP], col("bp2", 0, EXP)[0:8], ALU.add))
                link(dve.max(mx8[:, t, :], lg[:, t, :]))
                dve.tensor_scalar(nmx[:, t:t + 1], mx8[:, t, 0:1], -1.0, None, ALU.mult).then_inc(S["p2_logit"], 1)
            for t in range(HALVES):
                dve.wait_ge(S["p2_exp"], t + 1)
                link(dve.reciprocal(rs8[:, t:t + 1], sm8[:, t:t + 1]))
                link(dve.tensor_scalar(pr8[:, t, :], ex8[:, t, :], rs8[:, t:t + 1], None, ALU.mult))
                link(dve.max(mx8[:, t, :], pr8[:, t, :]))
                dve.max_index(pick[:, t, :], mx8[:, t, :], pr8[:, t, :]).then_inc(S["pick_ready"], 1)
                dve.wait_ge(S["pick_ready"], t + 1)
                link(dve.tensor_copy(pickf[:, t:t + 1], pick[:, t, 0:1]))
                dve.tensor_scalar(hot[:, t, :], const("iota")[0:8], pickf[:, t:t + 1], None, ALU.is_equal)\
                   .then_inc(S["hot_ready"], 1)
            for t in range(HALVES):
                dve.wait_ge(S["hot_mm"], t + 1)
                dve.tensor_copy(hotT[:, 8 * t:8 * t + 8, :],
                                ps[0:EXP, 4 * t, 16:24].unsqueeze(2).to_broadcast([EXP, 8, SLOT]))\
                   .then_inc(S["hot_ready"], 1)
            dve.wait_ge(S["w1a_in"], 16)
            for p in range(PAIRS + 2):
                if p < PAIRS:
                    dve.wait_ge(S["pick_ready"], p // HPAIRS + 1)
                    for i in range(2):
                        if i == 0 and p == 0:
                            dve.wait_ge(S["pv_mm"], PAIRS)
                        if i == 0 and p >= 2:
                            dve.wait_ge(S["f1_mm"], p - 1)
                        r = (2 * p + i) % 8
                        e = dve.value_load(pick[r:r + 1, p // HPAIRS, 0:1], min_val=0, max_val=EXP - 1)
                        dve.tensor_copy(w1s[:, p % 2, i, :, :], w1a[:, bass.ds(e, 1), :, :])\
                           .then_inc(S["w1_copied"], 1)
                if 1 <= p <= PAIRS:
                    dve.wait_ge(S["f1_t"], p)
                    if p >= 3:
                        dve.wait_ge(S["f2_mm"], p - 2)
                    dve.tensor_copy(hgT[:, (p - 1) % 2, :, :],
                                    ps[:, 2 + (p - 1) % 2, :].rearrange("p (k n) -> p k n", k=FC))\
                       .then_inc(S["f1_T_ready"], 1)
                if p >= 2:
                    dve.wait_ge(S["f2_t"], p - 1)
                    src = ps[:, 6 + p % 2, 0:2 * 128].rearrange("p (c i s) -> p c i s", c=CH, i=2)
                    dst = rT[:, :, 2 * (p - 2) * SEQ:2 * (p - 1) * SEQ].rearrange("p c (i s) -> p c i s", i=2)
                    for c in range(CH):
                        last = dve.tensor_copy(dst[:, c], src[:, c, :, 0:SEQ])
                    last.then_inc(S["r_ready"], 1)
            dve.wait_ge(S["setup"], 1)
            for t in range(HALVES):
                for c in range(CH):
                    link(dve.scalar_tensor_tensor(out=xs[:, c, half(t)], in0=xn[:, c, half(t)],
                                                  scalar=bo3[:, c:c + 1], in1=h[:, c, half(t)], op0=ALU.add,
                                                  op1=ALU.add))
            for t in range(HALVES):
                dve.wait_ge(S["wo_mm"], t + 1)
                dve.scalar_tensor_tensor(out=h[:, :, half(t)], in0=ps[:, 4 * t + 2:4 * t + 4, 0:HT], scalar=0.3,
                                         in1=xs[:, :, half(t)], op0=ALU.mult, op1=ALU.add)\
                   .then_inc(S["ffn_added"], 1)
            for t in range(HALVES):
                dve.wait_ge(S["ffn_added"], t + 1)
                norm(2, t, h, xn)
            for t in range(HALVES):
                dve.wait_ge(S["normed"], 2 * HALVES + t + 1)
                link(dve.tensor_copy(rT[:, :, half(t)], xn[:, :, half(t)]))
                norm(3, t, rT, xn, ("g1", "be1"))
                dve.wait_ge(S["normed"], 3 * HALVES + t + 1)
                dve.wait_ge(S["pool_setup"], 7)
                for c in range(CH):
                    last = dve.tensor_copy(
                        xp[:, c, 8 * SLOT * t:8 * SLOT * (t + 1)].rearrange("p (i s) -> p i s", s=SLOT)[:, :, 0:SEQ],
                        xn[:, c, half(t)].rearrange("p (i s) -> p i s", s=SEQ))
                last.then_inc(S["slotted"], 1)
            for t in range(HALVES):
                dve.wait_ge(S["lq_mm"], t + 1)
                for c in range(CH):
                    last = dve.tensor_scalar(xs[:, c, half(t)], ps[:, 4 * t + 2 + c, 0:HT], col("bq", c), 0.0,
                                             ALU.add, ALU.min)
                last.then_inc(S["lq_min"], 1)
                dve.wait_ge(S["lq_exp"], t + 1)
                dve.wait_ge(S["lq_relu"], t + 1)
                dve.tensor_tensor(q[:, :, half(t)], q[:, :, half(t)], xs[:, :, half(t)], ALU.add)\
                   .then_inc(S["lq_ready"], 1)
                dve.wait_ge(S["lq_ready"], t + 1)
                for c in range(CH):
                    link(dve.tensor_scalar(xs[:, c, half(t)], rT[:, c, half(t)], col("out_b", c), None, ALU.add))

            def keys(p):
                dve.wait_ge(S["kv_mm"], p + 1)
                if p == 0:
                    dve.wait_ge(S["kvb_in"], 16)
                if p >= 2:
                    dve.wait_ge(S["state_mm"], p - 1)
                kv = ps[:, p % 2, :]
                dve.tensor_tensor(kf[:, p % 2, 0:EMB], kv[:, 0:EMB], kvb[:, 0:EMB], ALU.add).then_inc(S["k_ready"], 1)
                dve.tensor_tensor(vx[:, p % 2, :, 0:128], kv[:, EMB:].rearrange("p (c n) -> p c n", c=CH),
                                  kvb[:, EMB:].rearrange("p (c n) -> p c n", c=CH), ALU.add).then_inc(S["v2_ready"], 1)
                dve.wait_ge(S["k_ready"], p + 1)
                dve.tensor_scalar(ke[:, p % 2, 0:EMB], kf[:, p % 2, 0:EMB], 0.0, None, ALU.min).then_inc(S["k_min"], 1)

            def keys_b(p):
                dve.wait_ge(S["k_exp"], p + 1)
                dve.scalar_tensor_tensor(out=kf[:, p % 2, 0:EMB], in0=kf[:, p % 2, 0:EMB], scalar=0.0,
                                         in1=ke[:, p % 2, 0:EMB], op0=ALU.max, op1=ALU.add).then_inc(S["kf_ready"], 1)

            def state(p):
                dve.wait_ge(S["state_mm"], p + 1)
                if p >= 2:
                    dve.wait_ge(S["y_mm"], p - 1)
                for i in range(2):
                    last = dve.tensor_tensor(kvm[:, p % 2, i, :, :],
                                             ps[:, 2 + i, 0:CH * (128 + CHH)].rearrange("p (c n) -> p c n", c=CH),
                                             const("block").unsqueeze(1).to_broadcast([128, CH, 128 + CHH]), ALU.mult)
                last.then_inc(S["state_ready"], 1)

            def divide(p):
                dve.wait_ge(S["y_mm"], p + 1)
                y = ps[:, 4 + p % 2, 0:CH * (128 + CHH)].rearrange("p (c n) -> p c n", c=CH)
                link(dve.tensor_scalar(dinv[:, p % 2, :, :], y[:, :, 128:], DEN_EPS, None, ALU.max))
                link(dve.reciprocal(dinv[:, p % 2, :, :], dinv[:, p % 2, :, :]))
                if p >= 2:
                    dve.wait_ge(S["y_t"], p - 1)
                for c in range(CH):
                    last = dve.tensor_tensor(yt[:, p % 2, 128 * c:128 * c + 128].rearrange("p (g d) -> p g d", d=HD),
                                             y[:, c, 0:128].rearrange("p (g d) -> p g d", d=HD),
                                             dinv[:, p % 2, c, :].unsqueeze(2).to_broadcast([128, CHH, HD]), ALU.mult)
                last.then_inc(S["y_ready"], 1)

            for p in range(PAIRS + 2):
                if p < PAIRS:
                    keys(p)
                if p >= 2:
                    divide(p - 2)
                if p < PAIRS:
                    keys_b(p)
                if 1 <= p <= PAIRS:
                    state(p - 1)
            for t in range(HALVES):
                dve.wait_ge(S["out_mm"], t + 1)
                dve.tensor_tensor(xs[:, :, half(t)], xs[:, :, half(t)], ps[:, 4 * t + 2:4 * t + 4, 0:HT], ALU.add)\
                   .then_inc(S["x_ready"], 1)
            for t in range(HALVES):
                dve.wait_ge(S["x_ready"], t + 1)
                norm(4, t, xs, xn, ("g2", "be2"))
                for c in range(CH):
                    link(dve.scalar_tensor_tensor(out=h[:, c, half(t)], in0=xs[:, c, half(t)], scalar=col("b2", c),
                                                  in1=h[:, c, half(t)], op0=ALU.add, op1=ALU.add))
            for t in range(HALVES):
                dve.wait_ge(S["ff_mm"], t + 1)
                dve.tensor_tensor(h[:, :, half(t)], h[:, :, half(t)], ps[:, 4 * t + 2:4 * t + 4, 0:HT], ALU.add)\
                   .then_inc(S["ff_added"], 1)
            for t in range(HALVES):
                dve.wait_ge(S["ff_added"], t + 1)
                norm(5, t, h, xn)
                dve.wait_ge(S["normed"], 5 * HALVES + t + 1)
                dve.wait_ge(S["f1_mm"], PAIRS)
                dve.wait_ge(S["f2_mm"], PAIRS)
                dve.tensor_copy(xhi[:, :, half(t)], xn[:, :, half(t)]).then_inc(S["x_hi"], 1)
                dve.wait_ge(S["x_hi"], t + 1)
                dve.tensor_tensor(xlo[:, :, half(t)], xn[:, :, half(t)], xhi[:, :, half(t)].bitcast(F32),
                                  ALU.subtract).then_inc(S["x_lo"], 1)
            for t in range(HALVES):
                dve.wait_ge(S["r_t"], t + 1)
                src = ps[0:RT, 4 * t + 1, 0:RC * ROUTE].rearrange("p (c e) -> p c e", c=RC)
                link(dve.tensor_reduce(rsum[:, t, :], src[:, :, 0:EXP], AX.X, ALU.max))
                dve.tensor_tensor(rtok[:, t, :, 0:EXP], src[:, :, 0:EXP],
                                  rsum[:, t, :].unsqueeze(2).to_broadcast([RT, RC, EXP]), ALU.subtract)
                dve.tensor_scalar(rtok[:, t, :, EXP:], src[:, :, EXP:], -1.0, None, ALU.mult).then_inc(S["r_max"], 1)
            for t in range(HALVES):
                dve.wait_ge(S["r_exp"], t + 1)
                link(dve.tensor_reduce(rsum[:, t, :], rex[:, t, :, 0:EXP], AX.X, ALU.add))
                link(dve.reciprocal(rsum[:, t, :], rsum[:, t, :]))
                link(dve.tensor_tensor(rex[:, t, :, 0:EXP], rex[:, t, :, 0:EXP],
                                       rsum[:, t, :].unsqueeze(2).to_broadcast([RT, RC, EXP]), ALU.mult))
                for c in range(RC):
                    last = dve.max(rmx[:, t, c, :], rex[:, t, c, 0:EXP])
                link(last)
                for c in range(RC):
                    last = dve.max_index(rix[:, t, c, :], rmx[:, t, c, :], rex[:, t, c, 0:EXP])
                link(last)
                link(dve.tensor_copy(rixf[:, t, :, :], rix[:, t, :, :]))
                for c in range(RC):
                    dve.tensor_scalar(rm2[:, t, c, :], const("iota")[0:RT], rixf[:, t, c, 1:2], None, ALU.is_equal)
                    last = dve.tensor_scalar(rw[:, t, c, 0:EXP], const("iota")[0:RT], rixf[:, t, c, 0:1], None,
                                             ALU.is_equal)
                link(last)
                link(dve.tensor_tensor(rm2[:, t, :, :], rm2[:, t, :, :], rw[:, t, :, 0:EXP], ALU.add))
                link(dve.tensor_tensor(rw[:, t, :, 0:EXP], rm2[:, t, :, :], rex[:, t, :, 0:EXP], ALU.mult))
                link(dve.tensor_scalar(rw[:, t, :, EXP:], rex[:, t, :, EXP:], 1.0, None, ALU.add))
                dve.reciprocal(rw[:, t, :, EXP:], rw[:, t, :, EXP:]).then_inc(S["r_w"], 1)

            def split_weights(e):
                if e >= 2:
                    dve.wait_ge(S["down_mm"], e - 1)
                for n, (lo, hi, raw) in enumerate((
                        (gulo[:, e % 2, :], guhi[:, e % 2, :], guraw[:, e % 2, :]),
                        (dnlo[:, e % 2, 0:2 * EMB], dnhi[:, e % 2, 0:2 * EMB], dnraw[:, e % 2, 0:2 * EMB]),
                        (dnlo[0:96, e % 2, 2 * EMB:], dnhi[0:96, e % 2, 2 * EMB:], dnraw[0:96, e % 2, 2 * EMB:]))):
                    dve.wait_ge(S["w_hi"], 3 * e + n + 1)
                    dve.tensor_tensor(lo, raw, hi.bitcast(F32), ALU.subtract).then_inc(S["w_lo"], 1)

            split_weights(0)
            n = 0
            for e in range(BLOCKS):
                for m, (_, rows) in enumerate(MCH):
                    for t in range(HALVES):
                        dve.wait_ge(S["gated"], n + 1)
                        dve.wait_ge(S["u_mm"], n + 1)
                        if n >= 2:
                            dve.wait_ge(S["h_hi"], n - 1)
                            dve.wait_ge(S["h_lo"], n - 1)
                        dve.tensor_tensor(prod[0:rows, n % 2, :], sil[0:rows, 1, n % 2, :],
                                          ps[0:rows, 5 + 2 * (n % 2), 0:HT], ALU.mult).then_inc(S["h_mul"], 1)
                        dve.wait_ge(S["h_hi"], n + 1)
                        dve.tensor_tensor(hlo[0:rows, e % 2, m, half(t)], prod[0:rows, n % 2, :],
                                          hhi[0:rows, e % 2, m, half(t)].bitcast(F32), ALU.subtract)\
                           .then_inc(S["h_lo"], 1)
                        n += 1
                    if m == 1 and e + 1 < BLOCKS:
                        split_weights(e + 1)
            for c in range(CH):
                for t in range(HALVES):
                    dve.wait_ge(S["down_mm"], BLOCKS)
                    dve.tensor_tensor(xs[:, c, half(t)], h[:, c, half(t)], ps[:, 2 * c + t, 0:HT], ALU.add)\
                       .then_inc(S["moe_added"], 1)

        @block.tensor
        def _(pe):
            def dense(bank, w, m, x, t, ks=CH):
                for k in range(ks):
                    last = pe.matmul(ps[:, bank, 0:HT], w[:, k, 128 * m:128 * m + 128], x[:, k, half(t)],
                                     start=(k == 0), stop=(k == ks - 1))
                return last

            def norm(k, t, src):
                n = HALVES * k + t
                for c in range(CH):
                    last = pe.matmul(ps[:, 4 * t, 0:HT], ones_mean, src[:, c, half(t)], start=(c == 0),
                                     stop=(c == CH - 1))
                last.then_inc(S["mean_mm"], 1)
                pe.wait_ge(S["squared"], n + 1)
                for c in range(CH):
                    last = pe.matmul(ps[:, 4 * t + 1, 0:HT], ones_mean, sq[:, c, half(t)], start=(c == 0),
                                     stop=(c == CH - 1))
                last.then_inc(S["var_mm"], 1)

            pe.wait_ge(S["wp_in"], 16)
            pe.wait_ge(S["patch_in"], 16)
            for t in range(HALVES):
                for m in range(CH):
                    last = dense(4 * t + 2 + m, wp, m, X, t, KP)
                last.then_inc(S["tok_mm"], 1)
            pe.wait_ge(S["const_in"], 16)
            for t in range(HALVES):
                pe.wait_ge(S["h_ready"], CH * (t + 1))
                norm(0, t, h)
            pe.wait_ge(S["kqv_in"], 16)
            for t in range(HALVES):
                pe.wait_ge(S["normed"], t + 1)
                for m in range(CH):
                    last = dense(4 * t + 2 + m, kqv, CH + m, xn, t)
                last.then_inc(S["qk_mm"], 1)
                for m in range(CH):
                    last = dense(4 * t + m, kqv, m, xn, t)
                last.then_inc(S["qk_mm"], 1)
            pe.wait_ge(S["pool_setup"], 3)
            pe.wait_ge(S["normed"], HALVES)
            for t in range(HALVES):
                pe.wait_ge(S["q_ready"], t + 1)
                for n in range(8):
                    i = 8 * t + n
                    for o in range(2):
                        for k in range(CH):
                            last = pe.matmul(ps[64 * o:64 * o + 64, 4 * t + 2 + n // 4, 128 * (n % 4):128 * (n % 4) + 128],
                                             xn[:, k, slot(i)], kqv[:, k, 2 * EMB + 128 * o:2 * EMB + 128 * o + 128],
                                             start=(k == 0), stop=(k == CH - 1))
                last.then_inc(S["v_mm"], 1)

            def scores(p):
                if p == 0:
                    for name in ("q_ready", "kx_dve", "kx_act", "v_ready"):
                        pe.wait_ge(S[name], HALVES)
                if p >= 2:
                    pe.wait_ge(S["row_max"], p - 1)
                for c in range(CH):
                    for i in range(2):
                        a = 2 * p + i
                        t, o = a // 8, (a % 8) * SEQ
                        last = pe.matmul(ps[64 * i:64 * i + 64, 2 * (p % 2) + c, 0:CHH * SEQ], q[:, c, slot(a)],
                                         kx[:, t, c, :, o:o + SEQ], start=True, stop=True)
                last.then_inc(S["score_mm"], 1)

            def turn_probs(p):
                pe.wait_ge(S["prob_ready"], p + 1)
                if p >= 1:
                    pe.wait_ge(S["pT_ready"], p)
                pr = prob[:, p % 2, :, :].rearrange("p (j o) s -> p j (o s)", o=2)
                for j in range(HEADS // 2):
                    last = pe.transpose(ps[:, 4 + j // 4, 128 * (j % 4):128 * (j % 4) + 128], pr[:, j, :], ident)
                last.then_inc(S["prob_mm"], 1)

            def values(p):
                pe.wait_ge(S["pT_ready"], p + 1)
                if p >= 2:
                    pe.wait_ge(S["attn_added"], p - 1)
                for c in range(CH):
                    for i in range(2):
                        for j in range(4):
                            o = 2 * SEQ * c + SEQ * i
                            last = pe.matmul(ps[32 * j:32 * j + 32, 6 + p % 2, o:o + SEQ], vbd[:, 2 * p + i, 4 * c + j, :],
                                             pT[:, p % 2, 4 * c + j, i, :], start=True, stop=True)
                last.then_inc(S["pv_mm"], 1)

            for p in range(PAIRS + 2):
                if p < PAIRS:
                    scores(p)
                if 1 <= p <= PAIRS:
                    turn_probs(p - 1)
                if p >= 2:
                    values(p - 2)
            for t in range(HALVES):
                pe.wait_ge(S["attn_added"], HPAIRS * (t + 1))
                norm(1, t, h)
            pe.wait_ge(S["wp1_in"], 16)
            pe.wait_ge(S["wp2_in"], 16)
            for t in range(HALVES):
                pe.wait_ge(S["normed"], HALVES + t + 1)
                for k in range(CH):
                    last = pe.matmul(ps[:, 4 * t, 0:8], wp1_sb[:, k, :],
                                     xn[:, k, half(t)].rearrange("p (i s) -> p i s", s=SEQ)[:, :, SEQ - 1],
                                     start=(k == 0), stop=(k == CH - 1))
                last.then_inc(S["p1_mm"], 1)
            for t in range(HALVES):
                pe.wait_ge(S["p1_act"], t + 1)
                pe.matmul(ps[0:8, 4 * t + 1, 0:EXP], act8[:, t, :], wp2_sb[:, :], start=True, stop=True)\
                  .then_inc(S["p2_mm"], 1)
            for t in range(HALVES):
                pe.wait_ge(S["hot_ready"], t + 1)
                pe.transpose(ps[0:EXP, 4 * t, 16:24], hot[:, t, :], ident[0:8, 0:8]).then_inc(S["hot_mm"], 1)
            pe.wait_ge(S["b1_in"], 16)
            pe.wait_ge(S["b2_in"], 16)
            pe.wait_ge(S["hot_ready"], 2 * HALVES)

            def rows_up(p):
                pe.wait_ge(S["w1_copied"], 2 * p + 2)
                if p >= 2:
                    pe.wait_ge(S["f1_gelu"], p - 1)
                for i in range(2):
                    pe.matmul(ps[64 * i:64 * i + 64, p % 2, :], hotT[:, 2 * p + i, :], b1_sb[:, :], start=True, stop=False)
                for k in range(CH):
                    for i in range(2):
                        last = pe.matmul(ps[64 * i:64 * i + 64, p % 2, :], xn[:, k, slot(2 * p + i)],
                                         w1s[:, p % 2, i, k, :], start=False, stop=(k == CH - 1))
                last.then_inc(S["f1_mm"], 1)

            def turn_rows(p):
                pe.wait_ge(S["f1_gelu"], p + 1)
                if p >= 2:
                    pe.wait_ge(S["f1_T_ready"], p - 1)
                for k in range(FC):
                    last = pe.transpose(ps[:, 2 + p % 2, 128 * k:128 * k + 128], hg[:, p % 2, 128 * k:128 * k + 128], ident)
                last.then_inc(S["f1_t"], 1)

            def rows_down(p):
                pe.wait_ge(S["f1_T_ready"], p + 1)
                pe.wait_ge(S["w2_copied"], 2 * p + 2)
                if p >= 2:
                    pe.wait_ge(S["f2_ready"], p - 1)
                for i in range(2):
                    pe.matmul(ps[64 * i:64 * i + 64, 4 + p % 2, 0:EMB], hotT[:, 2 * p + i, :], b2_sb[:, :], start=True,
                              stop=False)
                for k in range(FC):
                    for i in range(2):
                        last = pe.matmul(ps[64 * i:64 * i + 64, 4 + p % 2, 0:EMB], hgT[:, p % 2, k, 64 * i:64 * i + 64],
                                         w2s[:, p % 2, i, k, :], start=False, stop=(k == FC - 1))
                last.then_inc(S["f2_mm"], 1)

            def turn_out(p):
                pe.wait_ge(S["f2_ready"], p + 1)
                if p >= 2:
                    pe.wait_ge(S["r_ready"], p - 1)
                for c in range(CH):
                    last = pe.transpose(ps[:, 6 + p % 2, 128 * c:128 * c + 128], rr[:, p % 2, 128 * c:128 * c + 128], ident)
                last.then_inc(S["f2_t"], 1)

            for p in range(PAIRS + 2):
                if p < PAIRS:
                    rows_up(p)
                if 1 <= p <= PAIRS:
                    turn_rows(p - 1)
                    rows_down(p - 1)
                if p >= 2:
                    turn_out(p - 2)
            pe.wait_ge(S["wo_in"], 16)
            pe.wait_ge(S["r_ready"], PAIRS)
            for t in range(HALVES):
                for m in range(CH):
                    last = dense(4 * t + 2 + m, wo_sb, m, rT, t)
                last.then_inc(S["wo_mm"], 1)
            for t in range(HALVES):
                pe.wait_ge(S["ffn_added"], t + 1)
                norm(2, t, h)
            for t in range(HALVES):
                pe.wait_ge(S["normed"], 2 * HALVES + t + 1)
                norm(3, t, xn)
            pe.wait_ge(S["qkv_in"], 16)
            for t in range(HALVES):
                pe.wait_ge(S["normed"], 3 * HALVES + t + 1)
                for m in range(CH):
                    last = dense(4 * t + 2 + m, qkv, m, xn, t)
                last.then_inc(S["lq_mm"], 1)

            def keys_values(p):
                if p == 0:
                    pe.wait_ge(S["slotted"], HALVES)
                if p >= 2:
                    pe.wait_ge(S["v2_ready"], p - 1)
                for k in range(CH):
                    last = pe.matmul(ps[:, p % 2, :], xp[:, k, 128 * p:128 * p + 128], qkv[:, k, EMB:3 * EMB], start=(k == 0),
                                     stop=(k == CH - 1))
                last.then_inc(S["kv_mm"], 1)

            def states(p):
                pe.wait_ge(S["kf_ready"], p + 1)
                pe.wait_ge(S["v2_ready"], p + 1)
                if p == 0:
                    pe.wait_ge(S["lq_ready"], HALVES)
                if p >= 1:
                    pe.wait_ge(S["state_ready"], p)
                w = 128 + CHH
                for c in range(CH):
                    for i in range(2):
                        a = 64 * i
                        last = pe.matmul(ps[:, 2 + i, w * c:w * c + w], kf[a:a + SEQ, p % 2, 128 * c:128 * c + 128],
                                         vx[a:a + SEQ, p % 2, c, :], start=True, stop=True)
                last.then_inc(S["state_mm"], 1)

            def outputs(p):
                pe.wait_ge(S["state_ready"], p + 1)
                if p == 0:
                    pe.wait_ge(S["lq_ready"], HALVES)
                if p >= 2:
                    pe.wait_ge(S["y_ready"], p - 1)
                w = 128 + CHH
                for c in range(CH):
                    for i in range(2):
                        last = pe.matmul(ps[64 * i:64 * i + 64, 4 + p % 2, w * c:w * c + w], q[:, c, slot(2 * p + i)],
                                         kvm[:, p % 2, i, c, :], start=True, stop=True)
                last.then_inc(S["y_mm"], 1)

            def turn_y(p):
                pe.wait_ge(S["y_ready"], p + 1)
                if p >= 2:
                    pe.wait_ge(S["yT_ready"], p - 1)
                for c in range(CH):
                    last = pe.transpose(ps[:, 6 + p % 2, 128 * c:128 * c + 128], yt[:, p % 2, 128 * c:128 * c + 128], ident)
                last.then_inc(S["y_t"], 1)

            for p in range(PAIRS + 3):
                if p < PAIRS:
                    keys_values(p)
                if 1 <= p <= PAIRS:
                    states(p - 1)
                if 2 <= p <= PAIRS + 1:
                    outputs(p - 2)
                if p >= 3:
                    turn_y(p - 3)
            pe.wait_ge(S["wout_in"], 16)
            pe.wait_ge(S["yT_ready"], PAIRS)
            for t in range(HALVES):
                for m in range(CH):
                    last = dense(4 * t + 2 + m, wout, m, yT, t)
                last.then_inc(S["out_mm"], 1)
            for t in range(HALVES):
                pe.wait_ge(S["x_ready"], t + 1)
                norm(4, t, xs)
            pe.wait_ge(S["fw_in"], 32)
            for t in range(HALVES):
                pe.wait_ge(S["normed"], 4 * HALVES + t + 1)
                for m in range(DC):
                    if m >= 2:
                        pe.wait_ge(S["up_gelu"], DC * t + m - 1)
                    dense(4 * t + m % 2, fw1, m, xn, t).then_inc(S["up_mm"], 1)
                pe.wait_ge(S["up_gelu"], DC * (t + 1))
                for m in range(CH):
                    for k in range(DC):
                        last = pe.matmul(ps[:, 4 * t + 2 + m, 0:HT], fw2[:, k, 128 * m:128 * m + 128], hid[:, k, :],
                                         start=(k == 0), stop=(k == DC - 1))
                last.then_inc(S["ff_mm"], 1)
            for t in range(HALVES):
                pe.wait_ge(S["ff_added"], t + 1)
                norm(5, t, h)
            pe.wait_ge(S["route_in"], 16)
            for t in range(HALVES):
                pe.wait_ge(S["normed"], 5 * HALVES + t + 1)
                for k in range(CH):
                    last = pe.matmul(ps[0:ROUTE, 4 * t, 0:HT], route_sb[:, k, :], xn[:, k, half(t)], start=(k == 0),
                                     stop=(k == CH - 1))
                last.then_inc(S["r_mm"], 1)
            for t in range(HALVES):
                pe.wait_ge(S["r_copied"], t + 1)
                for c in range(RC):
                    a = t * HT + RT * c
                    last = pe.transpose(ps[0:RT, 4 * t + 1, ROUTE * c:ROUTE * c + ROUTE], rlog[:, a:a + RT],
                                        ident[0:ROUTE, 0:ROUTE])
                last.then_inc(S["r_t"], 1)
            for t in range(HALVES):
                pe.wait_ge(S["r_w"], t + 1)
                for c in range(RC):
                    last = pe.transpose(ps[0:ROUTE, 4 * t + 2, RT * c:RT * c + RT], rw[:, t, c, :], ident[0:RT, 0:RT])
                last.then_inc(S["r_back"], 1)
            pe.wait_ge(S["w_rows"], HALVES)
            pe.wait_ge(S["x_lo"], HALVES)

            def exact(bank, rows, whi, wlo, xh, xl, first, final):
                pe.matmul(bank, whi, xh, start=first, stop=False)
                pe.matmul(bank, wlo, xh, start=False, stop=False)
                return pe.matmul(bank, whi, xl, start=False, stop=final)

            def down(e):
                pe.wait_ge(S["h_lo"], 2 * MC * (e + 1))
                pe.wait_ge(S["w_lo"], 3 * (e + 1))
                for c in range(CH):
                    for m, (_, rows) in enumerate(MCH):
                        o = EMB * m + 128 * c
                        for t in range(HALVES):
                            last = exact(ps[:, 2 * c + t, 0:HT], 128, dnhi[0:rows, e % 2, o:o + 128],
                                         dnlo[0:rows, e % 2, o:o + 128], hhi[0:rows, e % 2, m, half(t)],
                                         hlo[0:rows, e % 2, m, half(t)], e == 0 and m == 0,
                                         e == BLOCKS - 1 and m == MC - 1)
                last.then_inc(S["down_mm"], 1)

            n = 0
            for e in range(BLOCKS):
                pe.wait_ge(S["w_lo"], 3 * e + 1)
                for m, (r0, rows) in enumerate(MCH):
                    for t in range(HALVES):
                        if n >= 2:
                            pe.wait_ge(S["h_mul"], n - 1)
                        for u, done in enumerate(("g_mm", "u_mm")):
                            for k in range(CH):
                                o = 2 * MOE_I * k + MOE_I * u + r0
                                last = exact(ps[0:rows, 4 + 2 * (n % 2) + u, 0:HT], rows, guhi[:, e % 2, o:o + rows],
                                             gulo[:, e % 2, o:o + rows], xhi[:, k, half(t)], xlo[:, k, half(t)],
                                             k == 0, k == CH - 1)
                            last.then_inc(S[done], 1)
                        n += 1
                    if m == 0 and e >= 1:
                        down(e - 1)
            down(BLOCKS - 1)


def wt(w):
    k, m = w.shape
    return np.ascontiguousarray(w.reshape(k // 128, 128, m).transpose(1, 0, 2))


def kernel(**inp):
    import concourse.bacc as bacc
    from concourse.bass_utils import run_bass_kernel_spmd

    a = {k: np.asarray(v) for k, v in inp.items()}
    side = 96 // 16
    x = a["x"].reshape(IMGS, side, 16, side, 16, 3).transpose(2, 4, 5, 0, 1, 3).reshape(PATCH, TOK)
    kqv = a["L0_attn_W_kqv"].T
    v = kqv[:, 2 * EMB:].reshape(EMB, HEADS // 2, 2, HD).transpose(0, 2, 1, 3).reshape(EMB, EMB)
    cols = np.zeros((128, NCOLS), np.float32)

    def put(name, value):
        cols[:, COLS[name][0]:COLS[name][1]] = value

    def per_feature(b):
        return b.reshape(-1, 128).T

    put("b_proj", per_feature(a["L0_tok_b_proj"]))
    put("pos", a["L0_tok_pos_emb"].T.reshape(CH, 128, SEQ).transpose(1, 0, 2).reshape(128, -1))
    put("bp1", a["L0_ffn_bp1"].reshape(128, 1))
    put("bp2", np.broadcast_to(a["L0_ffn_bp2"], (128, EXP)))
    put("bo", per_feature(a["L0_ffn_bo"]))
    put("bq", per_feature(a["L1_attn_qkv_b"][:EMB]))
    for name in ("out_b", "b1", "b2", "g1", "be1", "g2", "be2"):
        put(name, per_feature(a["L1_attn_" + name]))

    consts = np.zeros((128, NCONST), np.float32)

    def fix(name, value):
        consts[:, CONST[name][0]:CONST[name][1]] = value

    fix("ident", np.eye(128))
    fix("mean", 1.0 / EMB)
    base = (2 ** 8) ** (1.0 / HEADS)
    slopes = np.array([1.0 / base ** (i + 1) for i in range(HEADS)], np.float32)
    rel = (np.arange(SEQ)[None, :] - np.arange(SEQ)[:, None]).astype(np.float32)
    alibi = np.where(rel[:, None, :] > 0, np.float32(NEG), slopes[None, :, None] * rel[:, None, :])
    both = np.zeros((128, HEADS * SEQ), np.float32)
    both[0:SEQ] = both[64:64 + SEQ] = alibi.reshape(SEQ, -1)
    fix("alibi", both)
    part = np.arange(128)[:, None] // HD
    fix("head", part == np.arange(CHH)[None])
    fix("block", np.concatenate([part == np.arange(128)[None] // HD, part == np.arange(CHH)[None]], 1))
    fix("iota", np.arange(EXP)[None])

    w1 = a["L0_ffn_W1"].reshape(EXP, CH, 128, FFN).transpose(2, 0, 1, 3)
    w2 = a["L0_ffn_W2"].reshape(EXP, FC, 128, EMB).transpose(2, 0, 1, 3)
    qkv = a["L1_attn_qkv_w"]
    sg, su, sd = (a["L1_ffn_shared_" + n + "_w"] for n in ("gate", "up", "down"))
    gu = [a["L1_ffn_experts_gate_up"][e] for e in range(EXP)]
    gu += [np.concatenate([sg[s:s + MOE_I], su[s:s + MOE_I]], 0) for s in (0, MOE_I)]
    gu = np.stack([wt(g.T).reshape(128, GU) for g in gu])
    dn = [a["L1_ffn_experts_down"][e].T for e in range(EXP)] + [sd.T[s:s + MOE_I] for s in (0, MOE_I)]
    down = np.zeros((BLOCKS, 128, MC, EMB), np.float32)
    for e, d in enumerate(dn):
        for m, (r0, rows) in enumerate(MCH):
            down[e, :rows, m] = d[r0:r0 + rows]
    route = np.concatenate([a["L1_ffn_gate_w"], a["L1_ffn_shared_expert_gate_w"]], 0).T

    arrays = {
        "patches": wt(x), "w_proj": wt(a["L0_tok_W_proj"].T), "w_kqv": wt(np.concatenate([kqv[:, :2 * EMB], v], 1)),
        "cols": cols, "consts": consts, "wp1": wt(a["L0_ffn_Wp1"]), "wp2": a["L0_ffn_Wp2"],
        "w1x": w1, "b1x": a["L0_ffn_b1"], "w2x": w2, "b2x": a["L0_ffn_b2"], "wo": wt(a["L0_ffn_Wo"]),
        "qkv_w": wt(qkv), "kv_b": a["L1_attn_qkv_b"][EMB:], "out_w": wt(a["L1_attn_out_w"]),
        "ffn_w1": wt(a["L1_attn_w1"]), "ffn_w2": wt(a["L1_attn_w2"]), "route_w": wt(route),
        "moe_gu": gu, "moe_down": down.reshape(BLOCKS, 128, DOWN),
    }
    arrays = {k: np.ascontiguousarray(v) for k, v in arrays.items()}
    nc = bacc.Bacc("TRN2", target_bir_lowering=False, num_devices=1)
    args = {k: nc.dram_tensor(k, v.shape, F32, kind="ExternalInput").ap() for k, v in arrays.items()}
    out = nc.dram_tensor("out", (128, CH, TOK), F32, kind="ExternalOutput").ap()
    tower(nc, out=out, **args)
    r = run_bass_kernel_spmd(nc, [arrays], core_ids=[0])
    got = r.results[0]["out"]
    return np.ascontiguousarray(got.transpose(2, 1, 0).reshape(IMGS, SEQ, EMB))
```

```python
from contextlib import ExitStack

import numpy as np

import concourse.bass as bass
from concourse import mybir

F32 = mybir.dt.float32
F32R = mybir.dt.float32r
BF16 = mybir.dt.bfloat16
U32 = mybir.dt.uint32
ALU = mybir.AluOpType
ACT = mybir.ActivationFunctionType
AX = mybir.AxisListType

IMGS, SEQ, EMB, PATCH = 16, 36, 256, 768
TOK = IMGS * SEQ
CH = EMB // 128
HALVES = 2
HT = TOK // HALVES
PAIRS = IMGS // 2
HPAIRS = PAIRS // HALVES
HEADS, HD = 16, 16
CHH = 128 // HD
SLOT = 64
PAD = SLOT - SEQ
KP = PATCH // 128
EXP, FFN = 8, 512
PARTS = 3
FC = FFN // 128
NAV = 128
DFF = 1024
DC = DFF // 128
MOE_I = 352
MCH = [(0, 128), (128, 128), (256, 96)]
MC = len(MCH)
SHARED = 2
BLOCKS = SHARED + EXP
STEPS = HALVES * MC
SPLIT_AT = (1, 4, 5)
DOWN_AFTER = 1
FIRST_DOWN_AFTER = STEPS + 2
GU = CH * 2 * MOE_I
DOWN = MC * EMB
RT = 96
RC = HT // RT
ROUTE = EXP + 1
NORM_BANK = ((0, 4), (7, 6), (6, 7), (6, 7), (6, 7), (2, 5))
QUERY_BANK = (2, 6)
OUT_BANK = (6, 0)
EPS = 1e-5
DEN_EPS = 1e-6
NEG = -1e30

COLS = {}
_at = 0
for _name, _n in (("b_proj", CH), ("pos", CH * SEQ), ("bp1", 1), ("bp2", EXP), ("bo", CH), ("bq", CH),
                  ("out_b", CH), ("b1", DC), ("b2", CH), ("g1", CH), ("be1", CH), ("g2", CH), ("be2", CH)):
    COLS[_name] = (_at, _at + _n)
    _at += _n
NCOLS = _at
CONST = {}
_at = 0
for _name, _n in (("ident", 128), ("mean", 128), ("head", CHH), ("block", 128 + CHH), ("iota", PARTS * EXP), ("ones", 2 * HD),
                  ("later", PARTS - 1), ("alibi", HEADS * SEQ)):
    CONST[_name] = (_at, _at + _n)
    _at += _n
NCONST = _at


def moe_step(n):
    return n // STEPS, n // MC % HALVES, n % MC


def tower(nc, patches, w_proj, w_kqv, cols, consts, wp1, wp2, w1x, b1x, w2x, b2x, wo,
          qkv_w, kv_b, out_w, ffn_w1, ffn_w2, route_w, moe_gu, moe_down, out):
    with ExitStack() as ctx:
        def sb(name, shape, dt=F32, where=ctx):
            return where.enter_context(nc.sbuf_tensor(name, shape, dt))

        def sem(name):
            return ctx.enter_context(nc.semaphore(name))

        gate_dram = nc.dram_tensor("gate_dram", (ROUTE, TOK), F32, kind="Internal").ap()
        ps = ctx.enter_context(nc.psum_tensor("ps", [128, 8, 512], F32))

        h = sb("h", [128, CH, TOK])
        xc = sb("xc", [128, CH, TOK])
        sq = sb("sq", [128, CH, TOK])
        rstd = sb("rstd", [128, TOK])
        xn = sb("xn", [128, CH, TOK + PAD])
        xs = sb("xs", [128, CH, TOK])
        rT = sb("rT", [128, CH, TOK])
        q = sb("q", [128, CH, TOK + PAD])
        vec = sb("vec", [128, NCOLS])
        cst = sb("cst", [128, NCONST])
        eps = sb("eps", [128, 1])
        bo3 = sb("bo3", [128, CH])
        kqv = sb("kqv", [128, CH, 3 * EMB])
        wo_sb = sb("wo_sb", [128, CH, EMB])
        wp1_sb = sb("wp1_sb", [128, CH, NAV])
        wp2_sb = sb("wp2_sb", [128, EXP])
        route_sb = sb("route_sb", [128, CH, ROUTE])
        sc = sb("sc", [128, 2, HEADS * SEQ])
        top = sb("top", [128, 2, HEADS])
        rsums = sb("rsums", [128, 2, CH, 2 * SEQ])
        attn = sb("attn", [128, 2, CH, 2 * SEQ])
        act8 = sb("act8", [128, HALVES, 8])
        lg = sb("lg", [8, HALVES, EXP])
        mx8 = sb("mx8", [8, HALVES, 8])
        nmx = sb("nmx", [8, HALVES])
        ex8 = sb("ex8", [8, HALVES, EXP])
        sm8 = sb("sm8", [8, HALVES])
        rs8 = sb("rs8", [8, HALVES])
        pr8 = sb("pr8", [8, HALVES, EXP])
        pick = sb("pick", [8, HALVES, 8], U32)
        pickf = sb("pickf", [8, HALVES])
        hot = sb("hot", [8, HALVES, PARTS * EXP])
        hotT = sb("hotT", [PARTS * EXP, IMGS, SLOT], BF16)
        bias_parts = sb("bias_parts", [PARTS * EXP, FFN + EMB], BF16)

        bias_raw = xs[0:PARTS * EXP].rearrange("p c n -> p (c n)")[:, 0:FFN + EMB]
        bias_off = rT[0:PARTS * EXP].rearrange("p c n -> p (c n)")[:, 0:FFN + EMB]

        def col(name, a=0, n=1):
            return vec[:, COLS[name][0] + a:COLS[name][0] + a + n]

        def const(name):
            return cst[:, CONST[name][0]:CONST[name][1]]

        ident = const("ident")
        ones_mean = const("mean")

        with ExitStack() as reg:
            kx = sb("kx", [128, HALVES, CH, CHH, HT], where=reg)
        with ExitStack() as reg:
            fw1 = sb("fw1", [128, CH, DFF], where=reg)
            fw2 = sb("fw2", [128, DC, EMB], where=reg)
            hid = sb("hid", [128, DC, HT], where=reg)
            qkv = sb("qkv", [128, CH, 3 * EMB], where=reg)
            wout = sb("wout", [128, CH, EMB], where=reg)
            kvb = sb("kvb", [128, 2 * EMB], where=reg)
        with ExitStack() as reg:
            hhi = sb("hhi", [128, 2, MC, TOK], F32R, where=reg)
            hlo = sb("hlo", [128, 2, MC, TOK], F32R, where=reg)
        holdC = sb("holdC", [128, 9216])
        with ExitStack() as reg:
            X = sb("X", [128, KP, TOK], where=reg)
            wp = sb("wp", [128, KP, EMB], where=reg)
        with ExitStack() as reg:
            vbd = sb("vbd", [128, IMGS, HEADS // 2, 2 * HD], where=reg)
            prob = sb("prob", [128, 2, HEADS, SLOT], where=reg)
            pT = sb("pT", [128, 2, HEADS // 2, 2, SEQ], where=reg)
        with ExitStack() as reg:
            w1s = sb("w1s", [128, 2, 2, CH, FFN], where=reg)
            w2s = sb("w2s", [128, 2, 2, FC, EMB], where=reg)
        with ExitStack() as reg:
            vx = sb("vx", [128, 2, CH, 128 + CHH], where=reg)
            kvm = sb("kvm", [128, 2, 2, CH, 128 + CHH], where=reg)
            xp = sb("xp", [128, CH, IMGS * SLOT], where=reg)
        with ExitStack() as reg:
            gate = sb("gate", [128, ROUTE, TOK], where=reg)
            xhi = sb("xhi", [128, CH, TOK], F32R, where=reg)
            xlo = sb("xlo", [128, CH, TOK], F32R, where=reg)
        holdB = sb("holdB", [128, 8192])
        with ExitStack() as reg:
            w1a = sb("w1a", [128, EXP, CH, FFN], where=reg)
            w2a = sb("w2a", [128, EXP, FC, EMB], where=reg)
        with ExitStack() as reg:
            guhi = sb("guhi", [128, 2, GU], F32R, where=reg)
            gulo = sb("gulo", [128, 2, GU], F32R, where=reg)
            dnhi = sb("dnhi", [128, 2, DOWN], F32R, where=reg)
            dnlo = sb("dnlo", [128, 2, DOWN], F32R, where=reg)
            guraw = sb("guraw", [128, 2, GU], where=reg)
            dnraw = sb("dnraw", [128, 2, DOWN], where=reg)
            sil = sb("sil", [128, 2, 2, HT], where=reg)
            prod = sb("prod", [128, 2, HT], where=reg)
            wrows = sb("wrows", [ROUTE, TOK], where=reg)
            rlog = sb("rlog", [ROUTE, TOK], where=reg)
        holdA = sb("holdA", [128, 16384])
        hg = sb("hg", [128, 2, FFN])
        hgT = sb("hgT", [128, 2, FC, 128])
        rr = sb("rr", [128, 2, EMB])
        kf = hg
        ke = sc
        yt = rr
        dinv = sb("dinv", [128, 2, CH, CHH])
        yT = rT

        S = {}
        for name in (
            "alibi_in", "cols_in", "const_in", "kqv_in", "qkv_in", "wout_in", "wo_in", "kvb_in",
            "wp1_in", "wp2_in", "bias_in", "bias_step", "route_in", "w1a_in", "w2a_in", "fw_in",
            "setup", "bias_ready", "act_setup", "pool_setup", "dve_step", "act_step", "pool_step",
            "tok_mm", "h_ready", 
            "qk_mm", "q_ready", "kx_dve", "kx_act", "v_mm", "v_act", "v_dve",
            "score_mm", "biased", "row_max", "shifted", "prob_ready", "prob_mm", "pT_ready", "pv_mm", "inverted", "attn_scaled", "attn_added",
            "p1_mm", "p1_act", "p2_mm", "p2_logit", "p2_exp", "pick_ready", "hot_mm", "hot_ready", "hot_columns",
            "w1_copied", "w2_copied", "f1_mm", "f1_gelu", "f1_t", "f1_T_ready", "f2_mm", "f2_ready", "f2_t", "r_ready",
            "wo_mm", "ffn_added",
            "lq_mm", "slotted", "lq_min", "lq_relu", "lq_exp", "lq_ready", "kv_mm", "k_ready", "k_min", "k_exp", "kf_ready", "v2_ready", "state_mm", "state_ready",
            "y_mm", "y_ready", "y_t", "yT_ready", "out_mm", "x_ready",
            "up_mm", "up_gelu", "ff_k_mm", "ff_mm", "ff_added",
            "x_hi", "x_lo", "r_mm", "r_copied", "r_t", "r_max", "r_exp", "r_w", "r_back", "w_rows", "gate_out", "shared_added",
            "g_mm", "u_mm", "silu", "gated", "h_mul", "h_hi", "h_lo", "down_mm", "last_down", "w_hi", "w_lo",
            "moe_added", "stored",
        ):
            S[name] = sem(name)
        raw_in = [sem(f"raw_in{i}") for i in range(2)]
        mean_mm, centred, squared, var_mm, rstd_ready, normed = (
            [sem(f"{name}{t}") for t in range(HALVES)]
            for name in ("mean_mm", "centred", "squared", "var_mm", "rstd_ready", "normed"))
        patch_in = [sem(f"patch_in{k}") for k in range(KP)]
        gate_in = [sem(f"gate_in{e}") for e in range(ROUTE)]
        rtok = sb("rtok", [RT, HALVES, RC, ROUTE])
        rex = sb("rex", [RT, HALVES, RC, ROUTE])
        rw = sb("rw", [RT, HALVES, RC, ROUTE])
        rmx = sb("rmx", [RT, HALVES, RC, 8])
        rix = sb("rix", [RT, HALVES, RC, 8], U32)
        rixf = sb("rixf", [RT, HALVES, RC, 8])
        rsum = sb("rsum", [RT, HALVES, RC])
        rm2 = sb("rm2", [RT, HALVES, RC, EXP])

        def half(t):
            return slice(t * HT, (t + 1) * HT)

        def img(i):
            return slice(i * SEQ, (i + 1) * SEQ)

        def slot(i):
            return slice(i * SEQ, i * SEQ + SLOT)

        def value_block(t, b, o):
            rows, i0 = slice(64 * o, 64 * o + 64), 8 * t + 4 * b
            dst = vbd[rows, i0:i0 + 4, :, HD * o:HD * o + HD].rearrange("p i j d -> p (i j) d")
            return dst, ps[rows, 4 * t + 2 + b, :].rearrange("p (i d) -> p i d", d=HD)

        block = ctx.enter_context(nc.Block())

        @block.sync
        def _(sp):
            for k in range(KP):
                sp.dma_start(wp[:, k, :], w_proj[:, k, :]).then_inc(patch_in[k], 16)
                sp.dma_start(X[:, k, :], patches[:, k, :]).then_inc(patch_in[k], 16)
            small = CONST["alibi"][0]
            sp.dma_start(vec[:, :], cols).then_inc(S["cols_in"], 16)
            sp.dma_start(cst[:, 0:small], consts[:, 0:small]).then_inc(S["const_in"], 16)
            sp.dma_start(kqv[:, :, :], w_kqv).then_inc(S["kqv_in"], 16)
            sp.dma_start(cst[:, small:], consts[:, small:]).then_inc(S["alibi_in"], 16)
            sp.dma_start(w1a[:, :, :, :], w1x).then_inc(S["w1a_in"], 16)
            sp.dma_start(w2a[:, :, :, :], w2x).then_inc(S["w2a_in"], 16)
            sp.dma_start(wo_sb[:, :, :], wo).then_inc(S["wo_in"], 16)
            sp.wait_ge(S["score_mm"], PAIRS)
            sp.dma_start(qkv[:, :, :], qkv_w).then_inc(S["qkv_in"], 16)
            sp.dma_start(kvb[:, :], kv_b.partition_broadcast(128)).then_inc(S["kvb_in"], 16)
            sp.dma_start(wout[:, :, :], out_w).then_inc(S["wout_in"], 16)
            sp.dma_start(fw1[:, :, :], ffn_w1).then_inc(S["fw_in"], 16)
            sp.dma_start(fw2[:, :, :], ffn_w2).then_inc(S["fw_in"], 16)
            sp.wait_ge(S["w1_copied"], IMGS)
            sp.wait_ge(S["w2_copied"], IMGS)
            for e in range(BLOCKS):
                if e == SHARED + 2:
                    sp.wait_ge(S["w_rows"], HALVES)
                    sp.dma_start(gate_dram, wrows[:, :]).then_inc(S["gate_out"], 16)
                    sp.wait_ge(S["gate_out"], 16)
                    for g in (0, EXP) + tuple(range(1, EXP)):
                        sp.dma_start(gate[:, g, :], gate_dram[g, :].partition_broadcast(128)).then_inc(gate_in[g], 16)
                if e >= 2:
                    sp.wait_ge(S["w_hi"], 3 * (e - 1))
                    sp.wait_ge(S["w_lo"], 3 * (e - 1))
                sp.dma_start(guraw[:, e % 2, :], moe_gu[e]).then_inc(raw_in[e % 2], 16)
                sp.dma_start(dnraw[:, e % 2, 0:2 * EMB], moe_down[e, :, 0:2 * EMB]).then_inc(raw_in[e % 2], 16)
                sp.dma_start(dnraw[0:96, e % 2, 2 * EMB:], moe_down[e, 0:96, 2 * EMB:]).then_inc(raw_in[e % 2], 16)
            for c in range(CH):
                sp.wait_ge(S["moe_added"], c + 1)
                sp.dma_start(out[:, c, :], xs[:, c, :]).then_inc(S["stored"], 16)
            sp.wait_ge(S["stored"], 16 * CH)

        @block.gpsimd
        def _(pool):
            pool.dma_start(wp1_sb[:, :, :], wp1).then_inc(S["wp1_in"], 16)
            pool.dma_start(wp2_sb[:, :], wp2).then_inc(S["wp2_in"], 16)
            for part in range(PARTS):
                rows = slice(EXP * part, EXP * part + EXP)
                pool.dma_start(bias_raw[rows, 0:FFN], b1x).then_inc(S["bias_in"], 16)
                pool.dma_start(bias_raw[rows, FFN:], b2x).then_inc(S["bias_in"], 16)
            pool.dma_start(route_sb[:, :, :], route_w).then_inc(S["route_in"], 16)
            pool.memset(eps[:, :], EPS).then_inc(S["pool_setup"], 1)
            pool.memset(xn[:, :, TOK:], 0.0).then_inc(S["pool_setup"], 1)
            pool.memset(q[:, :, TOK:], 0.0).then_inc(S["pool_setup"], 1)
            pool.wait_ge(S["tok_mm"], HALVES)
            pool.memset(vbd[:, :, :, :], 0.0).then_inc(S["pool_setup"], 1)
            pool.memset(prob[:, :, :, :], 0.0).then_inc(S["pool_setup"], 1)
            steps = 0
            pool.wait_ge(S["bias_in"], 2 * 16 * PARTS)
            pool.wait_ge(S["const_in"], 16)
            for part in range(PARTS - 1):
                later = cst[0:PARTS * EXP, CONST["later"][0] + part:CONST["later"][0] + part + 1]
                for step in range(3):
                    if step == 0:
                        ins = pool.tensor_copy(bias_parts[:, :], bias_raw)
                    elif step == 1:
                        ins = pool.tensor_scalar(bias_off, bias_parts[:, :], later, None, ALU.mult)
                    else:
                        ins = pool.tensor_tensor(bias_raw, bias_raw, bias_off, ALU.add)
                    ins.then_inc(S["bias_step"], 1)
                    steps += 1
                    pool.wait_ge(S["bias_step"], steps)
            pool.tensor_copy(bias_parts[:, :], bias_raw).then_inc(S["bias_ready"], 1)
            for p in range(PAIRS + 3):
                if p < PAIRS:
                    pool.wait_ge(S["row_max"], p + 1)
                    s = sc[:, p % 2, :].rearrange("p (h k) -> p h k", k=SEQ)
                    pool.tensor_tensor(s, s, top[:, p % 2, :].unsqueeze(2).to_broadcast([128, HEADS, SEQ]),
                                       ALU.subtract).then_inc(S["shifted"], 1)
                if p >= 3:
                    d = p - 3
                    toks = slice(2 * d * SEQ, 2 * (d + 1) * SEQ)
                    pool.wait_ge(S["inverted"], d + 1)
                    pool.tensor_tensor(attn[:, d % 2, :, :], attn[:, d % 2, :, :], rsums[:, d % 2, :, :],
                                       ALU.mult).then_inc(S["attn_scaled"], 1)
                    pool.wait_ge(S["attn_scaled"], d + 1)
                    pool.tensor_tensor(h[:, :, toks], h[:, :, toks], attn[:, d % 2, :, :], ALU.add)\
                        .then_inc(S["attn_added"], 1)
            pool.wait_ge(S["f1_mm"], PAIRS)
            pool.wait_ge(S["f2_mm"], PAIRS)
            pool.memset(vx[:, :, :, 128:], 1.0).then_inc(S["pool_setup"], 1)
            pool.memset(xp[:, :, :], 0.0).then_inc(S["pool_setup"], 1)
            for n in range(STEPS * SHARED, STEPS * BLOCKS):
                e, t, m = moe_step(n)
                rows = MCH[m][1]
                if n % STEPS == 0:
                    pool.wait_ge(gate_in[e - SHARED], 16)
                pool.wait_ge(S["silu"], n + 1)
                pool.wait_ge(S["h_mul"], n - 1)
                pool.tensor_tensor(sil[0:rows, 1, n % 2, :], sil[0:rows, 0, n % 2, :],
                                   gate[0:rows, e - SHARED, half(t)], ALU.mult).then_inc(S["gated"], 1)

        @block.scalar
        def _(act):
            steps = [0]

            def link(ins):
                steps[0] += 1
                ins.then_inc(S["act_step"], 1)
                act.wait_ge(S["act_step"], steps[0])

            def square(k, t):
                act.wait_ge(centred[t], k + 1)
                act.activation(sq[:, :, half(t)], xc[:, :, half(t)], ACT.Square).then_inc(squared[t], 1)

            def inverse_root(k, t):
                act.wait_ge(var_mm[t], k + 1)
                link(act.activation(rstd[:, half(t)], ps[:, NORM_BANK[k][t], 0:HT], ACT.Ln, bias=eps[:, :]))
                act.activation(rstd[:, half(t)], rstd[:, half(t)], ACT.Exp, scale=-0.5).then_inc(rstd_ready[t], 1)

            act.preload_act_table_set("natural_log_exp_and_others")
            act.wait_ge(S["pool_setup"], 3)
            for t in range(HALVES):
                square(0, t)
            for t in range(HALVES):
                inverse_root(0, t)
            act.wait_ge(S["const_in"], 16)
            for t in range(HALVES):
                act.wait_ge(S["qk_mm"], 2 * t + 1)
                act.activation(q[:, :, half(t)], ps[:, 4 * t + 2:4 * t + 4, 0:HT], ACT.Copy,
                               scale=float(EMB) ** -0.5).then_inc(S["q_ready"], 1)
                act.wait_ge(S["qk_mm"], 2 * t + 2)
                for g in range(CHH):
                    last = act.activation(kx[:, t, 1, g, :], ps[:, 4 * t + 1, 0:HT], ACT.Copy,
                                          scale=const("head")[:, g:g + 1])
                last.then_inc(S["kx_act"], 1)
            act.wait_ge(S["pool_setup"], 5)
            for t in range(HALVES):
                act.wait_ge(S["v_mm"], t + 1)
                for o in range(2):
                    dst, src = value_block(t, 0, o)
                    last = act.activation(dst, src, ACT.Copy)
                last.then_inc(S["v_act"], 1)
            def turned_probs(p):
                act.wait_ge(S["prob_mm"], p + 1)
                if p >= 2:
                    act.wait_ge(S["pv_mm"], p - 1)
                src = ps[:, 4:6, :].rearrange("p b (j i s) -> p (b j) i s", j=4, i=2)
                for i in range(2):
                    last = act.activation(pT[:, p % 2, :, i, :], src[:, :, i, 0:SEQ], ACT.Copy)
                last.then_inc(S["pT_ready"], 1)

            for p in range(PAIRS + 2):
                if p >= 2:
                    turned_probs(p - 2)
                if p < PAIRS:
                    act.wait_ge(S["shifted"], p + 1)
                    if p >= 2:
                        act.wait_ge(S["prob_mm"], p - 1)
                    act.activation(prob[:, p % 2, :, 0:SEQ], sc[:, p % 2, :].rearrange("p (h k) -> p h k", k=SEQ),
                                   ACT.Exp).then_inc(S["prob_ready"], 1)
                if p == PAIRS:
                    square(1, 0)
            inverse_root(1, 0)

            def predictor_gelu(t):
                act.wait_ge(S["p1_mm"], t + 1)
                act.activation(act8[:, t, :], ps[:, NORM_BANK[1][t], 0:8], ACT.Gelu, bias=col("bp1"))\
                   .then_inc(S["p1_act"], 1)

            def predictor_exp(t):
                act.wait_ge(S["p2_logit"], t + 1)
                act.activation(ex8[:, t, :], lg[:, t, :], ACT.Exp, bias=nmx[:, t:t + 1],
                               accum_out=sm8[:, t:t + 1]).then_inc(S["p2_exp"], 1)

            def one_hot_columns(t):
                act.wait_ge(S["hot_mm"], t + 1)
                act.activation(hotT[:, 8 * t:8 * t + 8, :], ps[0:PARTS * EXP, NORM_BANK[1][t], 64:72].unsqueeze(2)
                               .to_broadcast([PARTS * EXP, 8, SLOT]), ACT.Copy).then_inc(S["hot_columns"], 1)

            act.preload_act_table_set("gelu_and_others")
            predictor_gelu(0)
            act.preload_act_table_set("natural_log_exp_and_others")
            predictor_exp(0)
            square(1, 1)
            one_hot_columns(0)
            inverse_root(1, 1)
            act.preload_act_table_set("gelu_and_others")
            def second_matrix(p):
                act.wait_ge(S["pick_ready"], p // HPAIRS + 1)
                if p >= 2:
                    act.wait_ge(S["f2_mm"], p - 1)
                for i in range(2):
                    r = (2 * p + i) % 8
                    e = act.value_load(pick[r:r + 1, p // HPAIRS, 0:1], min_val=0, max_val=EXP - 1)
                    act.activation(w2s[:, p % 2, i, :, :], w2a[:, bass.ds(e, 1), :, :], ACT.Copy)\
                       .then_inc(S["w2_copied"], 1)

            act.wait_ge(S["w2a_in"], 16)
            for p in range(PAIRS + 3):
                if p >= 3:
                    act.wait_ge(S["f2_mm"], p - 2)
                    if p >= 5:
                        act.wait_ge(S["f2_t"], p - 4)
                    act.activation(rr[:, (p - 3) % 2, :], ps[:, 4, 0:EMB], ACT.Copy).then_inc(S["f2_ready"], 1)
                if p < PAIRS:
                    act.wait_ge(S["f1_mm"], p + 1)
                    if p >= 2:
                        act.wait_ge(S["f1_t"], p - 1)
                    act.activation(hg[:, p % 2, :], ps[:, p % 2, :], ACT.Gelu).then_inc(S["f1_gelu"], 1)
                if p == 1:
                    predictor_gelu(1)
                if 1 <= p <= PAIRS:
                    second_matrix(p - 1)
                if p == 2:
                    act.preload_act_table_set("natural_log_exp_and_others")
                    predictor_exp(1)
                    act.preload_act_table_set("gelu_and_others")
                if p == 3:
                    one_hot_columns(1)
                if p == PAIRS - 1:
                    act.preload_act_table_set("natural_log_exp_and_others")
                if p == PAIRS:
                    square(2, 0)
            inverse_root(2, 0)
            square(3, 0)
            inverse_root(3, 0)
            square(2, 1)

            def query_parts(t):
                act.wait_ge(S["lq_min"], t + 1)
                for c in range(CH):
                    last = act.activation(q[:, c, half(t)], ps[:, QUERY_BANK[t] + c, 0:HT], ACT.Relu, bias=col("bq", c))
                last.then_inc(S["lq_relu"], 1)
                act.activation(xs[:, :, half(t)], xs[:, :, half(t)], ACT.Exp).then_inc(S["lq_exp"], 1)

            query_parts(0)
            for p in range(PAIRS + 3):
                if p < PAIRS:
                    act.wait_ge(S["k_min"], p + 1)
                    act.activation(ke[:, p % 2, 0:EMB], ke[:, p % 2, 0:EMB], ACT.Exp).then_inc(S["k_exp"], 1)
                if p == 0:
                    inverse_root(2, 1)
                if p == 1:
                    square(3, 1)
                if p == 2:
                    inverse_root(3, 1)
                if p == PAIRS:
                    square(4, 0)
                if p == PAIRS + 2:
                    inverse_root(4, 0)
                    act.preload_act_table_set("gelu_and_others")
                if p >= 3:
                    act.wait_ge(S["y_t"], p - 2)
                    src = ps[:, 5, 0:2 * 128].rearrange("p (c i s) -> p c i s", c=CH, i=2)
                    dst = yT[:, :, 2 * (p - 3) * SEQ:2 * (p - 2) * SEQ].rearrange("p c (i s) -> p c i s", i=2)
                    for c in range(CH):
                        last = act.activation(dst[:, c], src[:, c, :, 0:SEQ], ACT.Copy)
                    last.then_inc(S["yT_ready"], 1)
                if p == 3:
                    query_parts(1)

            def split_weights(e, part):
                if part == 0:
                    act.wait_ge(raw_in[e % 2], 48 * (e // 2 + 1))
                    if e >= 2:
                        act.wait_ge(S["u_mm"], STEPS * (e - 1))
                if part == 1 and e >= 2:
                    act.wait_ge(S["down_mm"], e - 1)
                rows = 96 if part == 2 else 128
                hi, raw = ((guhi[:, e % 2, :], guraw[:, e % 2, :]),
                           (dnhi[:, e % 2, 0:2 * EMB], dnraw[:, e % 2, 0:2 * EMB]),
                           (dnhi[0:96, e % 2, 2 * EMB:], dnraw[0:96, e % 2, 2 * EMB:]))[part]
                act.activation(hi, raw, ACT.Copy).then_inc(S["w_hi"], 1)

            for s in range(HALVES * DC):
                t, m = s // DC, s % DC
                act.wait_ge(S["up_mm"], s + 1)
                if t == 1:
                    act.wait_ge(S["ff_k_mm"], s - DC + 1)
                act.activation(hid[:, m, :], ps[:, 2 - 2 * t + m % 2, 0:HT], ACT.Gelu,
                               bias=col("b1", m)).then_inc(S["up_gelu"], 1)
                if s == 2:
                    square(4, 1)
                if s == 4:
                    act.preload_act_table_set("natural_log_exp_and_others")
                    inverse_root(4, 1)
                    act.preload_act_table_set("gelu_and_others")
                if 5 <= s <= 7:
                    split_weights(0, s - 5)
                if s == DC + 4:
                    square(5, 0)
                if s == DC + 5:
                    act.preload_act_table_set("natural_log_exp_and_others")
                    inverse_root(5, 0)
                    act.preload_act_table_set("gelu_and_others")
            act.preload_act_table_set("silu_and_others")

            def copy_logits(t):
                act.wait_ge(S["r_mm"], t + 1)
                act.activation(rlog[:, half(t)], ps[0:ROUTE, 6 + t, 0:HT], ACT.Copy).then_inc(S["r_copied"], 1)


            def high_part(n):
                e, t, m = moe_step(n)
                rows = MCH[m][1]
                act.wait_ge(S["h_mul"], n + 1)
                if e >= 2 and m == 0 and t == 0:
                    act.wait_ge(S["down_mm"], e - 1)
                act.activation(hhi[0:rows, e % 2, m, half(t)], prod[0:rows, n % 2, :], ACT.Copy)\
                   .then_inc(S["h_hi"], 1)

            for n in range(STEPS * BLOCKS):
                e, t, m = moe_step(n)
                rows = MCH[m][1]
                act.wait_ge(S["g_mm"], n + 1)
                if 2 <= n < STEPS * SHARED + 2:
                    act.wait_ge(S["h_mul"], n - 1)
                if n >= STEPS * SHARED + 2:
                    act.wait_ge(S["gated"], n - STEPS * SHARED - 1)
                act.activation(sil[0:rows, 0, n % 2, :], ps[0:rows, 2 * (n % 2), 0:HT], ACT.Silu)\
                   .then_inc(S["silu"], 1)
                if n >= 1:
                    high_part(n - 1)
                if n == 0:
                    square(5, 1)
                if n == 1:
                    act.preload_act_table_set("natural_log_exp_and_others")
                    inverse_root(5, 1)
                    act.preload_act_table_set("silu_and_others")
                    copy_logits(0)
                if n == 3:
                    copy_logits(1)
                if n == 5:
                    act.preload_act_table_set("natural_log_exp_and_others")
                    act.wait_ge(S["r_max"], 1)
                    act.activation(rex[:, :, :, :], rtok[:, :, :, :], ACT.Exp).then_inc(S["r_exp"], 1)
                    act.preload_act_table_set("silu_and_others")
                if n == 8:
                    for u in range(HALVES):
                        act.wait_ge(S["r_back"], u + 1)
                        act.activation(wrows[:, half(u)], ps[0:ROUTE, 6 + u, 0:HT], ACT.Copy).then_inc(S["w_rows"], 1)
                if e + 1 < BLOCKS and n % STEPS in SPLIT_AT:
                    split_weights(e + 1, SPLIT_AT.index(n % STEPS))
            high_part(STEPS * BLOCKS - 1)

        @block.vector
        def _(dve):
            steps = [0]

            def link(ins):
                steps[0] += 1
                ins.then_inc(S["dve_step"], 1)
                dve.wait_ge(S["dve_step"], steps[0])

            def centre(k, t, src):
                dve.wait_ge(mean_mm[t], k + 1)
                mean = ps[:, NORM_BANK[k][t], 0:HT].unsqueeze(1).to_broadcast([128, CH, HT])
                dve.tensor_tensor(xc[:, :, half(t)], src[:, :, half(t)], mean, ALU.subtract).then_inc(centred[t], 1)

            def scale(k, t, out_ap, gain=None):
                dve.wait_ge(rstd_ready[t], k + 1)
                by = rstd[:, half(t)].unsqueeze(1).to_broadcast([128, CH, HT])
                dve.wait_ge(centred[t], k + 1)
                if gain is None:
                    dve.tensor_tensor(out_ap[:, :, half(t)], xc[:, :, half(t)], by, ALU.mult).then_inc(normed[t], 1)
                else:
                    g, b = gain
                    link(dve.tensor_tensor(out_ap[:, :, half(t)], xc[:, :, half(t)], by, ALU.mult))
                    for c in range(CH):
                        last = dve.tensor_scalar(out_ap[:, c, half(t)], out_ap[:, c, half(t)], col(g, c), col(b, c),
                                                 ALU.mult, ALU.add)
                    last.then_inc(normed[t], 1)

            def split_tokens(t):
                dve.wait_ge(normed[t], 6)
                dve.tensor_copy(xhi[:, :, half(t)], xn[:, :, half(t)]).then_inc(S["x_hi"], 1)
                dve.wait_ge(S["x_hi"], t + 1)
                dve.tensor_tensor(xlo[:, :, half(t)], xn[:, :, half(t)], xhi[:, :, half(t)].bitcast(F32),
                                  ALU.subtract).then_inc(S["x_lo"], 1)

            dve.wait_ge(S["cols_in"], 16)
            dve.wait_ge(S["const_in"], 16)
            dve.tensor_scalar(bo3[:, :], col("bo", 0, CH), 0.3, None, ALU.mult).then_inc(S["setup"], 1)
            for t in range(HALVES):
                dve.wait_ge(S["tok_mm"], t + 1)
                for c in range(CH):
                    pos = col("pos", c * SEQ, SEQ).unsqueeze(1).to_broadcast([128, HT // SEQ, SEQ])
                    dve.scalar_tensor_tensor(
                        out=h[:, c, half(t)].rearrange("p (i s) -> p i s", s=SEQ),
                        in0=ps[:, 4 * t + 2 + c, 0:HT].rearrange("p (i s) -> p i s", s=SEQ),
                        scalar=col("b_proj", c), in1=pos, op0=ALU.add, op1=ALU.add).then_inc(S["h_ready"], 1)
            for t in range(HALVES):
                dve.wait_ge(S["h_ready"], CH * (t + 1))
                centre(0, t, h)
            for t in range(HALVES):
                scale(0, t, xn)
            for t in range(HALVES):
                dve.wait_ge(S["qk_mm"], 2 * t + 2)
                link(dve.tensor_copy(sq[:, 0, half(t)], ps[:, 4 * t, 0:HT]))
                for g in range(CHH):
                    last = dve.tensor_scalar(kx[:, t, 0, g, :], sq[:, 0, half(t)], const("head")[:, g:g + 1], None,
                                             ALU.mult)
                last.then_inc(S["kx_dve"], 1)
            dve.wait_ge(S["pool_setup"], 5)
            for t in range(HALVES):
                dve.wait_ge(S["v_mm"], t + 1)
                for o in range(2):
                    dst, src = value_block(t, 1, o)
                    last = dve.tensor_copy(dst, src)
                last.then_inc(S["v_dve"], 1)
            def scores_max(p):
                dve.wait_ge(S["score_mm"], p + 1)
                if p >= 2:
                    dve.wait_ge(S["prob_ready"], p - 1)
                b0 = 2 * (p % 2)
                link(dve.tensor_tensor(sc[:, p % 2, :].rearrange("p (b n) -> p b n", b=2), ps[:, b0:b0 + 2, 0:CHH * SEQ],
                                       const("alibi").rearrange("p (b n) -> p b n", b=2), ALU.add))
                dve.tensor_reduce(top[:, p % 2, :], sc[:, p % 2, :].rearrange("p (h k) -> p h k", k=SEQ), AX.X,
                                  ALU.max).then_inc(S["row_max"], 1)

            def invert_sums(p):
                dve.wait_ge(S["pv_mm"], p + 1)
                if p >= 2:
                    dve.wait_ge(S["attn_added"], p - 1)
                bank = ps[:, 6, 0:2 * CH * 2 * SEQ].rearrange("p (o c n) -> p o c n", o=2, c=CH)
                dve.tensor_copy(attn[:, p % 2, :, :], bank[:, 0])
                dve.reciprocal(rsums[:, p % 2, :, :], bank[:, 1]).then_inc(S["inverted"], 1)

            dve.wait_ge(S["pool_setup"], 5)
            dve.wait_ge(S["alibi_in"], 16)
            for p in range(PAIRS + 3):
                if p < PAIRS:
                    scores_max(p)
                if p == PAIRS:
                    centre(1, 0, h)
                if p == PAIRS + 2:
                    scale(1, 0, xn)
                if p >= 3:
                    invert_sums(p - 3)

            def predictor_logits(t):
                dve.wait_ge(S["p2_mm"], t + 1)
                link(dve.tensor_tensor(lg[:, t, :], ps[0:8, NORM_BANK[1][t], 32:40], col("bp2", 0, EXP)[0:8], ALU.add))
                link(dve.max(mx8[:, t, :], lg[:, t, :]))
                dve.tensor_scalar(nmx[:, t:t + 1], mx8[:, t, 0:1], -1.0, None, ALU.mult).then_inc(S["p2_logit"], 1)

            def predictor_pick(t):
                dve.wait_ge(S["p2_exp"], t + 1)
                link(dve.reciprocal(rs8[:, t:t + 1], sm8[:, t:t + 1]))
                link(dve.tensor_scalar(pr8[:, t, :], ex8[:, t, :], rs8[:, t:t + 1], None, ALU.mult))
                link(dve.max(mx8[:, t, :], pr8[:, t, :]))
                dve.max_index(pick[:, t, :], mx8[:, t, :], pr8[:, t, :]).then_inc(S["pick_ready"], 1)
                dve.wait_ge(S["pick_ready"], t + 1)
                link(dve.tensor_copy(pickf[:, t:t + 1], pick[:, t, 0:1]))
                dve.tensor_scalar(hot[:, t, :], const("iota")[0:8, :], pickf[:, t:t + 1], None, ALU.is_equal)\
                   .then_inc(S["hot_ready"], 1)

            def residual(t):
                if t == 0:
                    dve.wait_ge(S["setup"], 1)
                for c in range(CH):
                    last = dve.scalar_tensor_tensor(out=xs[:, c, half(t)], in0=xn[:, c, half(t)],
                                                    scalar=bo3[:, c:c + 1], in1=h[:, c, half(t)], op0=ALU.add,
                                                    op1=ALU.add)
                link(last)

            def add_ffn(t):
                dve.wait_ge(S["wo_mm"], t + 1)
                b = OUT_BANK[t]
                dve.scalar_tensor_tensor(out=h[:, :, half(t)], in0=ps[:, b:b + 2, 0:HT], scalar=0.3,
                                         in1=xs[:, :, half(t)], op0=ALU.mult, op1=ALU.add)\
                   .then_inc(S["ffn_added"], 1)

            predictor_logits(0)
            predictor_pick(0)
            dve.wait_ge(S["w1a_in"], 16)
            def first_matrix(p):
                dve.wait_ge(S["pick_ready"], p // HPAIRS + 1)
                if p == 0:
                    dve.wait_ge(S["pv_mm"], PAIRS)
                if p >= 2:
                    dve.wait_ge(S["f1_mm"], p - 1)
                for i in range(2):
                    r = (2 * p + i) % 8
                    e = dve.value_load(pick[r:r + 1, p // HPAIRS, 0:1], min_val=0, max_val=EXP - 1)
                    dve.tensor_copy(w1s[:, p % 2, i, :, :], w1a[:, bass.ds(e, 1), :, :]).then_inc(S["w1_copied"], 1)

            first_matrix(0)
            centre(1, 1, h)
            for p in range(PAIRS + 4):
                if p == 3:
                    predictor_pick(1)
                if p + 1 < PAIRS:
                    first_matrix(p + 1)
                if p == 0:
                    scale(1, 1, xn)
                if p >= 4:
                    dve.wait_ge(S["f2_t"], p - 3)
                    src = ps[:, 5, 0:2 * 128].rearrange("p (c i s) -> p c i s", c=CH, i=2)
                    dst = rT[:, :, 2 * (p - 4) * SEQ:2 * (p - 3) * SEQ].rearrange("p c (i s) -> p c i s", i=2)
                    for c in range(CH):
                        last = dve.tensor_copy(dst[:, c], src[:, c, :, 0:SEQ])
                    last.then_inc(S["r_ready"], 1)
                if 1 <= p <= PAIRS:
                    dve.wait_ge(S["f1_t"], p)
                    if p >= 3:
                        dve.wait_ge(S["f2_mm"], p - 2)
                    dve.tensor_copy(hgT[:, (p - 1) % 2, :, :],
                                    ps[:, 2 + (p - 1) % 2, :].rearrange("p (k n) -> p k n", k=FC))\
                       .then_inc(S["f1_T_ready"], 1)
                if p == 2:
                    predictor_logits(1)
                if 3 <= p < 3 + HALVES:
                    residual(p - 3)
                if p == PAIRS - 1:
                    add_ffn(0)
                if p == PAIRS:
                    centre(2, 0, h)
                if p == PAIRS + 2:
                    scale(2, 0, rT)
            centre(3, 0, rT)
            add_ffn(1)

            def slots(t):
                dve.wait_ge(normed[t], 4)
                dve.wait_ge(S["pool_setup"], 7)
                for c in range(CH):
                    last = dve.tensor_copy(
                        xp[:, c, 8 * SLOT * t:8 * SLOT * (t + 1)].rearrange("p (i s) -> p i s", s=SLOT)[:, :, 0:SEQ],
                        xn[:, c, half(t)].rearrange("p (i s) -> p i s", s=SEQ))
                last.then_inc(S["slotted"], 1)

            def query_min(t):
                dve.wait_ge(S["lq_mm"], t + 1)
                for c in range(CH):
                    last = dve.tensor_scalar(xs[:, c, half(t)], ps[:, QUERY_BANK[t] + c, 0:HT], col("bq", c), 0.0,
                                             ALU.add, ALU.min)
                last.then_inc(S["lq_min"], 1)

            def query_sum(t):
                dve.wait_ge(S["lq_exp"], t + 1)
                dve.wait_ge(S["lq_relu"], t + 1)
                dve.tensor_tensor(q[:, :, half(t)], q[:, :, half(t)], xs[:, :, half(t)], ALU.add)\
                   .then_inc(S["lq_ready"], 1)
                dve.wait_ge(S["lq_ready"], t + 1)
                for c in range(CH):
                    last = dve.tensor_scalar(xs[:, c, half(t)], rT[:, c, half(t)], col("out_b", c), None, ALU.add)
                link(last)

            scale(3, 0, xn, ("g1", "be1"))
            slots(0)
            centre(2, 1, h)
            query_min(0)
            query_sum(0)

            def keys(p):
                dve.wait_ge(S["kv_mm"], p + 1)
                if p == 0:
                    dve.wait_ge(S["kvb_in"], 16)
                if p >= 2:
                    dve.wait_ge(S["state_mm"], p - 1)
                kv = ps[:, p % 2, :]
                dve.tensor_tensor(kf[:, p % 2, 0:EMB], kv[:, 0:EMB], kvb[:, 0:EMB], ALU.add).then_inc(S["k_ready"], 1)
                dve.tensor_tensor(vx[:, p % 2, :, 0:128], kv[:, EMB:].rearrange("p (c n) -> p c n", c=CH),
                                  kvb[:, EMB:].rearrange("p (c n) -> p c n", c=CH), ALU.add).then_inc(S["v2_ready"], 1)
                dve.wait_ge(S["k_ready"], p + 1)
                dve.tensor_scalar(ke[:, p % 2, 0:EMB], kf[:, p % 2, 0:EMB], 0.0, None, ALU.min).then_inc(S["k_min"], 1)

            def keys_b(p):
                dve.wait_ge(S["k_exp"], p + 1)
                dve.scalar_tensor_tensor(out=kf[:, p % 2, 0:EMB], in0=kf[:, p % 2, 0:EMB], scalar=0.0,
                                         in1=ke[:, p % 2, 0:EMB], op0=ALU.max, op1=ALU.add).then_inc(S["kf_ready"], 1)

            def state(p):
                dve.wait_ge(S["state_mm"], p + 1)
                if p >= 2:
                    dve.wait_ge(S["y_mm"], p - 1)
                for i in range(2):
                    last = dve.tensor_tensor(kvm[:, p % 2, i, :, :],
                                             ps[:, 2 + i, 0:CH * (128 + CHH)].rearrange("p (c n) -> p c n", c=CH),
                                             const("block").unsqueeze(1).to_broadcast([128, CH, 128 + CHH]), ALU.mult)
                last.then_inc(S["state_ready"], 1)

            def divide(p):
                dve.wait_ge(S["y_mm"], p + 1)
                y = ps[:, 4, 0:CH * (128 + CHH)].rearrange("p (c n) -> p c n", c=CH)
                link(dve.tensor_scalar(dinv[:, p % 2, :, :], y[:, :, 128:], DEN_EPS, None, ALU.max))
                link(dve.reciprocal(dinv[:, p % 2, :, :], dinv[:, p % 2, :, :]))
                if p >= 2:
                    dve.wait_ge(S["y_t"], p - 1)
                for c in range(CH):
                    last = dve.tensor_tensor(yt[:, p % 2, 128 * c:128 * c + 128].rearrange("p (g d) -> p g d", d=HD),
                                             y[:, c, 0:128].rearrange("p (g d) -> p g d", d=HD),
                                             dinv[:, p % 2, c, :].unsqueeze(2).to_broadcast([128, CHH, HD]), ALU.mult)
                last.then_inc(S["y_ready"], 1)

            def add_linear(t):
                dve.wait_ge(S["out_mm"], t + 1)
                b = OUT_BANK[t]
                dve.tensor_tensor(xs[:, :, half(t)], xs[:, :, half(t)], ps[:, b:b + 2, 0:HT], ALU.add)\
                   .then_inc(S["x_ready"], 1)
                dve.wait_ge(S["x_ready"], t + 1)

            def ffn_residual(t):
                for c in range(CH):
                    last = dve.scalar_tensor_tensor(out=h[:, c, half(t)], in0=xs[:, c, half(t)], scalar=col("b2", c),
                                                    in1=h[:, c, half(t)], op0=ALU.add, op1=ALU.add)
                link(last)

            for p in range(PAIRS + 2):
                if p < PAIRS:
                    keys(p)
                if p >= 2:
                    divide(p - 2)
                if p < PAIRS:
                    keys_b(p)
                if 1 <= p <= PAIRS:
                    state(p - 1)
                if p == 0:
                    scale(2, 1, rT)
                if p == 1:
                    dve.wait_ge(normed[1], 3)
                    centre(3, 1, rT)
                if p == 2:
                    scale(3, 1, xn, ("g1", "be1"))
                    slots(1)
                if p == 3:
                    query_min(1)
                if p == 4:
                    query_sum(1)
                if p == PAIRS - 1:
                    add_linear(0)
                if p == PAIRS:
                    centre(4, 0, xs)
            scale(4, 0, xn, ("g2", "be2"))
            add_linear(1)
            centre(4, 1, xs)
            ffn_residual(0)
            scale(4, 1, xn, ("g2", "be2"))
            ffn_residual(1)

            def split_weights(e, part):
                if e >= 2 and part == 0:
                    dve.wait_ge(S["u_mm"], STEPS * (e - 1))
                if e >= 2 and part == 1:
                    dve.wait_ge(S["down_mm"], e - 1)
                lo, hi, raw = (
                    (gulo[:, e % 2, :], guhi[:, e % 2, :], guraw[:, e % 2, :]),
                    (dnlo[:, e % 2, 0:2 * EMB], dnhi[:, e % 2, 0:2 * EMB], dnraw[:, e % 2, 0:2 * EMB]),
                    (dnlo[0:96, e % 2, 2 * EMB:], dnhi[0:96, e % 2, 2 * EMB:], dnraw[0:96, e % 2, 2 * EMB:]))[part]
                dve.wait_ge(S["w_hi"], 3 * e + part + 1)
                dve.tensor_tensor(lo, raw, hi.bitcast(F32), ALU.subtract).then_inc(S["w_lo"], 1)

            for part in range(3):
                split_weights(0, part)
            def add_ff(t):
                dve.wait_ge(S["ff_mm"], t + 1)
                dve.tensor_tensor(h[:, :, half(t)], h[:, :, half(t)], ps[:, 4 + 2 * t:6 + 2 * t, 0:HT], ALU.add)\
                   .then_inc(S["ff_added"], 1)
                dve.wait_ge(S["ff_added"], t + 1)

            add_ff(0)
            centre(5, 0, h)
            scale(5, 0, xn)
            split_tokens(0)
            add_ff(1)

            def router_max():
                src = ps[0:RT, 4, 0:HALVES * RC * ROUTE].rearrange("p (t c e) -> p t c e", t=HALVES, c=RC)
                dve.wait_ge(S["r_t"], 1)
                link(dve.tensor_reduce(rsum[:, :, :], src[:, :, :, 0:EXP], AX.X, ALU.max))
                link(dve.tensor_tensor(rtok[:, :, :, 0:EXP], src[:, :, :, 0:EXP],
                                       rsum[:, :, :].unsqueeze(3).to_broadcast([RT, HALVES, RC, EXP]), ALU.subtract))
                dve.tensor_scalar(rtok[:, :, :, EXP:], src[:, :, :, EXP:], -1.0, None, ALU.mult)\
                   .then_inc(S["r_max"], 1)

            def router_probs():
                dve.wait_ge(S["r_exp"], 1)
                link(dve.tensor_reduce(rsum[:, :, :], rex[:, :, :, 0:EXP], AX.X, ALU.add))
                link(dve.reciprocal(rsum[:, :, :], rsum[:, :, :]))
                link(dve.tensor_tensor(rex[:, :, :, 0:EXP], rex[:, :, :, 0:EXP],
                                       rsum[:, :, :].unsqueeze(3).to_broadcast([RT, HALVES, RC, EXP]), ALU.mult))
                link(dve.tensor_scalar(rw[:, :, :, EXP:], rex[:, :, :, EXP:], 1.0, None, ALU.add))
                link(dve.reciprocal(rw[:, :, :, EXP:], rw[:, :, :, EXP:]))

            def router_top():
                cells = [(t, c) for t in range(HALVES) for c in range(RC)]
                for t, c in cells:
                    last = dve.max(rmx[:, t, c, :], rex[:, t, c, 0:EXP])
                link(last)
                for t, c in cells:
                    last = dve.max_index(rix[:, t, c, :], rmx[:, t, c, :], rex[:, t, c, 0:EXP])
                link(last)
                link(dve.tensor_copy(rixf[:, :, :, :], rix[:, :, :, :]))

            def router_weights():
                full = [RT, HALVES, RC, EXP]
                iota = const("iota")[0:RT, 0:EXP].unsqueeze(1).unsqueeze(1).to_broadcast(full)
                link(dve.tensor_tensor(rm2[:, :, :, :], iota, rixf[:, :, :, 1:2].to_broadcast(full), ALU.is_equal))
                link(dve.tensor_tensor(rw[:, :, :, 0:EXP], iota, rixf[:, :, :, 0:1].to_broadcast(full), ALU.is_equal))
                link(dve.tensor_tensor(rm2[:, :, :, :], rm2[:, :, :, :], rw[:, :, :, 0:EXP], ALU.add))
                dve.tensor_tensor(rw[:, :, :, 0:EXP], rm2[:, :, :, :], rex[:, :, :, 0:EXP], ALU.mult)\
                   .then_inc(S["r_w"], 1)

            def add_shared():
                dve.wait_ge(S["down_mm"], SHARED)
                dve.wait_ge(gate_in[EXP], 16)
                for t in range(HALVES):
                    rows = ps[:, 4 + t:8:2, 0:HT]
                    link(dve.tensor_tensor(xs[:, :, half(t)], rows, gate[:, EXP, half(t)].unsqueeze(1).to_broadcast(
                        [128, CH, HT]), ALU.mult))
                    last = dve.tensor_tensor(h[:, :, half(t)], h[:, :, half(t)], xs[:, :, half(t)], ALU.add)
                last.then_inc(S["shared_added"], 1)

            def low_part(n):
                e, t, m = moe_step(n)
                rows = MCH[m][1]
                dve.wait_ge(S["h_hi"], n + 1)
                dve.tensor_tensor(hlo[0:rows, e % 2, m, half(t)], prod[0:rows, n % 2, :],
                                  hhi[0:rows, e % 2, m, half(t)].bitcast(F32), ALU.subtract)\
                   .then_inc(S["h_lo"], 1)

            def second_half_centre():
                centre(5, 1, h)

            def second_half_scale():
                scale(5, 1, xn)
                split_tokens(1)

            between = {0: second_half_centre, 1: second_half_scale, 4: router_max, 5: router_probs, 6: router_top,
                       7: router_weights, STEPS * SHARED + 4: add_shared}
            for n in range(STEPS * BLOCKS):
                e, t, m = moe_step(n)
                rows = MCH[m][1]
                if e < SHARED:
                    dve.wait_ge(S["silu"], n + 1)
                else:
                    dve.wait_ge(S["gated"], n - STEPS * SHARED + 1)
                dve.wait_ge(S["u_mm"], n + 1)
                if n >= 2:
                    dve.wait_ge(S["h_hi"], n - 1)
                    dve.wait_ge(S["h_lo"], n - 1)
                dve.tensor_tensor(prod[0:rows, n % 2, :], sil[0:rows, 0 if e < SHARED else 1, n % 2, :],
                                  ps[0:rows, 1 + 2 * (n % 2), 0:HT], ALU.mult).then_inc(S["h_mul"], 1)
                if n >= 1:
                    low_part(n - 1)
                if n in between:
                    between[n]()
                if e + 1 < BLOCKS and n % STEPS in SPLIT_AT:
                    split_weights(e + 1, SPLIT_AT.index(n % STEPS))
            low_part(STEPS * BLOCKS - 1)
            dve.wait_ge(S["shared_added"], 1)
            for c in range(CH):
                dve.wait_ge(S["last_down"], c + 1)
                dve.tensor_tensor(xs[:, c, :].rearrange("p (t n) -> p t n", t=HALVES),
                                  h[:, c, :].rearrange("p (t n) -> p t n", t=HALVES),
                                  ps[:, 4 + 2 * c:6 + 2 * c, 0:HT], ALU.add).then_inc(S["moe_added"], 1)

        @block.tensor
        def _(pe):
            def dense(bank, w, m, x, t, ks=CH):
                for k in range(ks):
                    last = pe.matmul(ps[:, bank, 0:HT], w[:, k, 128 * m:128 * m + 128], x[:, k, half(t)],
                                     start=(k == 0), stop=(k == ks - 1))
                return last

            def mean(k, t, src):
                for c in range(CH):
                    last = pe.matmul(ps[:, NORM_BANK[k][t], 0:HT], ones_mean, src[:, c, half(t)], start=(c == 0),
                                     stop=(c == CH - 1))
                last.then_inc(mean_mm[t], 1)

            def variance(k, t):
                pe.wait_ge(squared[t], k + 1)
                for c in range(CH):
                    last = pe.matmul(ps[:, NORM_BANK[k][t], 0:HT], ones_mean, sq[:, c, half(t)], start=(c == 0),
                                     stop=(c == CH - 1))
                last.then_inc(var_mm[t], 1)

            for k in range(KP):
                pe.wait_ge(patch_in[k], 32)
                for t in range(HALVES):
                    for m in range(CH):
                        last = pe.matmul(ps[:, 4 * t + 2 + m, 0:HT], wp[:, k, 128 * m:128 * m + 128], X[:, k, half(t)],
                                         start=(k == 0), stop=(k == KP - 1))
                    if k == KP - 1:
                        last.then_inc(S["tok_mm"], 1)
            pe.wait_ge(S["const_in"], 16)
            for t in range(HALVES):
                pe.wait_ge(S["h_ready"], CH * (t + 1))
                mean(0, t, h)
            for t in range(HALVES):
                variance(0, t)
            pe.wait_ge(S["kqv_in"], 16)
            for t in range(HALVES):
                pe.wait_ge(normed[t], 1)
                for m in range(CH):
                    last = dense(4 * t + 2 + m, kqv, CH + m, xn, t)
                last.then_inc(S["qk_mm"], 1)
                for m in range(CH):
                    last = dense(4 * t + m, kqv, m, xn, t)
                last.then_inc(S["qk_mm"], 1)
            pe.wait_ge(S["pool_setup"], 3)
            for t in range(HALVES):
                pe.wait_ge(S["q_ready"], t + 1)
                for n in range(8):
                    i = 8 * t + n
                    for o in range(2):
                        for k in range(CH):
                            last = pe.matmul(ps[64 * o:64 * o + 64, 4 * t + 2 + n // 4, 128 * (n % 4):128 * (n % 4) + 128],
                                             xn[:, k, slot(i)], kqv[:, k, 2 * EMB + 128 * o:2 * EMB + 128 * o + 128],
                                             start=(k == 0), stop=(k == CH - 1))
                last.then_inc(S["v_mm"], 1)

            def scores(p):
                if p == 0:
                    for name in ("q_ready", "kx_dve", "kx_act"):
                        pe.wait_ge(S[name], HALVES)
                if p == 1:
                    pe.wait_ge(S["v_act"], 1)
                    pe.wait_ge(S["v_dve"], 1)
                if p >= 2:
                    pe.wait_ge(S["row_max"], p - 1)
                for c in range(CH):
                    for i in range(2):
                        a = 2 * p + i
                        t, o = a // 8, (a % 8) * SEQ
                        last = pe.matmul(ps[64 * i:64 * i + 64, 2 * (p % 2) + c, 0:CHH * SEQ], q[:, c, slot(a)],
                                         kx[:, t, c, :, o:o + SEQ], start=True, stop=True)
                last.then_inc(S["score_mm"], 1)

            def turn_probs(p):
                pe.wait_ge(S["prob_ready"], p + 1)
                if p >= 1:
                    pe.wait_ge(S["pT_ready"], p)
                pr = prob[:, p % 2, :, :].rearrange("p (j o) s -> p j (o s)", o=2)
                for j in range(HEADS // 2):
                    last = pe.transpose(ps[:, 4 + j // 4, 128 * (j % 4):128 * (j % 4) + 128], pr[:, j, :], ident)
                last.then_inc(S["prob_mm"], 1)

            def values(p):
                pe.wait_ge(S["pT_ready"], p + 1)
                if p == 0:
                    pe.wait_ge(S["v_act"], HALVES)
                    pe.wait_ge(S["v_dve"], HALVES)
                if p >= 1:
                    pe.wait_ge(S["inverted"], p)
                for c in range(CH):
                    for i in range(2):
                        for j in range(4):
                            o = 2 * SEQ * c + SEQ * i
                            pe.matmul(ps[32 * j:32 * j + 32, 6, o:o + SEQ], vbd[:, 2 * p + i, 4 * c + j, :],
                                      pT[:, p % 2, 4 * c + j, i, :], start=True, stop=True)
                for c in range(CH):
                    for j in range(4):
                        o = 2 * SEQ * (CH + c)
                        last = pe.matmul(ps[32 * j:32 * j + 32, 6, o:o + 2 * SEQ], const("ones"),
                                         pT[:, p % 2, 4 * c + j, :, :], start=True, stop=True)
                last.then_inc(S["pv_mm"], 1)

            for p in range(PAIRS + 3):
                if p < PAIRS:
                    scores(p)
                if 2 <= p <= PAIRS + 1:
                    turn_probs(p - 2)
                if p >= 3:
                    values(p - 3)
                if p == PAIRS - 1:
                    pe.wait_ge(S["attn_added"], HPAIRS)
                    mean(1, 0, h)
                if p == PAIRS + 1:
                    variance(1, 0)

            def predictor_up(t):
                if t == 0:
                    pe.wait_ge(S["wp1_in"], 16)
                pe.wait_ge(normed[t], 2)
                for k in range(CH):
                    last = pe.matmul(ps[:, NORM_BANK[1][t], 0:8], wp1_sb[:, k, :],
                                     xn[:, k, half(t)].rearrange("p (i s) -> p i s", s=SEQ)[:, :, SEQ - 1],
                                     start=(k == 0), stop=(k == CH - 1))
                last.then_inc(S["p1_mm"], 1)

            def predictor_down(t):
                if t == 0:
                    pe.wait_ge(S["wp2_in"], 16)
                pe.wait_ge(S["p1_act"], t + 1)
                pe.matmul(ps[0:8, NORM_BANK[1][t], 32:40], act8[:, t, :], wp2_sb[:, :], start=True, stop=True)\
                  .then_inc(S["p2_mm"], 1)

            def turn_hot(t):
                pe.wait_ge(S["hot_ready"], t + 1)
                pe.transpose(ps[0:PARTS * EXP, NORM_BANK[1][t], 64:72], hot[:, t, :], ident[0:8, 0:8])\
                  .then_inc(S["hot_mm"], 1)

            predictor_up(0)
            predictor_down(0)
            pe.wait_ge(S["attn_added"], PAIRS)
            mean(1, 1, h)
            turn_hot(0)
            pe.wait_ge(S["bias_ready"], 1)

            def rows_up(p):
                pe.wait_ge(S["w1_copied"], 2 * p + 2)
                if p >= 2:
                    pe.wait_ge(S["f1_gelu"], p - 1)
                if p == HPAIRS - 1:
                    pe.wait_ge(normed[1], 2)
                for k in range(CH):
                    for i in range(2):
                        pe.matmul(ps[64 * i:64 * i + 64, p % 2, :], xn[:, k, slot(2 * p + i)],
                                  w1s[:, p % 2, i, k, :], start=(k == 0), stop=False)
                pe.wait_ge(S["hot_columns"], p // HPAIRS + 1)
                for i in range(2):
                    last = pe.matmul(ps[64 * i:64 * i + 64, p % 2, :], hotT[:, 2 * p + i, :], bias_parts[:, 0:FFN],
                                     start=False, stop=True)
                last.then_inc(S["f1_mm"], 1)

            def turn_rows(p):
                pe.wait_ge(S["f1_gelu"], p + 1)
                if p >= 2:
                    pe.wait_ge(S["f1_T_ready"], p - 1)
                for k in range(FC):
                    last = pe.transpose(ps[:, 2 + p % 2, 128 * k:128 * k + 128], hg[:, p % 2, 128 * k:128 * k + 128], ident)
                last.then_inc(S["f1_t"], 1)

            def rows_down(p):
                pe.wait_ge(S["f1_T_ready"], p + 1)
                pe.wait_ge(S["w2_copied"], 2 * p + 2)
                if p >= 1:
                    pe.wait_ge(S["f2_ready"], p)
                for i in range(2):
                    pe.matmul(ps[64 * i:64 * i + 64, 4, 0:EMB], hotT[:, 2 * p + i, :], bias_parts[:, FFN:], start=True,
                              stop=False)
                for k in range(FC):
                    for i in range(2):
                        last = pe.matmul(ps[64 * i:64 * i + 64, 4, 0:EMB], hgT[:, p % 2, k, 64 * i:64 * i + 64],
                                         w2s[:, p % 2, i, k, :], start=False, stop=(k == FC - 1))
                last.then_inc(S["f2_mm"], 1)

            def turn_out(p):
                pe.wait_ge(S["f2_ready"], p + 1)
                if p >= 1:
                    pe.wait_ge(S["r_ready"], p)
                for c in range(CH):
                    last = pe.transpose(ps[:, 5, 128 * c:128 * c + 128], rr[:, p % 2, 128 * c:128 * c + 128], ident)
                last.then_inc(S["f2_t"], 1)

            def reasoned(t):
                if t == 0:
                    pe.wait_ge(S["wo_in"], 16)
                pe.wait_ge(S["r_ready"], HPAIRS * (t + 1))
                for m in range(CH):
                    last = dense(OUT_BANK[t] + m, wo_sb, m, rT, t)
                last.then_inc(S["wo_mm"], 1)

            for p in range(PAIRS + 3):
                if p < PAIRS:
                    rows_up(p)
                if 1 <= p <= PAIRS:
                    turn_rows(p - 1)
                if p == 2:
                    predictor_down(1)
                if 2 <= p <= PAIRS + 1:
                    rows_down(p - 2)
                if p >= 3:
                    turn_out(p - 3)
                if p == 0:
                    variance(1, 1)
                if p == 1:
                    predictor_up(1)
                if p == 3:
                    turn_hot(1)
                if p == PAIRS - 1:
                    reasoned(0)
                if p == PAIRS:
                    pe.wait_ge(S["ffn_added"], 1)
                    mean(2, 0, h)
                if p == PAIRS + 1:
                    variance(2, 0)
                if p == PAIRS + 2:
                    pe.wait_ge(normed[0], 3)
                    mean(3, 0, rT)

            def queries(t):
                pe.wait_ge(normed[t], 4)
                for m in range(CH):
                    last = dense(QUERY_BANK[t] + m, qkv, m, xn, t)
                last.then_inc(S["lq_mm"], 1)

            reasoned(1)
            variance(3, 0)
            pe.wait_ge(S["ffn_added"], 2)
            mean(2, 1, h)
            pe.wait_ge(S["qkv_in"], 16)
            queries(0)

            def keys_values(p):
                if p % HPAIRS == 0:
                    pe.wait_ge(S["slotted"], p // HPAIRS + 1)
                if p >= 2:
                    pe.wait_ge(S["v2_ready"], p - 1)
                for k in range(CH):
                    last = pe.matmul(ps[:, p % 2, :], xp[:, k, 128 * p:128 * p + 128], qkv[:, k, EMB:3 * EMB], start=(k == 0),
                                     stop=(k == CH - 1))
                last.then_inc(S["kv_mm"], 1)

            def states(p):
                pe.wait_ge(S["kf_ready"], p + 1)
                pe.wait_ge(S["v2_ready"], p + 1)
                if p == 0:
                    pe.wait_ge(S["lq_ready"], 1)
                if p >= 1:
                    pe.wait_ge(S["state_ready"], p)
                w = 128 + CHH
                for c in range(CH):
                    for i in range(2):
                        a = 64 * i
                        last = pe.matmul(ps[:, 2 + i, w * c:w * c + w], kf[a:a + SEQ, p % 2, 128 * c:128 * c + 128],
                                         vx[a:a + SEQ, p % 2, c, :], start=True, stop=True)
                last.then_inc(S["state_mm"], 1)

            def outputs(p):
                pe.wait_ge(S["state_ready"], p + 1)
                if p == HPAIRS - 1:
                    pe.wait_ge(S["lq_ready"], 2)
                if p >= 1:
                    pe.wait_ge(S["y_ready"], p)
                w = 128 + CHH
                for c in range(CH):
                    for i in range(2):
                        last = pe.matmul(ps[64 * i:64 * i + 64, 4, w * c:w * c + w], q[:, c, slot(2 * p + i)],
                                         kvm[:, p % 2, i, c, :], start=True, stop=True)
                last.then_inc(S["y_mm"], 1)

            def turn_y(p):
                pe.wait_ge(S["y_ready"], p + 1)
                if p >= 1:
                    pe.wait_ge(S["yT_ready"], p)
                for c in range(CH):
                    last = pe.transpose(ps[:, 5, 128 * c:128 * c + 128], yt[:, p % 2, 128 * c:128 * c + 128], ident)
                last.then_inc(S["y_t"], 1)

            def linear_out(t):
                if t == 0:
                    pe.wait_ge(S["wout_in"], 16)
                pe.wait_ge(S["yT_ready"], HPAIRS * (t + 1))
                for m in range(CH):
                    last = dense(OUT_BANK[t] + m, wout, m, yT, t)
                last.then_inc(S["out_mm"], 1)

            for p in range(PAIRS + 3):
                if p < PAIRS:
                    keys_values(p)
                if 1 <= p <= PAIRS:
                    states(p - 1)
                if 2 <= p <= PAIRS + 1:
                    outputs(p - 2)
                if p >= 3:
                    turn_y(p - 3)
                if p == 0:
                    variance(2, 1)
                if p == 1:
                    pe.wait_ge(normed[1], 3)
                    mean(3, 1, rT)
                if p == 2:
                    variance(3, 1)
                if p == 3:
                    queries(1)
                if p == PAIRS - 1:
                    linear_out(0)
                if p == PAIRS:
                    pe.wait_ge(S["x_ready"], 1)
                    mean(4, 0, xs)
                if p == PAIRS + 1:
                    variance(4, 0)
            linear_out(1)
            pe.wait_ge(S["fw_in"], 32)
            for s in range(HALVES * DC + 2):
                if s < HALVES * DC:
                    t, m = s // DC, s % DC
                    if m == 0:
                        pe.wait_ge(normed[t], 5)
                    if m >= 2:
                        pe.wait_ge(S["up_gelu"], s - 1)
                    dense(2 - 2 * t + m % 2, fw1, m, xn, t).then_inc(S["up_mm"], 1)
                if s >= 2:
                    t, k = (s - 2) // DC, (s - 2) % DC
                    pe.wait_ge(S["up_gelu"], s - 1)
                    for m in range(CH):
                        last = pe.matmul(ps[:, 4 + 2 * t + m, 0:HT], fw2[:, k, 128 * m:128 * m + 128], hid[:, k, :],
                                         start=(k == 0), stop=(k == DC - 1))
                    if k == DC - 1:
                        last.then_inc(S["ff_mm"], 1)
                    else:
                        last.then_inc(S["ff_k_mm"], 1)
                if s == 1:
                    pe.wait_ge(S["x_ready"], 2)
                    mean(4, 1, xs)
                if s == 3:
                    variance(4, 1)
                if s == DC + 3:
                    pe.wait_ge(S["ff_added"], 1)
                    mean(5, 0, h)
                if s == DC + 5:
                    variance(5, 0)

            def logits(t):
                pe.wait_ge(normed[t], 6)
                for k in range(CH):
                    last = pe.matmul(ps[0:ROUTE, 6 + t, 0:HT], route_sb[:, k, :], xn[:, k, half(t)], start=(k == 0),
                                     stop=(k == CH - 1))
                last.then_inc(S["r_mm"], 1)

            def turn_logits():
                pe.wait_ge(S["r_copied"], HALVES)
                for c in range(HALVES * RC):
                    last = pe.transpose(ps[0:RT, 4, ROUTE * c:ROUTE * c + ROUTE], rlog[:, RT * c:RT * c + RT],
                                        ident[0:ROUTE, 0:ROUTE])
                last.then_inc(S["r_t"], 1)

            def turn_weights():
                pe.wait_ge(S["r_w"], 1)
                for t in range(HALVES):
                    for c in range(RC):
                        last = pe.transpose(ps[0:ROUTE, 6 + t, RT * c:RT * c + RT], rw[:, t, c, :],
                                            ident[0:RT, 0:RT])
                    last.then_inc(S["r_back"], 1)

            def second_half_mean():
                pe.wait_ge(S["ff_added"], 2)
                mean(5, 1, h)

            def second_half_variance():
                variance(5, 1)
                pe.wait_ge(S["route_in"], 16)
                logits(0)

            def exact(bank, whi, wlo, xh, xl, first, final):
                pe.matmul(bank, whi, xh, start=first, stop=False)
                pe.matmul(bank, wlo, xh, start=False, stop=False)
                return pe.matmul(bank, whi, xl, start=False, stop=final)

            def down(e):
                pe.wait_ge(S["h_lo"], STEPS * (e + 1))
                pe.wait_ge(S["w_lo"], 3 * (e + 1))
                if e == 0:
                    pe.wait_ge(S["w_rows"], HALVES)
                if e == SHARED:
                    pe.wait_ge(S["shared_added"], 1)
                for c in range(CH):
                    for m, (_, rows) in enumerate(MCH):
                        o = EMB * m + 128 * c
                        for t in range(HALVES):
                            last = exact(ps[:, 4 + 2 * c + t, 0:HT], dnhi[0:rows, e % 2, o:o + 128],
                                         dnlo[0:rows, e % 2, o:o + 128], hhi[0:rows, e % 2, m, half(t)],
                                         hlo[0:rows, e % 2, m, half(t)], e in (0, SHARED) and m == 0,
                                         e in (SHARED - 1, BLOCKS - 1) and m == MC - 1)
                    if e == BLOCKS - 1:
                        last.then_inc(S["last_down"], 1)
                if e < BLOCKS - 1:
                    last.then_inc(S["down_mm"], 1)

            def second_half_logits():
                logits(1)

            between = {0: second_half_mean, 1: second_half_variance, 3: second_half_logits, 4: turn_logits,
                       7: turn_weights}
            for n in range(STEPS * BLOCKS):
                e, t, m = moe_step(n)
                r0, rows = MCH[m]
                if n % STEPS == 0:
                    pe.wait_ge(S["w_lo"], 3 * e + 1)
                if n < STEPS and m == 0:
                    pe.wait_ge(S["x_lo"], t + 1)
                if n >= 2:
                    pe.wait_ge(S["h_mul"], n - 1)
                for u, done in enumerate(("g_mm", "u_mm")):
                    for k in range(CH):
                        o = 2 * MOE_I * k + MOE_I * u + r0
                        last = exact(ps[0:rows, 2 * (n % 2) + u, 0:HT], guhi[:, e % 2, o:o + rows],
                                     gulo[:, e % 2, o:o + rows], xhi[:, k, half(t)], xlo[:, k, half(t)],
                                     k == 0, k == CH - 1)
                    last.then_inc(S[done], 1)
                if n in between:
                    between[n]()
                if n == FIRST_DOWN_AFTER or (e >= 2 and n % STEPS == DOWN_AFTER):
                    down(e - 1)
            down(BLOCKS - 1)


def wt(w):
    k, m = w.shape
    return np.ascontiguousarray(w.reshape(k // 128, 128, m).transpose(1, 0, 2))


def kernel(**inp):
    import concourse.bacc as bacc
    from concourse.bass_utils import run_bass_kernel_spmd

    a = {k: np.asarray(v) for k, v in inp.items()}
    side = 96 // 16
    x = a["x"].reshape(IMGS, side, 16, side, 16, 3).transpose(2, 4, 5, 0, 1, 3).reshape(PATCH, TOK)
    kqv = a["L0_attn_W_kqv"].T
    v = kqv[:, 2 * EMB:].reshape(EMB, HEADS // 2, 2, HD).transpose(0, 2, 1, 3).reshape(EMB, EMB)
    cols = np.zeros((128, NCOLS), np.float32)

    def put(name, value):
        cols[:, COLS[name][0]:COLS[name][1]] = value

    def per_feature(b):
        return b.reshape(-1, 128).T

    put("b_proj", per_feature(a["L0_tok_b_proj"]))
    put("pos", a["L0_tok_pos_emb"].T.reshape(CH, 128, SEQ).transpose(1, 0, 2).reshape(128, -1))
    put("bp1", a["L0_ffn_bp1"].reshape(128, 1))
    put("bp2", np.broadcast_to(a["L0_ffn_bp2"], (128, EXP)))
    put("bo", per_feature(a["L0_ffn_bo"]))
    put("bq", per_feature(a["L1_attn_qkv_b"][:EMB]))
    for name in ("out_b", "b1", "b2", "g1", "be1", "g2", "be2"):
        put(name, per_feature(a["L1_attn_" + name]))

    consts = np.zeros((128, NCONST), np.float32)

    def fix(name, value):
        consts[:, CONST[name][0]:CONST[name][1]] = value

    fix("ident", np.eye(128))
    fix("mean", 1.0 / EMB)
    base = (2 ** 8) ** (1.0 / HEADS)
    slopes = np.array([1.0 / base ** (i + 1) for i in range(HEADS)], np.float32)
    rel = (np.arange(SEQ)[None, :] - np.arange(SEQ)[:, None]).astype(np.float32)
    alibi = np.where(rel[:, None, :] > 0, np.float32(NEG), slopes[None, :, None] * rel[:, None, :])
    both = np.zeros((128, HEADS * SEQ), np.float32)
    both[0:SEQ] = both[64:64 + SEQ] = alibi.reshape(SEQ, -1)
    fix("alibi", both)
    part = np.arange(128)[:, None] // HD
    fix("head", part == np.arange(CHH)[None])
    fix("block", np.concatenate([part == np.arange(128)[None] // HD, part == np.arange(CHH)[None]], 1))
    fix("iota", np.tile(np.arange(EXP), PARTS)[None])
    fix("ones", np.arange(128)[:, None] // SLOT == np.arange(2 * HD)[None] // HD)
    fix("later", -1.0 * (np.arange(128)[:, None] >= EXP * np.arange(1, PARTS)[None]))

    w1 = a["L0_ffn_W1"].reshape(EXP, CH, 128, FFN).transpose(2, 0, 1, 3)
    w2 = a["L0_ffn_W2"].reshape(EXP, FC, 128, EMB).transpose(2, 0, 1, 3)
    qkv = a["L1_attn_qkv_w"]
    sg, su, sd = (a["L1_ffn_shared_" + n + "_w"] for n in ("gate", "up", "down"))
    gu = [np.concatenate([sg[s:s + MOE_I], su[s:s + MOE_I]], 0) for s in (0, MOE_I)]
    gu += [a["L1_ffn_experts_gate_up"][e] for e in range(EXP)]
    gu = np.stack([wt(g.T).reshape(128, GU) for g in gu])
    dn = [sd.T[s:s + MOE_I] for s in (0, MOE_I)] + [a["L1_ffn_experts_down"][e].T for e in range(EXP)]
    down = np.zeros((BLOCKS, 128, MC, EMB), np.float32)
    for e, d in enumerate(dn):
        for m, (r0, rows) in enumerate(MCH):
            down[e, :rows, m] = d[r0:r0 + rows]
    route = np.concatenate([a["L1_ffn_gate_w"], a["L1_ffn_shared_expert_gate_w"]], 0).T

    arrays = {
        "patches": wt(x), "w_proj": wt(a["L0_tok_W_proj"].T), "w_kqv": wt(np.concatenate([kqv[:, :2 * EMB], v], 1)),
        "cols": cols, "consts": consts, "wp1": wt(a["L0_ffn_Wp1"]), "wp2": a["L0_ffn_Wp2"],
        "w1x": w1, "b1x": a["L0_ffn_b1"], "w2x": w2, "b2x": a["L0_ffn_b2"], "wo": wt(a["L0_ffn_Wo"]),
        "qkv_w": wt(qkv), "kv_b": a["L1_attn_qkv_b"][EMB:], "out_w": wt(a["L1_attn_out_w"]),
        "ffn_w1": wt(a["L1_attn_w1"]), "ffn_w2": wt(a["L1_attn_w2"]), "route_w": wt(route),
        "moe_gu": gu, "moe_down": down.reshape(BLOCKS, 128, DOWN),
    }
    arrays = {k: np.ascontiguousarray(v) for k, v in arrays.items()}
    nc = bacc.Bacc("TRN2", target_bir_lowering=False, num_devices=1)
    args = {k: nc.dram_tensor(k, v.shape, F32, kind="ExternalInput").ap() for k, v in arrays.items()}
    out = nc.dram_tensor("out", (128, CH, TOK), F32, kind="ExternalOutput").ap()
    tower(nc, out=out, **args)
    r = run_bass_kernel_spmd(nc, [arrays], core_ids=[0])
    got = r.results[0]["out"]
    return np.ascontiguousarray(got.transpose(2, 1, 0).reshape(IMGS, SEQ, EMB))
```

```python
from contextlib import ExitStack

import numpy as np

import concourse.bass as bass
from concourse import mybir

F32 = mybir.dt.float32
F32R = mybir.dt.float32r
BF16 = mybir.dt.bfloat16
U32 = mybir.dt.uint32
ALU = mybir.AluOpType
ACT = mybir.ActivationFunctionType
AX = mybir.AxisListType

IMGS, SEQ, EMB, PATCH = 16, 36, 256, 768
TOK = IMGS * SEQ
CH = EMB // 128
HALVES = 2
HT = TOK // HALVES
PAIRS = IMGS // 2
HPAIRS = PAIRS // HALVES
HEADS, HD = 16, 16
CHH = 128 // HD
SLOT = 64
PAD = SLOT - SEQ
KP = PATCH // 128
EXP, FFN = 8, 512
PARTS = 3
FC = FFN // 128
NAV = 128
DFF = 1024
DC = DFF // 128
HID_SLOTS = 4
GELU_SLOTS = 3
UP_BANKS = 4
SKEW = 3
MOE_I = 352
MCH = [(0, 128), (128, 128), (256, 96)]
MC = len(MCH)
SHARED = 2
BLOCKS = SHARED + EXP
STEPS = HALVES * MC
SPLIT_AFTER = {n + part_at: (e, part) for e in range(SHARED + 1, SHARED + EXP) for n in (STEPS * (e - 1),)
               for part, part_at in enumerate((1, 4, 5))}
SPLIT_AFTER.update({STEPS * SHARED - 3: (SHARED, 0), STEPS * SHARED - 1: (SHARED, 1), STEPS * SHARED: (SHARED, 2)})
DOWN_AFTER = {STEPS * (e + 1) + 1: e for e in range(1, BLOCKS - 2)}
DOWN_AFTER[STEPS * SHARED - 1] = 0
DOWN_AFTER[STEPS * BLOCKS - 1] = BLOCKS - 2
GU = CH * 2 * MOE_I
DOWN = MC * EMB
RT = 96
RC = HT // RT
ROUTE = EXP + 1
NORM_BANK = ((0, 4), (7, 6), (6, 7), (6, 7), (6, 7), (4, 5))
QUERY_BANK = (2, 6)
OUT_BANK = (6, 0)
EPS = 1e-5
DEN_EPS = 1e-6
NEG = -1e30

COLS = {}
_at = 0
for _name, _n in (("b_proj", CH), ("pos", CH * SEQ), ("bp1", 1), ("bp2", EXP), ("bo", CH), ("bq", CH),
                  ("out_b", CH), ("b1", DC), ("b2", CH), ("g1", CH), ("be1", CH), ("g2", CH), ("be2", CH)):
    COLS[_name] = (_at, _at + _n)
    _at += _n
NCOLS = _at
CONST = {}
_at = 0
for _name, _n in (("ident", 128), ("mean", 128), ("head", CHH), ("block", 128 + CHH), ("iota", PARTS * EXP),
                  ("ones", 2 * HD), ("later", PARTS - 1), ("alibi", HEADS * SEQ)):
    CONST[_name] = (_at, _at + _n)
    _at += _n
NCONST = _at


def moe_step(n):
    if n < SHARED * STEPS:
        return n // MC % SHARED, n // (MC * SHARED), n % MC
    return n // STEPS, n // MC % HALVES, n % MC


def steps_done(e):
    return max(n for n in range(STEPS * BLOCKS) if moe_step(n)[0] == e) + 1


def tower(nc, patches, w_proj, w_kqv, cols, consts, wp1, wp2, w1x, b1x, w2x, b2x, wo,
          qkv_w, kv_b, out_w, ffn_w1, ffn_w2, route_w, moe_gu, moe_down, out):
    with ExitStack() as ctx:
        def sb(name, shape, dt=F32, where=ctx):
            return where.enter_context(nc.sbuf_tensor(name, shape, dt))

        def sem(name):
            return ctx.enter_context(nc.semaphore(name))

        gate_dram = nc.dram_tensor("gate_dram", (ROUTE, TOK), F32, kind="Internal").ap()
        ps = ctx.enter_context(nc.psum_tensor("ps", [128, 8, 512], F32))

        h = sb("h", [128, CH, TOK])
        xc = sb("xc", [128, CH, TOK])
        sq = sb("sq", [128, CH, TOK])
        rstd = sb("rstd", [128, TOK])
        xn = sb("xn", [128, CH, TOK + PAD])
        xs = sb("xs", [128, CH, TOK])
        rT = sb("rT", [128, CH, TOK])
        with ExitStack() as reg:
            hid_lo = sb("hid_lo", [128, HID_SLOTS, HT], F32R, where=reg)
        q = sb("q", [128, CH, TOK + PAD])
        vec = sb("vec", [128, NCOLS])
        cst = sb("cst", [128, NCONST])
        eps = sb("eps", [128, 1])
        bo3 = sb("bo3", [128, CH])
        kqv = sb("kqv", [128, CH, 3 * EMB])
        wo_sb = sb("wo_sb", [128, CH, EMB])
        wp1_sb = sb("wp1_sb", [128, CH, NAV])
        wp2_sb = sb("wp2_sb", [128, EXP])
        route_sb = sb("route_sb", [128, CH, ROUTE])
        sc = sb("sc", [128, 2, HEADS * SEQ])
        top = sb("top", [128, 2, HEADS])
        rsums = sb("rsums", [128, 2, CH, 2 * SEQ])
        attn = sb("attn", [128, 2, CH, 2 * SEQ])
        act8 = sb("act8", [128, HALVES, 8])
        lg = sb("lg", [8, HALVES, EXP])
        mx8 = sb("mx8", [8, HALVES, 8])
        nmx = sb("nmx", [8, HALVES])
        ex8 = sb("ex8", [8, HALVES, EXP])
        sm8 = sb("sm8", [8, HALVES])
        rs8 = sb("rs8", [8, HALVES])
        pr8 = sb("pr8", [8, HALVES, EXP])
        pick = sb("pick", [8, HALVES, 8], U32)
        pickf = sb("pickf", [8, HALVES])
        hot = sb("hot", [8, HALVES, PARTS * EXP])
        hotT = sb("hotT", [PARTS * EXP, IMGS, SLOT], BF16)
        bias_parts = sb("bias_parts", [PARTS * EXP, FFN + EMB], BF16)

        bias_raw = xs[0:PARTS * EXP].rearrange("p c n -> p (c n)")[:, 0:FFN + EMB]
        bias_off = rT[0:PARTS * EXP].rearrange("p c n -> p (c n)")[:, 0:FFN + EMB]

        def col(name, a=0, n=1):
            return vec[:, COLS[name][0] + a:COLS[name][0] + a + n]

        def const(name):
            return cst[:, CONST[name][0]:CONST[name][1]]

        ident = const("ident")
        ones_mean = const("mean")

        with ExitStack() as reg:
            X_hi = sb("X_hi", [128, KP, TOK], F32R, where=reg)
            wp_hi = sb("wp_hi", [128, KP, EMB], F32R, where=reg)
        with ExitStack() as reg:
            kx = sb("kx", [128, HALVES, CH, CHH, HT], where=reg)
        with ExitStack() as reg:
            fw1_lo = sb("fw1_lo", [128, CH, DFF], F32R, where=reg)
            fw2_lo = sb("fw2_lo", [128, DC, EMB], F32R, where=reg)
        with ExitStack() as reg:
            fw1 = sb("fw1", [128, CH, DFF], where=reg)
            fw2 = sb("fw2", [128, DC, EMB], where=reg)
            wout = sb("wout", [128, CH, EMB], where=reg)
            kvb = sb("kvb", [128, 2 * EMB], where=reg)
            hid_hi = sb("hid_hi", [128, HID_SLOTS, HT], F32R, where=reg)
            with ExitStack() as same:
                kv_lo = sb("kv_lo", [128, CH, 3 * EMB], F32R, where=same)[:, :, EMB:]
            qkv = sb("qkv", [128, CH, 3 * EMB], where=reg)
            kv_hi = sb("kv_hi", [128, CH, 2 * EMB], F32R, where=reg)
        with ExitStack() as reg:
            hhi = sb("hhi", [128, 2, MC, TOK], F32R, where=reg)
            hlo = sb("hlo", [128, 2, MC, TOK], F32R, where=reg)
            xhi = sb("xhi", [128, CH, TOK], F32R, where=reg)
            xlo = sb("xlo", [128, CH, TOK], F32R, where=reg)
        holdC = sb("holdC", [128, 9216])
        with ExitStack() as reg:
            X_lo = sb("X_lo", [128, KP, TOK], F32R, where=reg)
            wp_lo = sb("wp_lo", [128, KP, EMB], F32R, where=reg)
        with ExitStack() as reg:
            X = sb("X", [128, KP, TOK], where=reg)
            wp = sb("wp", [128, KP, EMB], where=reg)
            sb("below_kq", [128, IMGS * HEADS * HD + 2 * HEADS * SLOT - KP * (TOK + EMB)], where=reg)
            kq_hi = sb("kq_hi", [128, CH, 2 * EMB], F32R, where=reg)
            kq_lo = sb("kq_lo", [128, CH, 2 * EMB], F32R, where=reg)
        with ExitStack() as reg:
            vbd = sb("vbd", [128, IMGS, HEADS // 2, 2 * HD], where=reg)
            prob = sb("prob", [128, 2, HEADS, SLOT], where=reg)
            pT = sb("pT", [128, 2, HEADS // 2, 2, SEQ], where=reg)
        with ExitStack() as reg:
            w1s = sb("w1s", [128, 2, 2, CH, FFN], where=reg)
            w2s = sb("w2s", [128, 2, 2, FC, EMB], where=reg)
        with ExitStack() as reg:
            vx = sb("vx", [128, 2, CH, 128 + CHH], where=reg)
            kvm = sb("kvm", [128, 2, 2, CH, 128 + CHH], where=reg)
            xp_hi = sb("xp_hi", [128, CH, IMGS * SLOT], F32R, where=reg)
            fw1_hi = sb("fw1_hi", [128, CH, DFF], F32R, where=reg)
            fw2_hi = sb("fw2_hi", [128, DC, EMB], F32R, where=reg)
        with ExitStack() as reg:
            gate = sb("gate", [128, ROUTE, TOK], where=reg)
        holdB = sb("holdB", [128, 8192])
        with ExitStack() as reg:
            w1a = sb("w1a", [128, EXP, CH, FFN], where=reg)
            w2a = sb("w2a", [128, EXP, FC, EMB], where=reg)
        with ExitStack() as reg:
            sb("below_xp", [128, 3 * 2 * (GU + DOWN)], where=reg)
            xp_lo = sb("xp_lo", [128, CH, IMGS * SLOT], F32R, where=reg)
        with ExitStack() as reg:
            guhi = sb("guhi", [128, 2, GU], F32R, where=reg)
            gulo = sb("gulo", [128, 2, GU], F32R, where=reg)
            dnhi = sb("dnhi", [128, 2, DOWN], F32R, where=reg)
            dnlo = sb("dnlo", [128, 2, DOWN], F32R, where=reg)
            guraw = sb("guraw", [128, 2, GU], where=reg)
            dnraw = sb("dnraw", [128, 2, DOWN], where=reg)
            sil = sb("sil", [128, 2, 2, HT], where=reg)
            prod = sb("prod", [128, 2, HT], where=reg)
            wrows = sb("wrows", [ROUTE, TOK], where=reg)
            rlog = sb("rlog", [ROUTE, TOK], where=reg)
        holdA = sb("holdA", [128, 16384])
        with ExitStack() as reg:
            xn_hi = sb("xn_hi", [128, CH, TOK], F32R, where=reg)
            xn_lo = sb("xn_lo", [128, CH, TOK], F32R, where=reg)
        hg = sb("hg", [128, 2, FFN])
        hgT = sb("hgT", [128, 2, FC, 128])
        rr = sb("rr", [128, 2, EMB])
        kf = hg
        ke = sc
        yt = rr
        dinv = sb("dinv", [128, 2, CH, CHH])
        yT = rT
        gelu_out = hg.rearrange("p a n -> p (a n)")[:, 0:GELU_SLOTS * HT].rearrange("p (a n) -> p a n", n=HT)

        S = {}
        for name in (
            "alibi_in", "cols_in", "const_in", "kqv_in", "qkv_in", "wout_in", "wo_in", "kvb_in",
            "wp1_in", "wp2_in", "bias_in", "route_in", "w1a_in", "w2a_in", "fw_in",
            "setup", "pool_setup", "bias_step", "bias_ready", "dve_step", "act_step",
            "patch_hi", "patch_lo", "tok_mm", "h_ready", "kq_hi", "kq_lo", "xn_hi", "xn_lo",
            "qk_mm", "q_ready", "kx_dve", "kx_act", "v_mm", "v_act", "v_dve",
            "score_mm", "row_max", "shifted", "prob_ready", "prob_mm", "pT_ready", "pv_mm", "inverted",
            "attn_scaled", "attn_added",
            "p1_mm", "p1_act", "p2_mm", "p2_logit", "p2_exp", "pick_ready", "hot_ready", "hot_mm", "hot_columns",
            "w1_copied", "w2_copied", "f1_mm", "f1_gelu", "f1_t", "f1_T_ready", "f2_mm", "f2_ready", "f2_t",
            "r_ready", "wo_mm", "ffn_added",
            "kv_hi", "kv_lo", "slot_hi", "slotted", "lq_mm", "lq_min", "lq_relu", "lq_exp", "lq_ready",
            "kv_mm", "k_ready", "k_min", "k_exp", "kf_ready", "v2_ready", "state_mm", "state_ready",
            "y_mm", "y_ready", "y_t", "yT_ready", "out_mm", "x_ready",
            "fw_hi", "fw_lo", "x_hi", "x_lo", "up_mm", "up_gelu", "hid_hi", "hid_lo", "ff_mm", "ff_added",
            "r_mm", "r_copied", "r_t", "r_max", "r_exp", "r_w", "r_back", "w_rows", "gate_out",
            "w_hi", "first_w_lo", "w_lo", "g_mm", "u_mm", "silu", "gated", "h_mul", "h_hi", "h_lo",
            "down_mm", "shared_added", "last_down", "moe_added", "stored",
        ):
            S[name] = sem(name)
        raw_in = [sem(f"raw_in{i}") for i in range(2)]
        mean_mm, centred, squared, var_mm, rstd_ready, normed = (
            [sem(f"{name}{t}") for t in range(HALVES)]
            for name in ("mean_mm", "centred", "squared", "var_mm", "rstd_ready", "normed"))
        patch_in = [sem(f"patch_in{k}") for k in range(KP)]
        gate_in = [sem(f"gate_in{e}") for e in range(ROUTE)]
        rtok = sb("rtok", [RT, HALVES, RC, ROUTE])
        rex = sb("rex", [RT, HALVES, RC, ROUTE])
        rw = sb("rw", [RT, HALVES, RC, ROUTE])
        rmx = sb("rmx", [RT, HALVES, RC, 8])
        rix = sb("rix", [RT, HALVES, RC, 8], U32)
        rixf = sb("rixf", [RT, HALVES, RC, 8])
        rsum = sb("rsum", [RT, HALVES, RC])
        rm2 = sb("rm2", [RT, HALVES, RC, EXP])

        def half(t):
            return slice(t * HT, (t + 1) * HT)

        def img(i):
            return slice(i * SEQ, (i + 1) * SEQ)

        def slot(i):
            return slice(i * SEQ, i * SEQ + SLOT)

        def value_block(t, b, o):
            rows, i0 = slice(64 * o, 64 * o + 64), 8 * t + 4 * b
            dst = vbd[rows, i0:i0 + 4, :, HD * o:HD * o + HD].rearrange("p i j d -> p (i j) d")
            return dst, ps[rows, 4 * t + 2 + b, :].rearrange("p (i d) -> p i d", d=HD)

        def lower_parts(e, n):
            return (S["first_w_lo"], 3 * e + n) if e < SHARED else (S["w_lo"], 3 * (e - SHARED) + n)

        def weight_parts(e):
            b, full, tail = e % 2, slice(0, 2 * EMB), slice(2 * EMB, DOWN)
            rows = slice(0, MCH[-1][1])
            return ((gulo[:, b, :], guhi[:, b, :], guraw[:, b, :]),
                    (dnlo[:, b, full], dnhi[:, b, full], dnraw[:, b, full]),
                    (dnlo[rows, b, tail], dnhi[rows, b, tail], dnraw[rows, b, tail]))

        block = ctx.enter_context(nc.Block())

        @block.sync
        def _(sp):
            for k in range(KP):
                sp.dma_start(wp[:, k, :], w_proj[:, k, :]).then_inc(patch_in[k], 16)
                sp.dma_start(X[:, k, :], patches[:, k, :]).then_inc(patch_in[k], 16)
            small = CONST["alibi"][0]
            sp.dma_start(vec[:, :], cols).then_inc(S["cols_in"], 16)
            sp.dma_start(cst[:, 0:small], consts[:, 0:small]).then_inc(S["const_in"], 16)
            sp.dma_start(kqv[:, :, :], w_kqv).then_inc(S["kqv_in"], 16)
            sp.dma_start(cst[:, small:], consts[:, small:]).then_inc(S["alibi_in"], 16)
            sp.dma_start(w1a[:, :, :, :], w1x).then_inc(S["w1a_in"], 16)
            sp.dma_start(w2a[:, :, :, :], w2x).then_inc(S["w2a_in"], 16)
            sp.dma_start(wo_sb[:, :, :], wo).then_inc(S["wo_in"], 16)
            sp.wait_ge(S["score_mm"], PAIRS)
            sp.dma_start(qkv[:, :, :], qkv_w).then_inc(S["qkv_in"], 16)
            sp.dma_start(kvb[:, :], kv_b.partition_broadcast(128)).then_inc(S["kvb_in"], 16)
            sp.dma_start(wout[:, :, :], out_w).then_inc(S["wout_in"], 16)
            sp.dma_start(fw1[:, :, :], ffn_w1).then_inc(S["fw_in"], 16)
            sp.dma_start(fw2[:, :, :], ffn_w2).then_inc(S["fw_in"], 16)
            sp.wait_ge(S["w1_copied"], IMGS)
            sp.wait_ge(S["w2_copied"], IMGS)
            for e in range(BLOCKS):
                if e == SHARED + 2:
                    sp.wait_ge(S["w_rows"], HALVES)
                    sp.dma_start(gate_dram, wrows[:, :]).then_inc(S["gate_out"], 16)
                    sp.wait_ge(S["gate_out"], 16)
                    for g in (0, EXP) + tuple(range(1, EXP)):
                        sp.dma_start(gate[:, g, :], gate_dram[g, :].partition_broadcast(128)).then_inc(gate_in[g], 16)
                if e >= 2:
                    sp.wait_ge(S["w_hi"], 3 * (e - 1))
                    lower_sem, count = lower_parts(e - 2, 3)
                    sp.wait_ge(lower_sem, count)
                sp.dma_start(guraw[:, e % 2, :], moe_gu[e]).then_inc(raw_in[e % 2], 16)
                sp.dma_start(dnraw[:, e % 2, 0:2 * EMB], moe_down[e, :, 0:2 * EMB]).then_inc(raw_in[e % 2], 16)
                sp.dma_start(dnraw[0:96, e % 2, 2 * EMB:], moe_down[e, 0:96, 2 * EMB:]).then_inc(raw_in[e % 2], 16)
            for c in range(CH):
                sp.wait_ge(S["moe_added"], c + 1)
                sp.dma_start(out[:, c, :], xs[:, c, :]).then_inc(S["stored"], 16)
            sp.wait_ge(S["stored"], 16 * CH)

        @block.gpsimd
        def _(pool):
            pool.dma_start(wp1_sb[:, :, :], wp1).then_inc(S["wp1_in"], 16)
            pool.dma_start(wp2_sb[:, :], wp2).then_inc(S["wp2_in"], 16)
            for part in range(PARTS):
                rows = slice(EXP * part, EXP * part + EXP)
                pool.dma_start(bias_raw[rows, 0:FFN], b1x).then_inc(S["bias_in"], 16)
                pool.dma_start(bias_raw[rows, FFN:], b2x).then_inc(S["bias_in"], 16)
            pool.dma_start(route_sb[:, :, :], route_w).then_inc(S["route_in"], 16)
            pool.memset(eps[:, :], EPS).then_inc(S["pool_setup"], 1)
            pool.memset(xn[:, :, TOK:], 0.0).then_inc(S["pool_setup"], 1)
            pool.memset(q[:, :, TOK:], 0.0).then_inc(S["pool_setup"], 1)
            pool.wait_ge(S["kq_hi"], 1)
            pool.tensor_tensor(kq_lo[:, :, :], kqv[:, :, 0:2 * EMB], kq_hi[:, :, :].bitcast(F32), ALU.subtract)\
                .then_inc(S["kq_lo"], 1)
            pool.wait_ge(S["tok_mm"], HALVES)
            pool.memset(vbd[:, :, :, :], 0.0).then_inc(S["pool_setup"], 1)
            pool.memset(prob[:, :, :, :], 0.0).then_inc(S["pool_setup"], 1)
            steps = 0
            pool.wait_ge(S["bias_in"], 2 * 16 * PARTS)
            pool.wait_ge(S["const_in"], 16)
            for part in range(PARTS - 1):
                later = cst[0:PARTS * EXP, CONST["later"][0] + part:CONST["later"][0] + part + 1]
                for step in range(3):
                    if step == 0:
                        ins = pool.tensor_copy(bias_parts[:, :], bias_raw)
                    elif step == 1:
                        ins = pool.tensor_scalar(bias_off, bias_parts[:, :], later, None, ALU.mult)
                    else:
                        ins = pool.tensor_tensor(bias_raw, bias_raw, bias_off, ALU.add)
                    ins.then_inc(S["bias_step"], 1)
                    steps += 1
                    pool.wait_ge(S["bias_step"], steps)
            pool.tensor_copy(bias_parts[:, :], bias_raw).then_inc(S["bias_ready"], 1)
            for p in range(PAIRS + 3):
                if p < PAIRS:
                    pool.wait_ge(S["row_max"], p + 1)
                    s = sc[:, p % 2, :].rearrange("p (h k) -> p h k", k=SEQ)
                    pool.tensor_tensor(s, s, top[:, p % 2, :].unsqueeze(2).to_broadcast([128, HEADS, SEQ]),
                                       ALU.subtract).then_inc(S["shifted"], 1)
                if p >= 3:
                    d = p - 3
                    toks = slice(2 * d * SEQ, 2 * (d + 1) * SEQ)
                    pool.wait_ge(S["inverted"], d + 1)
                    pool.tensor_tensor(attn[:, d % 2, :, :], attn[:, d % 2, :, :], rsums[:, d % 2, :, :],
                                       ALU.mult).then_inc(S["attn_scaled"], 1)
                    pool.wait_ge(S["attn_scaled"], d + 1)
                    pool.tensor_tensor(h[:, :, toks], h[:, :, toks], attn[:, d % 2, :, :], ALU.add)\
                        .then_inc(S["attn_added"], 1)
            pool.wait_ge(S["qkv_in"], 16)
            pool.tensor_copy(kv_hi[:, :, :], qkv[:, :, EMB:]).then_inc(S["kv_hi"], 1)
            pool.wait_ge(S["kv_hi"], 1)
            pool.tensor_tensor(kv_lo, qkv[:, :, EMB:], kv_hi[:, :, :].bitcast(F32), ALU.subtract)\
                .then_inc(S["kv_lo"], 1)
            pool.wait_ge(S["f1_mm"], PAIRS)
            pool.wait_ge(S["f2_mm"], PAIRS)
            pool.memset(vx[:, :, :, 128:], 1.0).then_inc(S["pool_setup"], 1)
            pool.memset(xp_hi[:, :, :].bitcast(F32), 0.0).then_inc(S["pool_setup"], 1)
            pool.memset(xp_lo[:, :, :].bitcast(F32), 0.0).then_inc(S["pool_setup"], 1)
            pool.wait_ge(S["fw_in"], 32)
            n = 0
            for raw, upper, lower in ((fw1, fw1_hi, fw1_lo), (fw2, fw2_hi, fw2_lo)):
                for k in range(CH):
                    width = raw.shape[1] // CH
                    part = slice(k * width, (k + 1) * width)
                    n += 1
                    pool.tensor_copy(upper[:, part, :], raw[:, part, :]).then_inc(S["fw_hi"], 1)
                    pool.wait_ge(S["fw_hi"], n)
                    pool.tensor_tensor(lower[:, part, :], raw[:, part, :], upper[:, part, :].bitcast(F32),
                                       ALU.subtract).then_inc(S["fw_lo"], 1)
            for n, (lo, hi, raw) in enumerate(weight_parts(0) + weight_parts(1)):
                pool.wait_ge(S["w_hi"], n + 1)
                pool.tensor_tensor(lo, raw, hi.bitcast(F32), ALU.subtract).then_inc(S["first_w_lo"], 1)
            for n in range(STEPS * SHARED):
                e, t, m = moe_step(n)
                rows = MCH[m][1]
                pool.wait_ge(S["h_hi"], n + 1)
                pool.tensor_tensor(hlo[0:rows, e % 2, m, half(t)], prod[0:rows, n % 2, :],
                                   hhi[0:rows, e % 2, m, half(t)].bitcast(F32), ALU.subtract).then_inc(S["h_lo"], 1)
            for n in range(STEPS * SHARED, STEPS * BLOCKS):
                e, t, m = moe_step(n)
                rows = MCH[m][1]
                if n % STEPS == 0:
                    pool.wait_ge(gate_in[e - SHARED], 16)
                pool.wait_ge(S["silu"], n + 1)
                pool.wait_ge(S["h_mul"], n - 1)
                pool.tensor_tensor(sil[0:rows, 1, n % 2, :], sil[0:rows, 0, n % 2, :],
                                   gate[0:rows, e - SHARED, half(t)], ALU.mult).then_inc(S["gated"], 1)

        @block.scalar
        def _(act):
            steps = [0]

            def link(ins):
                steps[0] += 1
                ins.then_inc(S["act_step"], 1)
                act.wait_ge(S["act_step"], steps[0])

            def square(k, t):
                act.wait_ge(centred[t], k + 1)
                act.activation(sq[:, :, half(t)], xc[:, :, half(t)], ACT.Square).then_inc(squared[t], 1)

            def inverse_root(k, t):
                act.wait_ge(var_mm[t], k + 1)
                link(act.activation(rstd[:, half(t)], ps[:, NORM_BANK[k][t], 0:HT], ACT.Ln, bias=eps[:, :]))
                act.activation(rstd[:, half(t)], rstd[:, half(t)], ACT.Exp, scale=-0.5).then_inc(rstd_ready[t], 1)

            act.preload_act_table_set("natural_log_exp_and_others")
            for k in range(1, KP):
                act.wait_ge(patch_in[k], 32)
                act.activation(X_hi[:, k, :], X[:, k, :], ACT.Copy)
                act.activation(wp_hi[:, k, :], wp[:, k, :], ACT.Copy).then_inc(S["patch_hi"], 1)
            act.wait_ge(S["kqv_in"], 16)
            act.activation(kq_hi[:, :, :], kqv[:, :, 0:2 * EMB], ACT.Copy).then_inc(S["kq_hi"], 1)
            act.wait_ge(S["pool_setup"], 3)
            for t in range(HALVES):
                square(0, t)
            for t in range(HALVES):
                inverse_root(0, t)
            for t in range(HALVES):
                act.wait_ge(normed[t], 1)
                act.activation(xn_hi[:, :, half(t)], xn[:, :, half(t)], ACT.Copy).then_inc(S["xn_hi"], 1)
            act.wait_ge(S["const_in"], 16)
            for t in range(HALVES):
                act.wait_ge(S["qk_mm"], 2 * t + 1)
                act.activation(q[:, :, half(t)], ps[:, 4 * t + 2:4 * t + 4, 0:HT], ACT.Copy,
                               scale=float(EMB) ** -0.5).then_inc(S["q_ready"], 1)
                act.wait_ge(S["qk_mm"], 2 * t + 2)
                for g in range(CHH):
                    last = act.activation(kx[:, t, 1, g, :], ps[:, 4 * t + 1, 0:HT], ACT.Copy,
                                          scale=const("head")[:, g:g + 1])
                last.then_inc(S["kx_act"], 1)
            act.wait_ge(S["pool_setup"], 5)
            for t in range(HALVES):
                act.wait_ge(S["v_mm"], t + 1)
                for o in range(2):
                    dst, src = value_block(t, 0, o)
                    last = act.activation(dst, src, ACT.Copy)
                last.then_inc(S["v_act"], 1)

            def turned_probs(p):
                act.wait_ge(S["prob_mm"], p + 1)
                if p >= 2:
                    act.wait_ge(S["pv_mm"], p - 1)
                src = ps[:, 4:6, :].rearrange("p b (j i s) -> p (b j) i s", j=4, i=2)
                for i in range(2):
                    last = act.activation(pT[:, p % 2, :, i, :], src[:, :, i, 0:SEQ], ACT.Copy)
                last.then_inc(S["pT_ready"], 1)

            for p in range(PAIRS + 2):
                if p >= 2:
                    turned_probs(p - 2)
                if p < PAIRS:
                    act.wait_ge(S["shifted"], p + 1)
                    if p >= 2:
                        act.wait_ge(S["prob_mm"], p - 1)
                    act.activation(prob[:, p % 2, :, 0:SEQ], sc[:, p % 2, :].rearrange("p (h k) -> p h k", k=SEQ),
                                   ACT.Exp).then_inc(S["prob_ready"], 1)
                if p == PAIRS:
                    square(1, 0)
            inverse_root(1, 0)

            def predictor_gelu(t):
                act.wait_ge(S["p1_mm"], t + 1)
                act.activation(act8[:, t, :], ps[:, NORM_BANK[1][t], 0:8], ACT.Gelu, bias=col("bp1"))\
                   .then_inc(S["p1_act"], 1)

            def predictor_exp(t):
                act.wait_ge(S["p2_logit"], t + 1)
                act.activation(ex8[:, t, :], lg[:, t, :], ACT.Exp, bias=nmx[:, t:t + 1],
                               accum_out=sm8[:, t:t + 1]).then_inc(S["p2_exp"], 1)

            def one_hot_columns(t):
                act.wait_ge(S["hot_mm"], t + 1)
                act.activation(hotT[:, 8 * t:8 * t + 8, :], ps[0:PARTS * EXP, NORM_BANK[1][t], 64:72].unsqueeze(2)
                               .to_broadcast([PARTS * EXP, 8, SLOT]), ACT.Copy).then_inc(S["hot_columns"], 1)

            act.preload_act_table_set("gelu_and_others")
            predictor_gelu(0)
            act.preload_act_table_set("natural_log_exp_and_others")
            predictor_exp(0)
            square(1, 1)
            one_hot_columns(0)
            inverse_root(1, 1)
            act.preload_act_table_set("gelu_and_others")

            def second_matrix(p):
                act.wait_ge(S["pick_ready"], p // HPAIRS + 1)
                if p >= 2:
                    act.wait_ge(S["f2_mm"], p - 1)
                for i in range(2):
                    r = (2 * p + i) % 8
                    e = act.value_load(pick[r:r + 1, p // HPAIRS, 0:1], min_val=0, max_val=EXP - 1)
                    act.activation(w2s[:, p % 2, i, :, :], w2a[:, bass.ds(e, 1), :, :], ACT.Copy)\
                       .then_inc(S["w2_copied"], 1)

            act.wait_ge(S["w2a_in"], 16)
            for p in range(PAIRS + 3):
                if p >= 3:
                    act.wait_ge(S["f2_mm"], p - 2)
                    if p >= 5:
                        act.wait_ge(S["f2_t"], p - 4)
                    act.activation(rr[:, (p - 3) % 2, :], ps[:, 4, 0:EMB], ACT.Copy).then_inc(S["f2_ready"], 1)
                if p < PAIRS:
                    act.wait_ge(S["f1_mm"], p + 1)
                    if p >= 2:
                        act.wait_ge(S["f1_t"], p - 1)
                    act.activation(hg[:, p % 2, :], ps[:, p % 2, :], ACT.Gelu).then_inc(S["f1_gelu"], 1)
                if p == 1:
                    predictor_gelu(1)
                if 1 <= p <= PAIRS:
                    second_matrix(p - 1)
                if p == 2:
                    act.preload_act_table_set("natural_log_exp_and_others")
                    predictor_exp(1)
                    act.preload_act_table_set("gelu_and_others")
                if p == 3:
                    one_hot_columns(1)
                if p == PAIRS - 1:
                    act.preload_act_table_set("natural_log_exp_and_others")
                if p == PAIRS + 1:
                    square(2, 0)
            inverse_root(2, 0)
            square(3, 0)
            inverse_root(3, 0)
            square(2, 1)
            inverse_root(2, 1)

            def query_parts(t):
                act.wait_ge(S["lq_min"], t + 1)
                for c in range(CH):
                    last = act.activation(q[:, c, half(t)], ps[:, QUERY_BANK[t] + c, 0:HT], ACT.Relu, bias=col("bq", c))
                last.then_inc(S["lq_relu"], 1)
                act.activation(xs[:, :, half(t)], xs[:, :, half(t)], ACT.Exp).then_inc(S["lq_exp"], 1)

            query_parts(0)
            square(3, 1)

            def split_weights(e, part):
                if part == 0:
                    act.wait_ge(raw_in[e % 2], 48 * (e // 2 + 1))
                    if e >= 2:
                        act.wait_ge(S["u_mm"], steps_done(e - 2))
                if part == 1 and e >= 2:
                    act.wait_ge(S["down_mm"], e - 1)
                _, hi, raw = weight_parts(e)[part]
                act.activation(hi, raw, ACT.Copy).then_inc(S["w_hi"], 1)

            for p in range(PAIRS + 3):
                if p < PAIRS:
                    act.wait_ge(S["k_min"], p + 1)
                    act.activation(ke[:, p % 2, 0:EMB], ke[:, p % 2, 0:EMB], ACT.Exp).then_inc(S["k_exp"], 1)
                if p == 0:
                    inverse_root(3, 1)
                if p == PAIRS:
                    square(4, 0)
                if p == PAIRS + 1:
                    inverse_root(4, 0)
                if p >= 3:
                    act.wait_ge(S["y_t"], p - 2)
                    src = ps[:, 5, 0:2 * 128].rearrange("p (c i s) -> p c i s", c=CH, i=2)
                    dst = yT[:, :, 2 * (p - 3) * SEQ:2 * (p - 2) * SEQ].rearrange("p c (i s) -> p c i s", i=2)
                    for c in range(CH):
                        last = act.activation(dst[:, c], src[:, c, :, 0:SEQ], ACT.Copy)
                    last.then_inc(S["yT_ready"], 1)
                if p == PAIRS + 2:
                    act.preload_act_table_set("gelu_and_others")
                if p == 2:
                    query_parts(1)
                if 2 <= p <= 7:
                    split_weights((p - 2) // 3, (p - 2) % 3)

            for s in range(HALVES * DC):
                t, m = s // DC, s % DC
                act.wait_ge(S["up_mm"], s + 1)
                if s >= GELU_SLOTS:
                    act.wait_ge(S["hid_lo"], s - GELU_SLOTS + 1)
                act.activation(gelu_out[:, s % GELU_SLOTS, :], ps[:, (s + 2) % UP_BANKS, 0:HT], ACT.Gelu,
                               bias=col("b1", m)).then_inc(S["up_gelu"], 1)
                if s == 2:
                    square(4, 1)
                if s == 4:
                    act.preload_act_table_set("natural_log_exp_and_others")
                    inverse_root(4, 1)
                    act.preload_act_table_set("gelu_and_others")
                if s == DC + 4:
                    square(5, 0)
                if s == DC + 5:
                    act.preload_act_table_set("natural_log_exp_and_others")
                    inverse_root(5, 0)
                    act.preload_act_table_set("gelu_and_others")
            act.preload_act_table_set("silu_and_others")

            def copy_logits(t):
                act.wait_ge(S["r_mm"], t + 1)
                act.activation(rlog[:, half(t)], ps[0:ROUTE, 6 + t, 0:HT], ACT.Copy).then_inc(S["r_copied"], 1)

            def high_part(n):
                e, t, m = moe_step(n)
                rows = MCH[m][1]
                act.wait_ge(S["h_mul"], n + 1)
                if e >= 2 and m == 0 and t == 0:
                    act.wait_ge(S["down_mm"], e - 1)
                act.activation(hhi[0:rows, e % 2, m, half(t)], prod[0:rows, n % 2, :], ACT.Copy)\
                   .then_inc(S["h_hi"], 1)

            for n in range(STEPS * BLOCKS):
                e, t, m = moe_step(n)
                rows = MCH[m][1]
                act.wait_ge(S["g_mm"], n + 1)
                if 2 <= n < STEPS * SHARED + 2:
                    act.wait_ge(S["h_mul"], n - 1)
                if n >= STEPS * SHARED + 2:
                    act.wait_ge(S["gated"], n - STEPS * SHARED - 1)
                act.activation(sil[0:rows, 0, n % 2, :], ps[0:rows, 2 * (n % 2), 0:HT], ACT.Silu)\
                   .then_inc(S["silu"], 1)
                if n >= 1:
                    high_part(n - 1)
                if n == 0:
                    square(5, 1)
                if n == 2:
                    act.preload_act_table_set("natural_log_exp_and_others")
                    inverse_root(5, 1)
                    act.preload_act_table_set("silu_and_others")
                    copy_logits(0)
                if n == 6:
                    copy_logits(1)
                if n == 7:
                    act.preload_act_table_set("natural_log_exp_and_others")
                    act.wait_ge(S["r_max"], 1)
                    act.activation(rex[:, :, :, :], rtok[:, :, :, :], ACT.Exp).then_inc(S["r_exp"], 1)
                    act.preload_act_table_set("silu_and_others")
                if n == 10:
                    for u in range(HALVES):
                        act.wait_ge(S["r_back"], u + 1)
                        act.activation(wrows[:, half(u)], ps[0:ROUTE, 6 + u, 0:HT], ACT.Copy).then_inc(S["w_rows"], 1)
                if n in SPLIT_AFTER:
                    split_weights(*SPLIT_AFTER[n])
            high_part(STEPS * BLOCKS - 1)

        @block.vector
        def _(dve):
            steps = [0]

            def link(ins):
                steps[0] += 1
                ins.then_inc(S["dve_step"], 1)
                dve.wait_ge(S["dve_step"], steps[0])

            def centre(k, t, src):
                dve.wait_ge(mean_mm[t], k + 1)
                mean = ps[:, NORM_BANK[k][t], 0:HT].unsqueeze(1).to_broadcast([128, CH, HT])
                dve.tensor_tensor(xc[:, :, half(t)], src[:, :, half(t)], mean, ALU.subtract).then_inc(centred[t], 1)

            def scale(k, t, out_ap, gain=None):
                dve.wait_ge(rstd_ready[t], k + 1)
                by = rstd[:, half(t)].unsqueeze(1).to_broadcast([128, CH, HT])
                dve.wait_ge(centred[t], k + 1)
                if gain is None:
                    dve.tensor_tensor(out_ap[:, :, half(t)], xc[:, :, half(t)], by, ALU.mult).then_inc(normed[t], 1)
                else:
                    g, b = gain
                    link(dve.tensor_tensor(out_ap[:, :, half(t)], xc[:, :, half(t)], by, ALU.mult))
                    for c in range(CH):
                        last = dve.tensor_scalar(out_ap[:, c, half(t)], out_ap[:, c, half(t)], col(g, c), col(b, c),
                                                 ALU.mult, ALU.add)
                    last.then_inc(normed[t], 1)

            def split_tokens(k, t):
                dve.wait_ge(normed[t], k + 1)
                dve.tensor_copy(xhi[:, :, half(t)], xn[:, :, half(t)]).then_inc(S["x_hi"], 1)
                dve.wait_ge(S["x_hi"], HALVES * (k - 4) + t + 1)
                dve.tensor_tensor(xlo[:, :, half(t)], xn[:, :, half(t)], xhi[:, :, half(t)].bitcast(F32),
                                  ALU.subtract).then_inc(S["x_lo"], 1)

            for k in range(1, KP):
                dve.wait_ge(S["patch_hi"], k)
                dve.tensor_tensor(wp_lo[:, k, :], wp[:, k, :], wp_hi[:, k, :].bitcast(F32), ALU.subtract)
                dve.tensor_tensor(X_lo[:, k, :], X[:, k, :], X_hi[:, k, :].bitcast(F32), ALU.subtract)\
                   .then_inc(S["patch_lo"], 1)
            dve.wait_ge(S["cols_in"], 16)
            dve.wait_ge(S["const_in"], 16)
            dve.tensor_scalar(bo3[:, :], col("bo", 0, CH), 0.3, None, ALU.mult).then_inc(S["setup"], 1)
            for t in range(HALVES):
                dve.wait_ge(S["tok_mm"], t + 1)
                for c in range(CH):
                    pos = col("pos", c * SEQ, SEQ).unsqueeze(1).to_broadcast([128, HT // SEQ, SEQ])
                    dve.scalar_tensor_tensor(
                        out=h[:, c, half(t)].rearrange("p (i s) -> p i s", s=SEQ),
                        in0=ps[:, 4 * t + 2 + c, 0:HT].rearrange("p (i s) -> p i s", s=SEQ),
                        scalar=col("b_proj", c), in1=pos, op0=ALU.add, op1=ALU.add).then_inc(S["h_ready"], 1)
            for t in range(HALVES):
                dve.wait_ge(S["h_ready"], CH * (t + 1))
                centre(0, t, h)
            for t in range(HALVES):
                scale(0, t, xn)
            for t in range(HALVES):
                dve.wait_ge(S["xn_hi"], t + 1)
                dve.tensor_tensor(xn_lo[:, :, half(t)], xn[:, :, half(t)], xn_hi[:, :, half(t)].bitcast(F32),
                                  ALU.subtract).then_inc(S["xn_lo"], 1)
            for t in range(HALVES):
                dve.wait_ge(S["qk_mm"], 2 * t + 2)
                link(dve.tensor_copy(sq[:, 0, half(t)], ps[:, 4 * t, 0:HT]))
                for g in range(CHH):
                    last = dve.tensor_scalar(kx[:, t, 0, g, :], sq[:, 0, half(t)], const("head")[:, g:g + 1], None,
                                             ALU.mult)
                last.then_inc(S["kx_dve"], 1)
            dve.wait_ge(S["pool_setup"], 5)
            for t in range(HALVES):
                dve.wait_ge(S["v_mm"], t + 1)
                for o in range(2):
                    dst, src = value_block(t, 1, o)
                    last = dve.tensor_copy(dst, src)
                last.then_inc(S["v_dve"], 1)

            def scores_max(p):
                dve.wait_ge(S["score_mm"], p + 1)
                if p >= 2:
                    dve.wait_ge(S["prob_ready"], p - 1)
                b0 = 2 * (p % 2)
                link(dve.tensor_tensor(sc[:, p % 2, :].rearrange("p (b n) -> p b n", b=2),
                                       ps[:, b0:b0 + 2, 0:CHH * SEQ],
                                       const("alibi").rearrange("p (b n) -> p b n", b=2), ALU.add))
                dve.tensor_reduce(top[:, p % 2, :], sc[:, p % 2, :].rearrange("p (h k) -> p h k", k=SEQ), AX.X,
                                  ALU.max).then_inc(S["row_max"], 1)

            def invert_sums(p):
                dve.wait_ge(S["pv_mm"], p + 1)
                if p >= 2:
                    dve.wait_ge(S["attn_added"], p - 1)
                bank = ps[:, 6, 0:2 * CH * 2 * SEQ].rearrange("p (o c n) -> p o c n", o=2, c=CH)
                dve.tensor_copy(attn[:, p % 2, :, :], bank[:, 0])
                dve.reciprocal(rsums[:, p % 2, :, :], bank[:, 1]).then_inc(S["inverted"], 1)

            dve.wait_ge(S["alibi_in"], 16)
            for p in range(PAIRS + 3):
                if p < PAIRS:
                    scores_max(p)
                if p == PAIRS:
                    centre(1, 0, h)
                if p == PAIRS + 2:
                    scale(1, 0, xn)
                if p >= 3:
                    invert_sums(p - 3)

            def predictor_logits(t):
                dve.wait_ge(S["p2_mm"], t + 1)
                link(dve.tensor_tensor(lg[:, t, :], ps[0:8, NORM_BANK[1][t], 32:40], col("bp2", 0, EXP)[0:8], ALU.add))
                link(dve.max(mx8[:, t, :], lg[:, t, :]))
                dve.tensor_scalar(nmx[:, t:t + 1], mx8[:, t, 0:1], -1.0, None, ALU.mult).then_inc(S["p2_logit"], 1)

            def predictor_pick(t):
                dve.wait_ge(S["p2_exp"], t + 1)
                link(dve.reciprocal(rs8[:, t:t + 1], sm8[:, t:t + 1]))
                link(dve.tensor_scalar(pr8[:, t, :], ex8[:, t, :], rs8[:, t:t + 1], None, ALU.mult))
                link(dve.max(mx8[:, t, :], pr8[:, t, :]))
                dve.max_index(pick[:, t, :], mx8[:, t, :], pr8[:, t, :]).then_inc(S["pick_ready"], 1)
                dve.wait_ge(S["pick_ready"], t + 1)
                link(dve.tensor_copy(pickf[:, t:t + 1], pick[:, t, 0:1]))
                dve.tensor_scalar(hot[:, t, :], const("iota")[0:8, :], pickf[:, t:t + 1], None, ALU.is_equal)\
                   .then_inc(S["hot_ready"], 1)

            def residual(t):
                if t == 0:
                    dve.wait_ge(S["setup"], 1)
                for c in range(CH):
                    last = dve.scalar_tensor_tensor(out=xs[:, c, half(t)], in0=xn[:, c, half(t)],
                                                    scalar=bo3[:, c:c + 1], in1=h[:, c, half(t)], op0=ALU.add,
                                                    op1=ALU.add)
                link(last)

            def add_ffn(t):
                dve.wait_ge(S["wo_mm"], t + 1)
                b = OUT_BANK[t]
                dve.scalar_tensor_tensor(out=h[:, :, half(t)], in0=ps[:, b:b + 2, 0:HT], scalar=0.3,
                                         in1=xs[:, :, half(t)], op0=ALU.mult, op1=ALU.add)\
                   .then_inc(S["ffn_added"], 1)

            predictor_logits(0)
            predictor_pick(0)
            dve.wait_ge(S["w1a_in"], 16)

            def first_matrix(p):
                dve.wait_ge(S["pick_ready"], p // HPAIRS + 1)
                if p == 0:
                    dve.wait_ge(S["pv_mm"], PAIRS)
                if p >= 2:
                    dve.wait_ge(S["f1_mm"], p - 1)
                for i in range(2):
                    r = (2 * p + i) % 8
                    e = dve.value_load(pick[r:r + 1, p // HPAIRS, 0:1], min_val=0, max_val=EXP - 1)
                    dve.tensor_copy(w1s[:, p % 2, i, :, :], w1a[:, bass.ds(e, 1), :, :]).then_inc(S["w1_copied"], 1)

            first_matrix(0)
            centre(1, 1, h)
            for p in range(PAIRS + 4):
                if p == 3:
                    predictor_pick(1)
                if p + 1 < PAIRS:
                    first_matrix(p + 1)
                if p == 0:
                    scale(1, 1, xn)
                if p >= 4:
                    dve.wait_ge(S["f2_t"], p - 3)
                    src = ps[:, 5, 0:2 * 128].rearrange("p (c i s) -> p c i s", c=CH, i=2)
                    dst = rT[:, :, 2 * (p - 4) * SEQ:2 * (p - 3) * SEQ].rearrange("p c (i s) -> p c i s", i=2)
                    for c in range(CH):
                        last = dve.tensor_copy(dst[:, c], src[:, c, :, 0:SEQ])
                    last.then_inc(S["r_ready"], 1)
                if 1 <= p <= PAIRS:
                    dve.wait_ge(S["f1_t"], p)
                    if p >= 3:
                        dve.wait_ge(S["f2_mm"], p - 2)
                    dve.tensor_copy(hgT[:, (p - 1) % 2, :, :],
                                    ps[:, 2 + (p - 1) % 2, :].rearrange("p (k n) -> p k n", k=FC))\
                       .then_inc(S["f1_T_ready"], 1)
                if p == 2:
                    predictor_logits(1)
                if 3 <= p < 3 + HALVES:
                    residual(p - 3)
                if p == PAIRS - 1:
                    add_ffn(0)
                if p == PAIRS:
                    centre(2, 0, h)
            scale(2, 0, rT)
            add_ffn(1)
            centre(3, 0, rT)
            centre(2, 1, h)

            def slots(t):
                dve.wait_ge(normed[t], 4)
                dve.wait_ge(S["pool_setup"], 8)

                def slotted(x, c):
                    images = x[:, c, 8 * SLOT * t:8 * SLOT * (t + 1)].rearrange("p (i s) -> p i s", s=SLOT)
                    return images[:, :, 0:SEQ]

                def tokens(c):
                    return xn[:, c, half(t)].rearrange("p (i s) -> p i s", s=SEQ)

                for c in range(CH):
                    last = dve.tensor_copy(slotted(xp_hi, c), tokens(c))
                last.then_inc(S["slot_hi"], 1)
                dve.wait_ge(S["slot_hi"], t + 1)
                for c in range(CH):
                    last = dve.tensor_tensor(slotted(xp_lo, c), tokens(c), slotted(xp_hi, c).bitcast(F32),
                                             ALU.subtract)
                last.then_inc(S["slotted"], 1)

            def query_min(t):
                dve.wait_ge(S["lq_mm"], t + 1)
                for c in range(CH):
                    last = dve.tensor_scalar(xs[:, c, half(t)], ps[:, QUERY_BANK[t] + c, 0:HT], col("bq", c), 0.0,
                                             ALU.add, ALU.min)
                last.then_inc(S["lq_min"], 1)

            def query_sum(t):
                dve.wait_ge(S["lq_exp"], t + 1)
                dve.wait_ge(S["lq_relu"], t + 1)
                dve.tensor_tensor(q[:, :, half(t)], q[:, :, half(t)], xs[:, :, half(t)], ALU.add)\
                   .then_inc(S["lq_ready"], 1)
                dve.wait_ge(S["lq_ready"], t + 1)
                for c in range(CH):
                    last = dve.tensor_scalar(xs[:, c, half(t)], rT[:, c, half(t)], col("out_b", c), None, ALU.add)
                link(last)

            scale(3, 0, xn, ("g1", "be1"))
            slots(0)
            scale(2, 1, rT)
            query_min(0)
            centre(3, 1, rT)

            def keys(p):
                dve.wait_ge(S["kv_mm"], p + 1)
                if p == 0:
                    dve.wait_ge(S["kvb_in"], 16)
                if p >= 2:
                    dve.wait_ge(S["state_mm"], p - 1)
                kv = ps[:, p % 2, :]
                dve.tensor_tensor(kf[:, p % 2, 0:EMB], kv[:, 0:EMB], kvb[:, 0:EMB], ALU.add).then_inc(S["k_ready"], 1)
                dve.tensor_tensor(vx[:, p % 2, :, 0:128], kv[:, EMB:].rearrange("p (c n) -> p c n", c=CH),
                                  kvb[:, EMB:].rearrange("p (c n) -> p c n", c=CH), ALU.add).then_inc(S["v2_ready"], 1)
                dve.wait_ge(S["k_ready"], p + 1)
                dve.tensor_scalar(ke[:, p % 2, 0:EMB], kf[:, p % 2, 0:EMB], 0.0, None, ALU.min).then_inc(S["k_min"], 1)

            def keys_sum(p):
                dve.wait_ge(S["k_exp"], p + 1)
                dve.scalar_tensor_tensor(out=kf[:, p % 2, 0:EMB], in0=kf[:, p % 2, 0:EMB], scalar=0.0,
                                         in1=ke[:, p % 2, 0:EMB], op0=ALU.max, op1=ALU.add).then_inc(S["kf_ready"], 1)

            def state(p):
                dve.wait_ge(S["state_mm"], p + 1)
                if p >= 2:
                    dve.wait_ge(S["y_mm"], p - 1)
                for i in range(2):
                    last = dve.tensor_tensor(kvm[:, p % 2, i, :, :],
                                             ps[:, 2 + i, 0:CH * (128 + CHH)].rearrange("p (c n) -> p c n", c=CH),
                                             const("block").unsqueeze(1).to_broadcast([128, CH, 128 + CHH]), ALU.mult)
                last.then_inc(S["state_ready"], 1)

            def divide(p):
                dve.wait_ge(S["y_mm"], p + 1)
                y = ps[:, 4, 0:CH * (128 + CHH)].rearrange("p (c n) -> p c n", c=CH)
                link(dve.tensor_scalar(dinv[:, p % 2, :, :], y[:, :, 128:], DEN_EPS, None, ALU.max))
                link(dve.reciprocal(dinv[:, p % 2, :, :], dinv[:, p % 2, :, :]))
                if p >= 2:
                    dve.wait_ge(S["y_t"], p - 1)
                for c in range(CH):
                    last = dve.tensor_tensor(yt[:, p % 2, 128 * c:128 * c + 128].rearrange("p (g d) -> p g d", d=HD),
                                             y[:, c, 0:128].rearrange("p (g d) -> p g d", d=HD),
                                             dinv[:, p % 2, c, :].unsqueeze(2).to_broadcast([128, CHH, HD]), ALU.mult)
                last.then_inc(S["y_ready"], 1)

            def add_linear(t):
                dve.wait_ge(S["out_mm"], t + 1)
                b = OUT_BANK[t]
                dve.tensor_tensor(xs[:, :, half(t)], xs[:, :, half(t)], ps[:, b:b + 2, 0:HT], ALU.add)\
                   .then_inc(S["x_ready"], 1)
                dve.wait_ge(S["x_ready"], t + 1)

            def ffn_residual(t):
                for c in range(CH):
                    last = dve.scalar_tensor_tensor(out=h[:, c, half(t)], in0=xs[:, c, half(t)], scalar=col("b2", c),
                                                    in1=h[:, c, half(t)], op0=ALU.add, op1=ALU.add)
                link(last)

            for p in range(PAIRS + 2):
                if p < PAIRS:
                    keys(p)
                if p == 0:
                    query_sum(0)
                if 1 <= p <= PAIRS:
                    state(p - 1)
                if p < PAIRS:
                    keys_sum(p)
                if p >= 2:
                    divide(p - 2)
                if p == 0:
                    scale(3, 1, xn, ("g1", "be1"))
                    slots(1)
                if p == 1:
                    query_min(1)
                if p == 3:
                    query_sum(1)
                if p == PAIRS - 1:
                    add_linear(0)
                if p == PAIRS:
                    centre(4, 0, xs)

            def split_weights(e, part):
                if e >= 2 and part == 0:
                    dve.wait_ge(S["u_mm"], steps_done(e - 2))
                if e >= 2 and part == 1:
                    dve.wait_ge(S["down_mm"], e - 1)
                lo, hi, raw = weight_parts(e)[part]
                dve.wait_ge(S["w_hi"], 3 * e + part + 1)
                dve.tensor_tensor(lo, raw, hi.bitcast(F32), ALU.subtract).then_inc(S["w_lo"], 1)

            def split_hidden(s):
                dve.wait_ge(S["up_gelu"], s + 1)
                if s >= HID_SLOTS:
                    dve.wait_ge(S["ff_mm"], s - HID_SLOTS + 1)
                dve.tensor_copy(hid_hi[:, s % HID_SLOTS, :], gelu_out[:, s % GELU_SLOTS, :]).then_inc(S["hid_hi"], 1)
                dve.wait_ge(S["hid_hi"], s + 1)
                dve.tensor_tensor(hid_lo[:, s % HID_SLOTS, :], gelu_out[:, s % GELU_SLOTS, :],
                                  hid_hi[:, s % HID_SLOTS, :].bitcast(F32), ALU.subtract).then_inc(S["hid_lo"], 1)

            def add_ff(t):
                dve.wait_ge(S["ff_mm"], DC * (t + 1))
                dve.tensor_tensor(h[:, :, half(t)], h[:, :, half(t)], ps[:, 4 + 2 * t:6 + 2 * t, 0:HT], ALU.add)\
                   .then_inc(S["ff_added"], 1)
                dve.wait_ge(S["ff_added"], t + 1)

            scale(4, 0, xn, ("g2", "be2"))
            split_tokens(4, 0)
            add_linear(1)
            for s in range(HALVES * DC):
                split_hidden(s)
                if s == 1:
                    centre(4, 1, xs)
                if s == 2:
                    ffn_residual(0)
                if s == 4:
                    scale(4, 1, xn, ("g2", "be2"))
                    split_tokens(4, 1)
                if s == 6:
                    ffn_residual(1)
                if s == DC + 2:
                    add_ff(0)
                if s == DC + 3:
                    centre(5, 0, h)
                if s == DC + 5:
                    scale(5, 0, xn)
                    split_tokens(5, 0)
            add_ff(1)

            def router_max():
                src = ps[0:RT, 4, 0:HALVES * RC * ROUTE].rearrange("p (t c e) -> p t c e", t=HALVES, c=RC)
                dve.wait_ge(S["r_t"], 1)
                link(dve.tensor_reduce(rsum[:, :, :], src[:, :, :, 0:EXP], AX.X, ALU.max))
                link(dve.tensor_tensor(rtok[:, :, :, 0:EXP], src[:, :, :, 0:EXP],
                                       rsum[:, :, :].unsqueeze(3).to_broadcast([RT, HALVES, RC, EXP]), ALU.subtract))
                dve.tensor_scalar(rtok[:, :, :, EXP:], src[:, :, :, EXP:], -1.0, None, ALU.mult)\
                   .then_inc(S["r_max"], 1)

            def router_probs():
                dve.wait_ge(S["r_exp"], 1)
                link(dve.tensor_reduce(rsum[:, :, :], rex[:, :, :, 0:EXP], AX.X, ALU.add))
                link(dve.reciprocal(rsum[:, :, :], rsum[:, :, :]))
                link(dve.tensor_tensor(rex[:, :, :, 0:EXP], rex[:, :, :, 0:EXP],
                                       rsum[:, :, :].unsqueeze(3).to_broadcast([RT, HALVES, RC, EXP]), ALU.mult))
                link(dve.tensor_scalar(rw[:, :, :, EXP:], rex[:, :, :, EXP:], 1.0, None, ALU.add))
                link(dve.reciprocal(rw[:, :, :, EXP:], rw[:, :, :, EXP:]))

            def router_top():
                cells = [(t, c) for t in range(HALVES) for c in range(RC)]
                for t, c in cells:
                    last = dve.max(rmx[:, t, c, :], rex[:, t, c, 0:EXP])
                link(last)
                for t, c in cells:
                    last = dve.max_index(rix[:, t, c, :], rmx[:, t, c, :], rex[:, t, c, 0:EXP])
                link(last)
                link(dve.tensor_copy(rixf[:, :, :, :], rix[:, :, :, :]))

            def router_weights():
                full = [RT, HALVES, RC, EXP]
                iota = const("iota")[0:RT, 0:EXP].unsqueeze(1).unsqueeze(1).to_broadcast(full)
                link(dve.tensor_tensor(rm2[:, :, :, :], iota, rixf[:, :, :, 1:2].to_broadcast(full), ALU.is_equal))
                link(dve.tensor_tensor(rw[:, :, :, 0:EXP], iota, rixf[:, :, :, 0:1].to_broadcast(full), ALU.is_equal))
                link(dve.tensor_tensor(rm2[:, :, :, :], rm2[:, :, :, :], rw[:, :, :, 0:EXP], ALU.add))
                dve.tensor_tensor(rw[:, :, :, 0:EXP], rm2[:, :, :, :], rex[:, :, :, 0:EXP], ALU.mult)\
                   .then_inc(S["r_w"], 1)

            def add_shared(t, step):
                if step == 0:
                    dve.wait_ge(S["down_mm"], SHARED)
                    dve.wait_ge(gate_in[EXP], 16)
                    link(dve.tensor_tensor(xs[:, :, half(t)], ps[:, 4 + t:8:2, 0:HT],
                                           gate[:, EXP, half(t)].unsqueeze(1).to_broadcast([128, CH, HT]), ALU.mult))
                else:
                    dve.tensor_tensor(h[:, :, half(t)], h[:, :, half(t)], xs[:, :, half(t)], ALU.add)\
                       .then_inc(S["shared_added"], 1)

            def low_part(n):
                e, t, m = moe_step(n)
                rows = MCH[m][1]
                dve.wait_ge(S["h_hi"], n + 1)
                dve.tensor_tensor(hlo[0:rows, e % 2, m, half(t)], prod[0:rows, n % 2, :],
                                  hhi[0:rows, e % 2, m, half(t)].bitcast(F32), ALU.subtract)\
                   .then_inc(S["h_lo"], 1)

            def second_half_centre():
                centre(5, 1, h)

            def second_half_scale():
                scale(5, 1, xn)
                split_tokens(5, 1)

            between = {0: second_half_centre, 3: second_half_scale, 6: router_max, 7: router_probs, 8: router_top,
                       9: router_weights}
            for i in range(2 * HALVES):
                between[STEPS * SHARED + 2 + i] = lambda t=i // 2, step=i % 2: add_shared(t, step)
            for n in range(STEPS * BLOCKS):
                e, t, m = moe_step(n)
                rows = MCH[m][1]
                if e < SHARED:
                    dve.wait_ge(S["silu"], n + 1)
                else:
                    dve.wait_ge(S["gated"], n - STEPS * SHARED + 1)
                dve.wait_ge(S["u_mm"], n + 1)
                if n >= 2:
                    dve.wait_ge(S["h_hi"], n - 1)
                    dve.wait_ge(S["h_lo"], n - 1)
                dve.tensor_tensor(prod[0:rows, n % 2, :], sil[0:rows, 0 if e < SHARED else 1, n % 2, :],
                                  ps[0:rows, 1 + 2 * (n % 2), 0:HT], ALU.mult).then_inc(S["h_mul"], 1)
                if n > STEPS * SHARED:
                    low_part(n - 1)
                if n in between:
                    between[n]()
                if n in SPLIT_AFTER:
                    split_weights(*SPLIT_AFTER[n])
            low_part(STEPS * BLOCKS - 1)
            dve.wait_ge(S["shared_added"], HALVES)
            for c in range(CH):
                dve.wait_ge(S["last_down"], c + 1)
                dve.tensor_tensor(xs[:, c, :].rearrange("p (t n) -> p t n", t=HALVES),
                                  h[:, c, :].rearrange("p (t n) -> p t n", t=HALVES),
                                  ps[:, 4 + 2 * c:6 + 2 * c, 0:HT], ALU.add).then_inc(S["moe_added"], 1)

        @block.tensor
        def _(pe):
            def dense(bank, w, m, x, t, ks=CH):
                for k in range(ks):
                    last = pe.matmul(ps[:, bank, 0:HT], w[:, k, 128 * m:128 * m + 128], x[:, k, half(t)],
                                     start=(k == 0), stop=(k == ks - 1))
                return last

            def mean(k, t, src):
                for c in range(CH):
                    last = pe.matmul(ps[:, NORM_BANK[k][t], 0:HT], ones_mean, src[:, c, half(t)], start=(c == 0),
                                     stop=(c == CH - 1))
                last.then_inc(mean_mm[t], 1)

            def variance(k, t):
                pe.wait_ge(squared[t], k + 1)
                for c in range(CH):
                    last = pe.matmul(ps[:, NORM_BANK[k][t], 0:HT], ones_mean, sq[:, c, half(t)], start=(c == 0),
                                     stop=(c == CH - 1))
                last.then_inc(var_mm[t], 1)

            def exact(bank, whi, wlo, xh, xl, first, final):
                pe.matmul(bank, whi, xh, start=first, stop=False)
                pe.matmul(bank, wlo, xh, start=False, stop=False)
                return pe.matmul(bank, whi, xl, start=False, stop=final)

            for k in range(KP):
                if k == 0:
                    pe.wait_ge(patch_in[0], 32)
                else:
                    pe.wait_ge(S["patch_lo"], k)
                for t in range(HALVES):
                    for m in range(CH):
                        bank, part = ps[:, 4 * t + 2 + m, 0:HT], slice(128 * m, 128 * m + 128)
                        if k == 0:
                            pe.matmul(bank, wp[:, 0, part], X[:, 0, half(t)], start=True, stop=False)
                        else:
                            last = exact(bank, wp_hi[:, k, part], wp_lo[:, k, part], X_hi[:, k, half(t)],
                                         X_lo[:, k, half(t)], False, k == KP - 1)
                    if k == KP - 1:
                        last.then_inc(S["tok_mm"], 1)
            pe.wait_ge(S["const_in"], 16)
            for t in range(HALVES):
                pe.wait_ge(S["h_ready"], CH * (t + 1))
                mean(0, t, h)
            for t in range(HALVES):
                variance(0, t)
            pe.wait_ge(S["kq_lo"], 1)
            for t in range(HALVES):
                pe.wait_ge(S["xn_hi"], t + 1)
                for at in (CH, 0):
                    for step in range(3):
                        if step == 2:
                            pe.wait_ge(S["xn_lo"], t + 1)
                        w, x = ((kq_hi, xn_hi), (kq_lo, xn_hi), (kq_hi, xn_lo))[step]
                        for m in range(CH):
                            part = slice(128 * (at + m), 128 * (at + m) + 128)
                            for k in range(CH):
                                last = pe.matmul(ps[:, 4 * t + at + m, 0:HT], w[:, k, part], x[:, k, half(t)],
                                                 start=(step == 0 and k == 0), stop=(step == 2 and k == CH - 1))
                    last.then_inc(S["qk_mm"], 1)
            pe.wait_ge(S["pool_setup"], 3)
            for t in range(HALVES):
                pe.wait_ge(S["q_ready"], t + 1)
                for n in range(8):
                    i, at = 8 * t + n, 128 * (n % 4)
                    for o in range(2):
                        for k in range(CH):
                            last = pe.matmul(ps[64 * o:64 * o + 64, 4 * t + 2 + n // 4, at:at + 128],
                                             xn[:, k, slot(i)], kqv[:, k, 2 * EMB + 128 * o:2 * EMB + 128 * o + 128],
                                             start=(k == 0), stop=(k == CH - 1))
                last.then_inc(S["v_mm"], 1)

            def scores(p):
                if p == 0:
                    for name in ("q_ready", "kx_dve", "kx_act"):
                        pe.wait_ge(S[name], HALVES)
                if p == 1:
                    pe.wait_ge(S["v_act"], 1)
                    pe.wait_ge(S["v_dve"], 1)
                if p >= 2:
                    pe.wait_ge(S["row_max"], p - 1)
                for c in range(CH):
                    for i in range(2):
                        a = 2 * p + i
                        t, o = a // 8, (a % 8) * SEQ
                        last = pe.matmul(ps[64 * i:64 * i + 64, 2 * (p % 2) + c, 0:CHH * SEQ], q[:, c, slot(a)],
                                         kx[:, t, c, :, o:o + SEQ], start=True, stop=True)
                last.then_inc(S["score_mm"], 1)

            def turn_probs(p):
                pe.wait_ge(S["prob_ready"], p + 1)
                if p >= 1:
                    pe.wait_ge(S["pT_ready"], p)
                pr = prob[:, p % 2, :, :].rearrange("p (j o) s -> p j (o s)", o=2)
                for j in range(HEADS // 2):
                    last = pe.transpose(ps[:, 4 + j // 4, 128 * (j % 4):128 * (j % 4) + 128], pr[:, j, :], ident)
                last.then_inc(S["prob_mm"], 1)

            def values(p):
                pe.wait_ge(S["pT_ready"], p + 1)
                if p == 0:
                    pe.wait_ge(S["v_act"], HALVES)
                    pe.wait_ge(S["v_dve"], HALVES)
                if p >= 1:
                    pe.wait_ge(S["inverted"], p)
                for c in range(CH):
                    for i in range(2):
                        for j in range(4):
                            o = 2 * SEQ * c + SEQ * i
                            pe.matmul(ps[32 * j:32 * j + 32, 6, o:o + SEQ], vbd[:, 2 * p + i, 4 * c + j, :],
                                      pT[:, p % 2, 4 * c + j, i, :], start=True, stop=True)
                for c in range(CH):
                    for j in range(4):
                        o = 2 * SEQ * (CH + c)
                        last = pe.matmul(ps[32 * j:32 * j + 32, 6, o:o + 2 * SEQ], const("ones"),
                                         pT[:, p % 2, 4 * c + j, :, :], start=True, stop=True)
                last.then_inc(S["pv_mm"], 1)

            for p in range(PAIRS + 3):
                if p < PAIRS:
                    scores(p)
                if 2 <= p <= PAIRS + 1:
                    turn_probs(p - 2)
                if p >= 3:
                    values(p - 3)
                if p == PAIRS - 1:
                    pe.wait_ge(S["attn_added"], HPAIRS)
                    mean(1, 0, h)
                if p == PAIRS + 1:
                    variance(1, 0)

            def predictor_up(t):
                if t == 0:
                    pe.wait_ge(S["wp1_in"], 16)
                pe.wait_ge(normed[t], 2)
                for k in range(CH):
                    last = pe.matmul(ps[:, NORM_BANK[1][t], 0:8], wp1_sb[:, k, :],
                                     xn[:, k, half(t)].rearrange("p (i s) -> p i s", s=SEQ)[:, :, SEQ - 1],
                                     start=(k == 0), stop=(k == CH - 1))
                last.then_inc(S["p1_mm"], 1)

            def predictor_down(t):
                if t == 0:
                    pe.wait_ge(S["wp2_in"], 16)
                pe.wait_ge(S["p1_act"], t + 1)
                pe.matmul(ps[0:8, NORM_BANK[1][t], 32:40], act8[:, t, :], wp2_sb[:, :], start=True, stop=True)\
                  .then_inc(S["p2_mm"], 1)

            def turn_hot(t):
                pe.wait_ge(S["hot_ready"], t + 1)
                pe.transpose(ps[0:PARTS * EXP, NORM_BANK[1][t], 64:72], hot[:, t, :], ident[0:8, 0:8])\
                  .then_inc(S["hot_mm"], 1)

            predictor_up(0)
            predictor_down(0)
            pe.wait_ge(S["attn_added"], PAIRS)
            mean(1, 1, h)
            turn_hot(0)
            pe.wait_ge(S["bias_ready"], 1)

            def rows_up(p):
                pe.wait_ge(S["w1_copied"], 2 * p + 2)
                if p >= 2:
                    pe.wait_ge(S["f1_gelu"], p - 1)
                if p == HPAIRS - 1:
                    pe.wait_ge(normed[1], 2)
                for k in range(CH):
                    for i in range(2):
                        pe.matmul(ps[64 * i:64 * i + 64, p % 2, :], xn[:, k, slot(2 * p + i)],
                                  w1s[:, p % 2, i, k, :], start=(k == 0), stop=False)
                pe.wait_ge(S["hot_columns"], p // HPAIRS + 1)
                for i in range(2):
                    last = pe.matmul(ps[64 * i:64 * i + 64, p % 2, :], hotT[:, 2 * p + i, :], bias_parts[:, 0:FFN],
                                     start=False, stop=True)
                last.then_inc(S["f1_mm"], 1)

            def turn_rows(p):
                pe.wait_ge(S["f1_gelu"], p + 1)
                if p >= 2:
                    pe.wait_ge(S["f1_T_ready"], p - 1)
                for k in range(FC):
                    part = slice(128 * k, 128 * k + 128)
                    last = pe.transpose(ps[:, 2 + p % 2, part], hg[:, p % 2, part], ident)
                last.then_inc(S["f1_t"], 1)

            def rows_down(p):
                pe.wait_ge(S["f1_T_ready"], p + 1)
                pe.wait_ge(S["w2_copied"], 2 * p + 2)
                if p >= 1:
                    pe.wait_ge(S["f2_ready"], p)
                for i in range(2):
                    pe.matmul(ps[64 * i:64 * i + 64, 4, 0:EMB], hotT[:, 2 * p + i, :], bias_parts[:, FFN:], start=True,
                              stop=False)
                for k in range(FC):
                    for i in range(2):
                        last = pe.matmul(ps[64 * i:64 * i + 64, 4, 0:EMB], hgT[:, p % 2, k, 64 * i:64 * i + 64],
                                         w2s[:, p % 2, i, k, :], start=False, stop=(k == FC - 1))
                last.then_inc(S["f2_mm"], 1)

            def turn_out(p):
                pe.wait_ge(S["f2_ready"], p + 1)
                if p >= 1:
                    pe.wait_ge(S["r_ready"], p)
                for c in range(CH):
                    last = pe.transpose(ps[:, 5, 128 * c:128 * c + 128], rr[:, p % 2, 128 * c:128 * c + 128], ident)
                last.then_inc(S["f2_t"], 1)

            def reasoned(t):
                if t == 0:
                    pe.wait_ge(S["wo_in"], 16)
                pe.wait_ge(S["r_ready"], HPAIRS * (t + 1))
                for m in range(CH):
                    last = dense(OUT_BANK[t] + m, wo_sb, m, rT, t)
                last.then_inc(S["wo_mm"], 1)

            for p in range(PAIRS + 3):
                if p < PAIRS:
                    rows_up(p)
                if 1 <= p <= PAIRS:
                    turn_rows(p - 1)
                if p == 2:
                    predictor_down(1)
                if 2 <= p <= PAIRS + 1:
                    rows_down(p - 2)
                if p >= 3:
                    turn_out(p - 3)
                if p == 0:
                    variance(1, 1)
                if p == 1:
                    predictor_up(1)
                if p == 3:
                    turn_hot(1)
                if p == PAIRS - 1:
                    reasoned(0)
                if p == PAIRS:
                    pe.wait_ge(S["ffn_added"], 1)
                    mean(2, 0, h)
                if p == PAIRS + 1:
                    variance(2, 0)

            def queries(t):
                pe.wait_ge(normed[t], 4)
                for m in range(CH):
                    last = dense(QUERY_BANK[t] + m, qkv, m, xn, t)
                last.then_inc(S["lq_mm"], 1)

            reasoned(1)
            pe.wait_ge(normed[0], 3)
            mean(3, 0, rT)
            pe.wait_ge(S["ffn_added"], 2)
            mean(2, 1, h)
            variance(3, 0)
            variance(2, 1)
            pe.wait_ge(S["qkv_in"], 16)
            queries(0)
            pe.wait_ge(normed[1], 3)
            mean(3, 1, rT)

            def keys_values(p):
                if p % HPAIRS == 0:
                    pe.wait_ge(S["slotted"], p // HPAIRS + 1)
                if p >= 2:
                    pe.wait_ge(S["v2_ready"], p - 1)
                if p == 0:
                    pe.wait_ge(S["kv_lo"], 1)
                for k in range(CH):
                    part = slice(128 * p, 128 * p + 128)
                    last = exact(ps[:, p % 2, :], xp_hi[:, k, part], xp_lo[:, k, part],
                                 kv_hi[:, k, :], kv_lo[:, k, :], k == 0, k == CH - 1)
                last.then_inc(S["kv_mm"], 1)

            def states(p):
                pe.wait_ge(S["kf_ready"], p + 1)
                pe.wait_ge(S["v2_ready"], p + 1)
                if p == 0:
                    pe.wait_ge(S["lq_ready"], 1)
                if p >= 1:
                    pe.wait_ge(S["state_ready"], p)
                w = 128 + CHH
                for c in range(CH):
                    for i in range(2):
                        a = 64 * i
                        last = pe.matmul(ps[:, 2 + i, w * c:w * c + w], kf[a:a + SEQ, p % 2, 128 * c:128 * c + 128],
                                         vx[a:a + SEQ, p % 2, c, :], start=True, stop=True)
                last.then_inc(S["state_mm"], 1)

            def outputs(p):
                pe.wait_ge(S["state_ready"], p + 1)
                if p == HPAIRS - 1:
                    pe.wait_ge(S["lq_ready"], 2)
                if p >= 1:
                    pe.wait_ge(S["y_ready"], p)
                w = 128 + CHH
                for c in range(CH):
                    for i in range(2):
                        last = pe.matmul(ps[64 * i:64 * i + 64, 4, w * c:w * c + w], q[:, c, slot(2 * p + i)],
                                         kvm[:, p % 2, i, c, :], start=True, stop=True)
                last.then_inc(S["y_mm"], 1)

            def turn_y(p):
                pe.wait_ge(S["y_ready"], p + 1)
                if p >= 1:
                    pe.wait_ge(S["yT_ready"], p)
                for c in range(CH):
                    last = pe.transpose(ps[:, 5, 128 * c:128 * c + 128], yt[:, p % 2, 128 * c:128 * c + 128], ident)
                last.then_inc(S["y_t"], 1)

            def linear_out(t):
                if t == 0:
                    pe.wait_ge(S["wout_in"], 16)
                pe.wait_ge(S["yT_ready"], HPAIRS * (t + 1))
                for m in range(CH):
                    last = dense(OUT_BANK[t] + m, wout, m, yT, t)
                last.then_inc(S["out_mm"], 1)

            for p in range(PAIRS + 3):
                if p < PAIRS:
                    keys_values(p)
                if p == 1:
                    queries(1)
                if 1 <= p <= PAIRS:
                    states(p - 1)
                if 2 <= p <= PAIRS + 1:
                    outputs(p - 2)
                if p == PAIRS + 1:
                    variance(4, 0)
                if p >= 3:
                    turn_y(p - 3)
                if p == 0:
                    variance(3, 1)
                if p == PAIRS - 1:
                    linear_out(0)
                if p == PAIRS:
                    pe.wait_ge(S["x_ready"], 1)
                    mean(4, 0, xs)
            linear_out(1)
            pe.wait_ge(S["fw_lo"], 2 * CH)

            for s in range(HALVES * DC + SKEW):
                if s < HALVES * DC:
                    t, m = s // DC, s % DC
                    if m == 0:
                        pe.wait_ge(S["x_lo"], t + 1)
                    if s >= UP_BANKS:
                        pe.wait_ge(S["up_gelu"], s - UP_BANKS + 1)
                    for k in range(CH):
                        part = slice(128 * m, 128 * m + 128)
                        last = exact(ps[:, (s + 2) % UP_BANKS, 0:HT], fw1_hi[:, k, part], fw1_lo[:, k, part],
                                     xhi[:, k, half(t)], xlo[:, k, half(t)], k == 0, k == CH - 1)
                    last.then_inc(S["up_mm"], 1)
                if s >= SKEW:
                    d = s - SKEW
                    t, k = d // DC, d % DC
                    pe.wait_ge(S["hid_lo"], d + 1)
                    for m in range(CH):
                        part = slice(128 * m, 128 * m + 128)
                        last = exact(ps[:, 4 + 2 * t + m, 0:HT], fw2_hi[:, k, part], fw2_lo[:, k, part],
                                     hid_hi[:, d % HID_SLOTS, :], hid_lo[:, d % HID_SLOTS, :],
                                     k == 0, k == DC - 1)
                    last.then_inc(S["ff_mm"], 1)
                if s == 1:
                    pe.wait_ge(S["x_ready"], 2)
                    mean(4, 1, xs)
                if s == 3:
                    variance(4, 1)
                if s == DC + 3:
                    pe.wait_ge(S["ff_added"], 1)
                    mean(5, 0, h)
                if s == DC + 5:
                    variance(5, 0)

            def logits(t):
                pe.wait_ge(normed[t], 6)
                for k in range(CH):
                    last = pe.matmul(ps[0:ROUTE, 6 + t, 0:HT], route_sb[:, k, :], xn[:, k, half(t)], start=(k == 0),
                                     stop=(k == CH - 1))
                last.then_inc(S["r_mm"], 1)

            def turn_logits():
                pe.wait_ge(S["r_copied"], HALVES)
                for c in range(HALVES * RC):
                    last = pe.transpose(ps[0:RT, 4, ROUTE * c:ROUTE * c + ROUTE], rlog[:, RT * c:RT * c + RT],
                                        ident[0:ROUTE, 0:ROUTE])
                last.then_inc(S["r_t"], 1)

            def turn_weights():
                pe.wait_ge(S["r_w"], 1)
                for t in range(HALVES):
                    for c in range(RC):
                        last = pe.transpose(ps[0:ROUTE, 6 + t, RT * c:RT * c + RT], rw[:, t, c, :],
                                            ident[0:RT, 0:RT])
                    last.then_inc(S["r_back"], 1)

            def second_half_mean():
                pe.wait_ge(S["ff_added"], 2)
                mean(5, 1, h)

            def second_half_variance():
                variance(5, 1)
                pe.wait_ge(S["route_in"], 16)
                logits(0)

            def down(e):
                pe.wait_ge(S["h_lo"], steps_done(e))
                lower_sem, count = lower_parts(e, 3)
                pe.wait_ge(lower_sem, count)
                if e == 0:
                    pe.wait_ge(S["w_rows"], HALVES)
                if e == SHARED:
                    pe.wait_ge(S["shared_added"], HALVES)
                for c in range(CH):
                    for m, (_, rows) in enumerate(MCH):
                        o = EMB * m + 128 * c
                        for t in range(HALVES):
                            last = exact(ps[:, 4 + 2 * c + t, 0:HT], dnhi[0:rows, e % 2, o:o + 128],
                                         dnlo[0:rows, e % 2, o:o + 128], hhi[0:rows, e % 2, m, half(t)],
                                         hlo[0:rows, e % 2, m, half(t)], e in (0, SHARED) and m == 0,
                                         e in (SHARED - 1, BLOCKS - 1) and m == MC - 1)
                    if e == BLOCKS - 1:
                        last.then_inc(S["last_down"], 1)
                if e < BLOCKS - 1:
                    last.then_inc(S["down_mm"], 1)

            def second_half_logits():
                logits(1)

            between = {0: second_half_mean, 1: second_half_variance, 5: second_half_logits, 6: turn_logits,
                       10: turn_weights}
            for n in range(STEPS * BLOCKS):
                e, t, m = moe_step(n)
                r0, rows = MCH[m]
                if m == 0:
                    lower_sem, count = lower_parts(e, 1)
                    pe.wait_ge(lower_sem, count)
                if n < STEPS * SHARED and m == 0:
                    pe.wait_ge(S["x_lo"], HALVES + t + 1)
                if n >= 2:
                    pe.wait_ge(S["h_mul"], n - 1)
                for u, done in enumerate(("g_mm", "u_mm")):
                    for k in range(CH):
                        o = 2 * MOE_I * k + MOE_I * u + r0
                        last = exact(ps[0:rows, 2 * (n % 2) + u, 0:HT], guhi[:, e % 2, o:o + rows],
                                     gulo[:, e % 2, o:o + rows], xhi[:, k, half(t)], xlo[:, k, half(t)],
                                     k == 0, k == CH - 1)
                    last.then_inc(S[done], 1)
                if n in between:
                    between[n]()
                if n in DOWN_AFTER:
                    down(DOWN_AFTER[n])
            down(BLOCKS - 1)


def wt(w):
    k, m = w.shape
    return np.ascontiguousarray(w.reshape(k // 128, 128, m).transpose(1, 0, 2))


def kernel(**inp):
    import concourse.bacc as bacc
    from concourse.bass_utils import run_bass_kernel_spmd

    a = {k: np.asarray(v) for k, v in inp.items()}
    side = 96 // 16
    x = a["x"].reshape(IMGS, side, 16, side, 16, 3).transpose(2, 4, 5, 0, 1, 3).reshape(PATCH, TOK)
    kqv = a["L0_attn_W_kqv"].T
    v = kqv[:, 2 * EMB:].reshape(EMB, HEADS // 2, 2, HD).transpose(0, 2, 1, 3).reshape(EMB, EMB)
    cols = np.zeros((128, NCOLS), np.float32)

    def put(name, value):
        cols[:, COLS[name][0]:COLS[name][1]] = value

    def per_feature(b):
        return b.reshape(-1, 128).T

    put("b_proj", per_feature(a["L0_tok_b_proj"]))
    put("pos", a["L0_tok_pos_emb"].T.reshape(CH, 128, SEQ).transpose(1, 0, 2).reshape(128, -1))
    put("bp1", a["L0_ffn_bp1"].reshape(128, 1))
    put("bp2", np.broadcast_to(a["L0_ffn_bp2"], (128, EXP)))
    put("bo", per_feature(a["L0_ffn_bo"]))
    put("bq", per_feature(a["L1_attn_qkv_b"][:EMB]))
    for name in ("out_b", "b1", "b2", "g1", "be1", "g2", "be2"):
        put(name, per_feature(a["L1_attn_" + name]))

    consts = np.zeros((128, NCONST), np.float32)

    def fix(name, value):
        consts[:, CONST[name][0]:CONST[name][1]] = value

    fix("ident", np.eye(128))
    fix("mean", 1.0 / EMB)
    base = (2 ** 8) ** (1.0 / HEADS)
    slopes = np.array([1.0 / base ** (i + 1) for i in range(HEADS)], np.float32)
    rel = (np.arange(SEQ)[None, :] - np.arange(SEQ)[:, None]).astype(np.float32)
    alibi = np.where(rel[:, None, :] > 0, np.float32(NEG), slopes[None, :, None] * rel[:, None, :])
    both = np.zeros((128, HEADS * SEQ), np.float32)
    both[0:SEQ] = both[64:64 + SEQ] = alibi.reshape(SEQ, -1)
    fix("alibi", both)
    part = np.arange(128)[:, None] // HD
    fix("head", part == np.arange(CHH)[None])
    fix("block", np.concatenate([part == np.arange(128)[None] // HD, part == np.arange(CHH)[None]], 1))
    fix("iota", np.tile(np.arange(EXP), PARTS)[None])
    fix("ones", np.arange(128)[:, None] // SLOT == np.arange(2 * HD)[None] // HD)
    fix("later", -1.0 * (np.arange(128)[:, None] >= EXP * np.arange(1, PARTS)[None]))

    w1 = a["L0_ffn_W1"].reshape(EXP, CH, 128, FFN).transpose(2, 0, 1, 3)
    w2 = a["L0_ffn_W2"].reshape(EXP, FC, 128, EMB).transpose(2, 0, 1, 3)
    qkv = a["L1_attn_qkv_w"]
    sg, su, sd = (a["L1_ffn_shared_" + n + "_w"] for n in ("gate", "up", "down"))
    gu = [np.concatenate([sg[s:s + MOE_I], su[s:s + MOE_I]], 0) for s in (0, MOE_I)]
    gu += [a["L1_ffn_experts_gate_up"][e] for e in range(EXP)]
    gu = np.stack([wt(g.T).reshape(128, GU) for g in gu])
    dn = [sd.T[s:s + MOE_I] for s in (0, MOE_I)] + [a["L1_ffn_experts_down"][e].T for e in range(EXP)]
    down = np.zeros((BLOCKS, 128, MC, EMB), np.float32)
    for e, d in enumerate(dn):
        for m, (r0, rows) in enumerate(MCH):
            down[e, :rows, m] = d[r0:r0 + rows]
    route = np.concatenate([a["L1_ffn_gate_w"], a["L1_ffn_shared_expert_gate_w"]], 0).T

    arrays = {
        "patches": wt(x), "w_proj": wt(a["L0_tok_W_proj"].T), "w_kqv": wt(np.concatenate([kqv[:, :2 * EMB], v], 1)),
        "cols": cols, "consts": consts, "wp1": wt(a["L0_ffn_Wp1"]), "wp2": a["L0_ffn_Wp2"],
        "w1x": w1, "b1x": a["L0_ffn_b1"], "w2x": w2, "b2x": a["L0_ffn_b2"], "wo": wt(a["L0_ffn_Wo"]),
        "qkv_w": wt(qkv), "kv_b": a["L1_attn_qkv_b"][EMB:], "out_w": wt(a["L1_attn_out_w"]),
        "ffn_w1": wt(a["L1_attn_w1"]), "ffn_w2": wt(a["L1_attn_w2"]), "route_w": wt(route),
        "moe_gu": gu, "moe_down": down.reshape(BLOCKS, 128, DOWN),
    }
    arrays = {k: np.ascontiguousarray(v) for k, v in arrays.items()}
    nc = bacc.Bacc("TRN2", target_bir_lowering=False, num_devices=1)
    args = {k: nc.dram_tensor(k, v.shape, F32, kind="ExternalInput").ap() for k, v in arrays.items()}
    out = nc.dram_tensor("out", (128, CH, TOK), F32, kind="ExternalOutput").ap()
    tower(nc, out=out, **args)
    r = run_bass_kernel_spmd(nc, [arrays], core_ids=[0])
    got = r.results[0]["out"]
    return np.ascontiguousarray(got.transpose(2, 1, 0).reshape(IMGS, SEQ, EMB))
```
